# Optimizing a Trainium2 kernel written in Bass

```python
import numpy as np
import jax
import jax.numpy as jnp

def _softmax(x, axis=-1):
    return jax.nn.softmax(x, axis=axis)

def _gelu(x):
    return jax.nn.gelu(x, approximate=True)

def _silu(x):
    return jax.nn.silu(x)

def _sigmoid(x):
    return jax.nn.sigmoid(x)

def _layernorm(x, axis=-1, eps=1e-05):
    m = jnp.mean(x, axis=axis, keepdims=True)
    v = jnp.var(x, axis=axis, keepdims=True)
    return (x - m) / jnp.sqrt(v + eps)

def _scatter_add(tgt, idx, src, axis=0):
    return tgt.at[idx].add(src)

def _segment_sum(src, seg, n):
    return jax.ops.segment_sum(src, seg, n)
kernel_name = 'mk_conv_preact_d4_conv_nchw64_r2_ab813c'

def setup_inputs(seed: int=0):
    np.random.seed(seed)
    _w = jnp.asarray

    def _rec_inputs():
        import jax
        import jax.numpy as jnp
        _gk = jax.random.key(seed)
        x = -0.0002928 + 1 * jax.random.normal(jax.random.fold_in(_gk, 1), (16, 32, 32, 32), jnp.float32)
        return x
    x = _rec_inputs()

    def _L0_conv_setup():
        import jax, jax.numpy as jnp
        import numpy as np
        B, E, H, W = (16, 32, 32, 32)
        K = 512
        NC = 8
        key = jax.random.key(seed)
        k_emb, k_cb = jax.random.split(key)
        embeddings = jax.random.normal(k_emb, (B, E, H, W), dtype=jnp.float32)
        init = 1.0 / K
        codebooks = jax.random.uniform(k_cb, (NC, K, E), dtype=jnp.float32, minval=-init, maxval=init)
        return {'embeddings': embeddings, 'codebooks': codebooks}
    _L0_conv_all = _L0_conv_setup()
    _L0_conv_in = {k: v for k, v in _L0_conv_all.items() if k in ('codebooks',)}
    del _L0_conv_all

    def _L1_conv_setup():
        import jax, jax.numpy as jnp
        import numpy as np
        PATCH = 8

        def _to_patches(t):
            b, c, H, W = t.shape
            t = t.reshape(b, c, H // PATCH, PATCH, W // PATCH, PATCH)
            return t.transpose(0, 1, 2, 4, 3, 5)

        def _from_patches(t):
            b, c, h, w, p1, p2 = t.shape
            return t.transpose(0, 1, 2, 4, 3, 5).reshape(b, c, h * p1, w * p2)
        key = jax.random.key(seed)
        ks = jax.random.split(key, 8)
        dim = 32
        hid = dim * 6
        x = jax.random.normal(ks[0], (4, dim, 128, 128), dtype=jnp.float32)
        w_hidden = jax.random.normal(ks[1], (hid, dim), dtype=jnp.float32) * 0.05
        b_hidden = jax.random.normal(ks[2], (hid,), dtype=jnp.float32) * 0.02
        w_dw = jax.random.normal(ks[3], (hid, 3, 3), dtype=jnp.float32) * 0.1
        b_dw = jax.random.normal(ks[4], (hid,), dtype=jnp.float32) * 0.02
        w_proj = jax.random.normal(ks[5], (dim, dim * 2), dtype=jnp.float32) * 0.05
        b_proj = jax.random.normal(ks[6], (dim,), dtype=jnp.float32) * 0.02
        ln_w = jnp.ones((dim * 2,), dtype=jnp.float32)
        ln_b = jnp.zeros((dim * 2,), dtype=jnp.float32)
        return {'x': x, 'w_hidden': w_hidden, 'b_hidden': b_hidden, 'w_dw': w_dw, 'b_dw': b_dw, 'w_proj': w_proj, 'b_proj': b_proj, 'ln_w': ln_w, 'ln_b': ln_b}
    _L1_conv_all = _L1_conv_setup()
    _L1_conv_in = {k: v for k, v in _L1_conv_all.items() if k in ('w_hidden', 'b_hidden', 'w_dw', 'b_dw', 'w_proj', 'b_proj', 'ln_w', 'ln_b')}
    del _L1_conv_all

    def _L2_conv_setup():
        import jax, jax.numpy as jnp
        import numpy as np
        from jax import lax
        C = 32
        K = 9
        PAD = 4

        def conv1d(x, w, b):
            y = lax.conv_general_dilated(x, w, window_strides=(1,), padding=[(PAD, PAD)], dimension_numbers=('NCH', 'OIH', 'NCH'))
            return y + b[None, :, None]

        def directional_scan(seq, w, b):
            first = seq[0]

            def step(carry, row):
                new = row + jax.nn.relu(conv1d(carry, w, b))
                return (new, new)
            _, rest = lax.scan(step, first, seq[1:])
            return jnp.concatenate([first[None], rest], axis=0)

        def scnn_forward(x, w_ud, b_ud, w_du, b_du, w_lr, b_lr, w_rl, b_rl):
            seq = jnp.transpose(x, (2, 0, 1, 3))
            seq = directional_scan(seq, w_ud, b_ud)
            seq = directional_scan(seq[::-1], w_du, b_du)[::-1]
            x = jnp.transpose(seq, (1, 2, 0, 3))
            seq = jnp.transpose(x, (3, 0, 1, 2))
            seq = directional_scan(seq, w_lr, b_lr)
            seq = directional_scan(seq[::-1], w_rl, b_rl)[::-1]
            return jnp.transpose(seq, (1, 2, 3, 0))
        key = jax.random.key(seed)
        ks = jax.random.split(key, 9)
        B, H, W = (8, 128, 256)
        fan_in = C * K
        scale = 1.0 / np.sqrt(fan_in)
        x = jax.random.normal(ks[0], (B, C, H, W), dtype=jnp.float32)
        w_ud = jax.random.uniform(ks[1], (C, C, K), jnp.float32, -scale, scale)
        b_ud = jax.random.uniform(ks[2], (C,), jnp.float32, -scale, scale)
        w_du = jax.random.uniform(ks[3], (C, C, K), jnp.float32, -scale, scale)
        b_du = jax.random.uniform(ks[4], (C,), jnp.float32, -scale, scale)
        w_lr = jax.random.uniform(ks[5], (C, C, K), jnp.float32, -scale, scale)
        b_lr = jax.random.uniform(ks[6], (C,), jnp.float32, -scale, scale)
        w_rl = jax.random.uniform(ks[7], (C, C, K), jnp.float32, -scale, scale)
        b_rl = jax.random.uniform(ks[8], (C,), jnp.float32, -scale, scale)
        return {'x': x, 'w_ud': w_ud, 'b_ud': b_ud, 'w_du': w_du, 'b_du': b_du, 'w_lr': w_lr, 'b_lr': b_lr, 'w_rl': w_rl, 'b_rl': b_rl}
    _L2_conv_all = _L2_conv_setup()
    _L2_conv_in = {k: v for k, v in _L2_conv_all.items() if k in ('w_ud', 'b_ud', 'w_du', 'b_du', 'w_lr', 'b_lr', 'w_rl', 'b_rl')}
    del _L2_conv_all

    def _L3_conv_setup():
        import jax, jax.numpy as jnp
        import numpy as np
        K = 9
        CENTER = K // 2
        EXT = 1.0
        EPS = 1e-05

        def conv2d(x, w, b, stride, padding):
            out = jax.lax.conv_general_dilated(x, w, window_strides=stride, padding=padding, dimension_numbers=('NCHW', 'OIHW', 'NCHW'))
            return out + b[None, :, None, None]

        def group_norm(x, gamma, beta, groups):
            B, C, H, W = x.shape
            xg = x.reshape(B, groups, C // groups, H, W)
            mu = xg.mean(axis=(2, 3, 4), keepdims=True)
            var = xg.var(axis=(2, 3, 4), keepdims=True)
            xn = ((xg - mu) / jnp.sqrt(var + EPS)).reshape(B, C, H, W)
            return xn * gamma[None, :, None, None] + beta[None, :, None, None]
        key = jax.random.key(seed)
        ks = jax.random.split(key, 6)
        B, Cin, Cout, H, W = (4, 32, 32, 64, 64)
        x = jax.random.normal(ks[0], (B, Cin, H, W), jnp.float32)
        w_off = jax.random.normal(ks[1], (2 * K, Cin, 3, 3), jnp.float32) * 0.05
        b_off = jax.random.normal(ks[2], (2 * K,), jnp.float32) * 0.01
        g_gn_off = jnp.ones((2 * K,), jnp.float32)
        b_gn_off = jnp.zeros((2 * K,), jnp.float32)
        w_dsc = jax.random.normal(ks[3], (Cout, Cin, K, 1), jnp.float32) * 0.05
        b_dsc = jax.random.normal(ks[4], (Cout,), jnp.float32) * 0.01
        g_gn = jnp.ones((Cout,), jnp.float32)
        b_gn = jnp.zeros((Cout,), jnp.float32)
        return {'x': x, 'w_off': w_off, 'b_off': b_off, 'g_gn_off': g_gn_off, 'b_gn_off': b_gn_off, 'w_dsc': w_dsc, 'b_dsc': b_dsc, 'g_gn': g_gn, 'b_gn': b_gn}
    _L3_conv_all = _L3_conv_setup()
    _L3_conv_in = {k: v for k, v in _L3_conv_all.items() if k in ('w_off', 'b_off', 'g_gn_off', 'b_gn_off', 'w_dsc', 'b_dsc', 'g_gn', 'b_gn')}
    del _L3_conv_all
    return {'x': x, 'L0_conv_codebooks': _L0_conv_in['codebooks'], 'L1_conv_w_hidden': _L1_conv_in['w_hidden'], 'L1_conv_b_hidden': _L1_conv_in['b_hidden'], 'L1_conv_w_dw': _L1_conv_in['w_dw'], 'L1_conv_b_dw': _L1_conv_in['b_dw'], 'L1_conv_w_proj': _L1_conv_in['w_proj'], 'L1_conv_b_proj': _L1_conv_in['b_proj'], 'L1_conv_ln_w': _L1_conv_in['ln_w'], 'L1_conv_ln_b': _L1_conv_in['ln_b'], 'L2_conv_w_ud': _L2_conv_in['w_ud'], 'L2_conv_b_ud': _L2_conv_in['b_ud'], 'L2_conv_w_du': _L2_conv_in['w_du'], 'L2_conv_b_du': _L2_conv_in['b_du'], 'L2_conv_w_lr': _L2_conv_in['w_lr'], 'L2_conv_b_lr': _L2_conv_in['b_lr'], 'L2_conv_w_rl': _L2_conv_in['w_rl'], 'L2_conv_b_rl': _L2_conv_in['b_rl'], 'L3_conv_w_off': _L3_conv_in['w_off'], 'L3_conv_b_off': _L3_conv_in['b_off'], 'L3_conv_g_gn_off': _L3_conv_in['g_gn_off'], 'L3_conv_b_gn_off': _L3_conv_in['b_gn_off'], 'L3_conv_w_dsc': _L3_conv_in['w_dsc'], 'L3_conv_b_dsc': _L3_conv_in['b_dsc'], 'L3_conv_g_gn': _L3_conv_in['g_gn'], 'L3_conv_b_gn': _L3_conv_in['b_gn']}

def reference(x, L0_conv_codebooks, L1_conv_w_hidden, L1_conv_b_hidden, L1_conv_w_dw, L1_conv_b_dw, L1_conv_w_proj, L1_conv_b_proj, L1_conv_ln_w, L1_conv_ln_b, L2_conv_w_ud, L2_conv_b_ud, L2_conv_w_du, L2_conv_b_du, L2_conv_w_lr, L2_conv_b_lr, L2_conv_w_rl, L2_conv_b_rl, L3_conv_w_off, L3_conv_b_off, L3_conv_g_gn_off, L3_conv_b_gn_off, L3_conv_w_dsc, L3_conv_b_dsc, L3_conv_g_gn, L3_conv_b_gn):
    import jax
    import jax.numpy as jnp

    def _L0_conv_ref(embeddings, codebooks):
        import jax, jax.numpy as jnp
        import numpy as np
        B, E, H, W = (16, 32, 32, 32)
        K = 512
        NC = 8
        b, e, h, w = embeddings.shape
        x = embeddings.transpose(0, 2, 3, 1).reshape(-1, e)

        def stage(res, cb):
            d = jnp.sum(res * res, axis=1, keepdims=True) - 2.0 * jnp.einsum('ne,ke->nk', res, cb) + jnp.sum(cb * cb, axis=1)
            idx = jnp.argmin(d, axis=1)
            q = cb[idx]
            return (res - q, q)
        _, qs = jax.lax.scan(stage, x, codebooks)
        quant = jnp.sum(qs, axis=0)
        return quant.reshape(b, h, w, e).transpose(0, 3, 1, 2)

    def _L1_conv_ref(x, w_hidden, b_hidden, w_dw, b_dw, w_proj, b_proj, ln_w, ln_b):
        import jax, jax.numpy as jnp
        import numpy as np
        PATCH = 8

        def _to_patches(t):
            b, c, H, W = t.shape
            t = t.reshape(b, c, H // PATCH, PATCH, W // PATCH, PATCH)
            return t.transpose(0, 1, 2, 4, 3, 5)

        def _from_patches(t):
            b, c, h, w, p1, p2 = t.shape
            return t.transpose(0, 1, 2, 4, 3, 5).reshape(b, c, h * p1, w * p2)
        hidden = jnp.einsum('bchw,oc->bohw', x, w_hidden) + b_hidden[None, :, None, None]
        hid = hidden.shape[1]
        hidden = jax.lax.conv_general_dilated(hidden, w_dw[:, None, :, :], window_strides=(1, 1), padding='SAME', feature_group_count=hid, dimension_numbers=('NCHW', 'OIHW', 'NCHW')) + b_dw[None, :, None, None]
        q, k, v = jnp.split(hidden, 3, axis=1)
        q_fft = jnp.fft.rfft2(_to_patches(q))
        k_fft = jnp.fft.rfft2(_to_patches(k))
        out = jnp.fft.irfft2(q_fft * k_fft, s=(PATCH, PATCH))
        out = _from_patches(out).astype(x.dtype)
        mu = jnp.mean(out, axis=1, keepdims=True)
        var = jnp.var(out, axis=1, keepdims=True)
        out = (out - mu) / jnp.sqrt(var + 1e-05) * ln_w[None, :, None, None] + ln_b[None, :, None, None]
        output = v * out
        return jnp.einsum('bchw,oc->bohw', output, w_proj) + b_proj[None, :, None, None]

    def _L2_conv_ref(x, w_ud, b_ud, w_du, b_du, w_lr, b_lr, w_rl, b_rl):
        import jax, jax.numpy as jnp
        import numpy as np
        from jax import lax
        C = 32
        K = 9
        PAD = 4

        def conv1d(x, w, b):
            y = lax.conv_general_dilated(x, w, window_strides=(1,), padding=[(PAD, PAD)], dimension_numbers=('NCH', 'OIH', 'NCH'))
            return y + b[None, :, None]

        def directional_scan(seq, w, b):
            first = seq[0]

            def step(carry, row):
                new = row + jax.nn.relu(conv1d(carry, w, b))
                return (new, new)
            _, rest = lax.scan(step, first, seq[1:])
            return jnp.concatenate([first[None], rest], axis=0)

        def scnn_forward(x, w_ud, b_ud, w_du, b_du, w_lr, b_lr, w_rl, b_rl):
            seq = jnp.transpose(x, (2, 0, 1, 3))
            seq = directional_scan(seq, w_ud, b_ud)
            seq = directional_scan(seq[::-1], w_du, b_du)[::-1]
            x = jnp.transpose(seq, (1, 2, 0, 3))
            seq = jnp.transpose(x, (3, 0, 1, 2))
            seq = directional_scan(seq, w_lr, b_lr)
            seq = directional_scan(seq[::-1], w_rl, b_rl)[::-1]
            return jnp.transpose(seq, (1, 2, 3, 0))
        return scnn_forward(x, w_ud, b_ud, w_du, b_du, w_lr, b_lr, w_rl, b_rl)

    def _L3_conv_ref(x, w_off, b_off, g_gn_off, b_gn_off, w_dsc, b_dsc, g_gn, b_gn):
        import jax, jax.numpy as jnp
        import numpy as np
        K = 9
        CENTER = K // 2
        EXT = 1.0
        EPS = 1e-05

        def conv2d(x, w, b, stride, padding):
            out = jax.lax.conv_general_dilated(x, w, window_strides=stride, padding=padding, dimension_numbers=('NCHW', 'OIHW', 'NCHW'))
            return out + b[None, :, None, None]

        def group_norm(x, gamma, beta, groups):
            B, C, H, W = x.shape
            xg = x.reshape(B, groups, C // groups, H, W)
            mu = xg.mean(axis=(2, 3, 4), keepdims=True)
            var = xg.var(axis=(2, 3, 4), keepdims=True)
            xn = ((xg - mu) / jnp.sqrt(var + EPS)).reshape(B, C, H, W)
            return xn * gamma[None, :, None, None] + beta[None, :, None, None]
        B, Cin, H, W = x.shape
        off = conv2d(x, w_off, b_off, (1, 1), 'SAME')
        off = jnp.tanh(group_norm(off, g_gn_off, b_gn_off, K))
        y_off = off[:, :K]
        upper = jnp.cumsum(y_off[:, CENTER + 1:], axis=1)
        lower = jnp.flip(jnp.cumsum(jnp.flip(y_off[:, :CENTER], axis=1), axis=1), axis=1)
        y_off_new = jnp.concatenate([lower, jnp.zeros_like(y_off[:, :1]), upper], axis=1)
        y_coord = jnp.arange(H, dtype=x.dtype)[None, None, :, None] + EXT * y_off_new
        x_spread = jnp.linspace(-CENTER, CENTER, K).astype(x.dtype)
        x_coord = jnp.broadcast_to(jnp.arange(W, dtype=x.dtype)[None, None, None, :] + x_spread[None, :, None, None], y_coord.shape)
        y_map = y_coord.transpose(0, 2, 1, 3).reshape(B, H * K, W)
        x_map = x_coord.transpose(0, 2, 1, 3).reshape(B, H * K, W)
        yc = jnp.clip(y_map, 0.0, H - 1.0)
        xc = jnp.clip(x_map, 0.0, W - 1.0)
        y0 = jnp.floor(yc)
        x0 = jnp.floor(xc)
        wy = yc - y0
        wx = xc - x0
        y0i = y0.astype(jnp.int32)
        x0i = x0.astype(jnp.int32)
        y1i = jnp.minimum(y0i + 1, H - 1)
        x1i = jnp.minimum(x0i + 1, W - 1)

        def samp(f, y0i, y1i, x0i, x1i, wy, wx):
            v00 = f[:, y0i, x0i]
            v01 = f[:, y0i, x1i]
            v10 = f[:, y1i, x0i]
            v11 = f[:, y1i, x1i]
            return v00 * (1 - wy) * (1 - wx) + v01 * (1 - wy) * wx + v10 * wy * (1 - wx) + v11 * wy * wx
        deformed = jax.vmap(samp)(x, y0i, y1i, x0i, x1i, wy, wx)
        out = conv2d(deformed, w_dsc, b_dsc, (K, 1), 'VALID')
        out = group_norm(out, g_gn, b_gn, w_dsc.shape[0] // 4)
        return jax.nn.relu(out)

    def _gn(v, G=32, eps=1e-05):
        B_, C_, H_, W_ = v.shape
        g = v.reshape(B_, G, C_ // G, H_, W_)
        m = jnp.mean(g, axis=(2, 3, 4), keepdims=True)
        s = jnp.var(g, axis=(2, 3, 4), keepdims=True)
        return ((g - m) / jnp.sqrt(s + eps)).reshape(v.shape)

    def _ln_c(v, eps=1e-06):
        m = jnp.mean(v, axis=1, keepdims=True)
        s = jnp.var(v, axis=1, keepdims=True)
        return (v - m) / jnp.sqrt(s + eps)

    def _ln_t(v, eps=1e-05):
        m = jnp.mean(v, axis=-1, keepdims=True)
        s = jnp.var(v, axis=-1, keepdims=True)
        return (v - m) / jnp.sqrt(s + eps)

    def _to_tokens(v):
        B_, C_, H_, W_ = v.shape
        return v.reshape(B_, C_, H_ * W_).transpose(0, 2, 1)

    def _from_tokens(t, like):
        B_, C_, H_, W_ = like.shape
        return t.transpose(0, 2, 1).reshape(B_, C_, H_, W_)
    x = x + _L0_conv_ref(_gn(x), L0_conv_codebooks)
    x = x + _L1_conv_ref(_gn(x), L1_conv_w_hidden, L1_conv_b_hidden, L1_conv_w_dw, L1_conv_b_dw, L1_conv_w_proj, L1_conv_b_proj, L1_conv_ln_w, L1_conv_ln_b)
    x = x + _L2_conv_ref(_gn(x), L2_conv_w_ud, L2_conv_b_ud, L2_conv_w_du, L2_conv_b_du, L2_conv_w_lr, L2_conv_b_lr, L2_conv_w_rl, L2_conv_b_rl)
    x = x + _L3_conv_ref(_gn(x), L3_conv_w_off, L3_conv_b_off, L3_conv_g_gn_off, L3_conv_b_gn_off, L3_conv_w_dsc, L3_conv_b_dsc, L3_conv_g_gn, L3_conv_b_gn)
    return x

_drawn_inputs = setup_inputs


def setup_inputs(seed=0):
    import zlib

    import numpy as np

    out = dict(_drawn_inputs(seed))
    spreads = {'L1_conv_ln_w': (1.0, 0.6),
     'L1_conv_ln_b': (0.0, 2.0),
     'L3_conv_g_gn_off': (1.0, 0.541),
     'L3_conv_b_gn_off': (0.0, 0.1),
     'L3_conv_g_gn': (1.0, 0.2),
     'L3_conv_b_gn': (0.0, 0.395)}
    factors = {'L0_conv_codebooks': 22.349,
     'L1_conv_b_hidden': 8.0,
     'L1_conv_b_dw': 3.242,
     'L1_conv_b_proj': 6.581,
     'L2_conv_b_ud': 3.588,
     'L2_conv_b_du': 4.569,
     'L2_conv_b_lr': 5.26,
     'L2_conv_b_rl': 6.117,
     'L3_conv_b_off': 8.0,
     'L3_conv_b_dsc': 8.0}
    for name, (base, spread) in spreads.items():
        noise = np.random.default_rng([zlib.crc32(name.encode()), seed]).standard_normal(out[name].shape)
        drawn = base * np.exp(spread * noise) if base else spread * noise
        out[name] = jnp.asarray(drawn.astype(out[name].dtype))
    for name, factor in factors.items():
        out[name] = (out[name] * factor).astype(out[name].dtype)
    return out
```

```python
from contextlib import ExitStack

import concourse.bass as bass
from concourse import mybir

F32 = mybir.dt.float32
BF16 = mybir.dt.bfloat16
F16 = mybir.dt.float16
U32 = mybir.dt.uint32
ALU = mybir.AluOpType
ACT = mybir.ActivationFunctionType
AX_X = mybir.AxisListType.X

P = 128
B, C, H, W = 16, 32, 32, 32
G = P // C
J = B // G
HW = H * W
BANK = 512
GN_EPS = 1e-5

NC, K = 8, 512
KC = K // P
HALF = HW // 2
TT = HALF // P
TILES = TT * G
PARTS = 3
LOADS = G + 2
LOWEST = -3.0e38


def block_l0(nc, ps, X, io, const):
    ident, ident16, iota, eps = const["ident"], const["ident16"], const["iota"], const["eps"]
    with ExitStack() as ctx:
        def t(name, shape, dt=F32):
            return ctx.enter_context(nc.sbuf_tensor("l0_" + name, shape, dt))

        def sem(name):
            return ctx.enter_context(nc.semaphore("l0_" + name))

        xn = t("xn", [P, HW])
        res = t("res", [P, HW])
        stats = t("stats", [P, 2, 6])
        mv = t("mv", [P, 2])
        std = t("std", [P, 1])
        rstd = t("rstd", [P, 1])
        ct_blk = t("ct_blk", [P, 2, G, K])
        csq = t("csq", [P, NC, K])
        csq_slot = t("csq_slot", [P, 2, K])
        cb = t("cb", [P, NC, KC, C])
        cb_left = t("cb_left", [P, NC, KC, C])
        cbp = t("cbp", [P, NC, PARTS, KC, C], BF16)
        cbp_slot = t("cbp_slot", [P, 2, PARTS, KC, C], BF16)
        scored = t("scored", [P, 4, K])
        top = t("top", [P, 2, TILES])
        idx8 = t("idx8", [P, 2, TILES, 8], U32)
        idx16 = t("idx16", [P, 2, TILES], F16)
        ib16 = t("ib16", [P, 2, HALF], F16)
        onehot = t("onehot", [P, 2, KC, HALF], BF16)
        ctsq = t("ctsq", [C, NC, K])

        s_in = sem("in")
        s_zero = sem("zero")
        s_sq = sem("sq")
        s_csqp = sem("csqp")
        s_csq = sem("csq")
        s_cbp = sem("cbp")
        s_slot = [sem("slot_even"), sem("slot_odd")]
        s_gn = sem("gn")
        s_std = sem("std")
        s_xn = sem("xn")
        s_init = sem("init")
        s_res = sem("res")
        s_score = sem("score")
        s_dve = sem("dve")
        s_idx = sem("idx")
        s_ibp = sem("ibp")
        s_ib = sem("ib")
        s_oh = sem("oh")
        s_pick = sem("pick")
        s_out = sem("out")
        s_alone = sem("alone")

        PER_HALF = 2 * TILES
        RES_PER_J = 2 + 2 * NC

        def max_count(n):
            return max(1, 2 * n)

        block = ctx.enter_context(nc.Block())

        def stages(eng, j, body):
            def stage(s, par, use):
                for h in range(2):
                    body(h, par, j * NC + s, j * (NC // 2) + use, s if isinstance(s, int) else None)
            stage(0, 0, 0)
            with eng.Fori(0, (NC - 2) // 2) as pair:
                stage(pair * 2 + 1, 1, pair)
                stage(pair * 2 + 2, 0, pair + 1)
            stage(NC - 1, 1, NC // 2 - 1)

        @block.sync
        def _(sp):
            sp.dma_start(cb[:], io["codes"]).then_inc(s_in, 16)
            sp.dma_start(ctsq[:], io["codes_t"].rearrange("s c k -> c s k")).then_inc(s_in, 16)

            def load(s, par):
                for g in range(G):
                    src = io["codes_t"][bass.ds(s, 1)].rearrange("s c k -> (s c) k")
                    sp.dma_start(ct_blk[C * g:C * g + C, par, g, :], src).then_inc(s_slot[par], 16)
                sp.dma_start(csq_slot[:, par, :],
                             csq[:, bass.ds(s, 1), :].rearrange("p s k -> p (s k)")).then_inc(s_slot[par], 16)
                sp.dma_start(cbp_slot[:, par].rearrange("p a k c -> p (a k c)"),
                             cbp[:, bass.ds(s, 1)].rearrange("p s a k c -> p (s a k c)")).then_inc(s_slot[par], 16)

            sp.wait_ge(s_zero, 2)
            sp.wait_ge(s_csq, NC)
            sp.wait_ge(s_cbp, 6)
            load(0, 0)
            with sp.Fori(0, J) as j:
                sp.wait_ge(s_pick, 2 * G * NC * j + 2)
                load(1, 1)
                with sp.Fori(0, (NC - 2) // 2) as pair:
                    for u in range(2):
                        s = pair * 2 + (1 + u)
                        sp.wait_ge(s_pick, (j * NC + s) * (2 * G) + 2)
                        load(s + 1, u)
                sp.wait_ge(s_pick, (j * NC + (NC - 1)) * (2 * G) + 2)
                load(0, 0)
            sp.wait_ge(s_slot[0], 16 * LOADS * (J * NC // 2 + 1))
            sp.wait_ge(s_slot[1], 16 * LOADS * (J * NC // 2))

        @block.tensor
        def _(pe):
            pe.wait_ge(s_sq, 1)
            for s in range(NC):
                pe.matmul(ps[:, s, :], const["neg_half"][0:C, :], ctsq[:, s, :],
                          start=True, stop=True).then_inc(s_csqp, 1)
            pe.wait_ge(s_csq, NC)

            def scores(h, par, hs, tt):
                for g in range(G):
                    n = G * tt + g
                    if n >= G:
                        pe.wait_ge(s_dve, hs * PER_HALF + (PER_HALF + max_count(n - G)))
                    else:
                        pe.wait_ge(s_dve, hs * PER_HALF + max_count(TILES - G + g))
                    at = HALF * h + P * tt
                    pe.matmul(ps[:, g, :], res[:, at:at + P], ct_blk[:, par, g, :],
                              start=True, stop=True).then_inc(s_score, 1)

            def spread(h, hs, g):
                if g == 0:
                    pe.wait_ge(s_idx, hs + 1)
                pe.wait_ge(s_ib, hs * G + (g + 1))
                for tt in range(TT):
                    mm = pe.matmul(ps[:, 4 + g % 2, P * tt:P * tt + P],
                                   idx16[:, h, G * tt + g:G * tt + g + 1].to_broadcast([P, P]), ident16[:],
                                   start=True, stop=True)
                mm.then_inc(s_ibp, 1)

            def pick(h, par, hs, g):
                pe.wait_ge(s_oh, hs * G + (g + 3))
                for a in range(PARTS):
                    for c in range(KC):
                        mm = pe.matmul(ps[C * g:C * g + C, 6 + h, :], cbp_slot[:, par, a, c, :],
                                       onehot[:, g % 2, c, :], start=False, stop=True, skip_group_check=True)
                mm.then_inc(s_pick, 1)

            with pe.Fori(0, J) as j:
                pe.wait_ge(s_xn, j + 1)
                pe.wait_ge(s_res, j * RES_PER_J)
                for h in range(2):
                    pe.matmul(ps[:, 6 + h, :], ident[:], xn[:, HALF * h:HALF * (h + 1)],
                              start=True, stop=True, skip_group_check=True).then_inc(s_init, 1)

                def half(h, par, st, use, s):
                    hs = st * 2 + h
                    if h == 0:
                        pe.wait_ge(s_slot[par], use * (16 * LOADS) + 16 * LOADS)
                    pe.wait_ge(s_res, hs + (j * 2 + 1))
                    if s == 0 and h == 0:
                        for tt in range(TT):
                            scores(h, par, hs, tt)
                        return
                    last, lh, lpar = hs - 1, 1 - h, par if h else 1 - par
                    scores(h, par, hs, 0)
                    spread(lh, last, 0)
                    spread(lh, last, 1)
                    scores(h, par, hs, 1)
                    pick(lh, lpar, last, 0)
                    spread(lh, last, 2)
                    pick(lh, lpar, last, 1)
                    spread(lh, last, 3)
                    scores(h, par, hs, 2)
                    pick(lh, lpar, last, 2)
                    pick(lh, lpar, last, 3)
                    scores(h, par, hs, 3)

                stages(pe, j, half)
                last = (j * NC + NC) * 2 - 1
                spread(1, last, 0)
                spread(1, last, 1)
                pick(1, 1, last, 0)
                spread(1, last, 2)
                pick(1, 1, last, 1)
                spread(1, last, 3)
                pick(1, 1, last, 2)
                pick(1, 1, last, 3)

        @block.scalar
        def _(act):
            act.sem_inc(s_ib, 2)
            act.wait_ge(s_in, 32)
            nc.scalar.activation(ctsq[:], ctsq[:], ACT.Square).then_inc(s_sq, 1)
            for s in range(NC):
                act.wait_ge(s_csqp, s + 1)
                nc.scalar.copy(csq[:, s, :], ps[:, s, :]).then_inc(s_csq, 1)
            with act.Fori(0, J) as j:
                act.wait_ge(s_gn, j * 4 + 3)
                nc.scalar.activation(std[:], mv[:, 1:2], ACT.Sqrt, bias=eps[:]).then_inc(s_std, 1)
                for h in range(2):
                    act.wait_ge(s_init, j * 2 + (h + 1))
                    nc.scalar.copy(res[:, HALF * h:HALF * (h + 1)], ps[:, 6 + h, :]).then_inc(s_res, 1)

                def half(h, par, st, use, s):
                    hs = st * 2 + h
                    act.wait_ge(s_dve, hs * PER_HALF + 2 * PER_HALF)
                    nc.scalar.copy(idx16[:, h, :], idx8[:, h, :, 0]).then_inc(s_idx, 1)
                    for g in range(G):
                        act.wait_ge(s_ibp, hs * G + (g + 1))
                        act.wait_ge(s_oh, hs * G + (g + 1))
                        nc.scalar.copy(ib16[:, g % 2, :], ps[:, 4 + g % 2, :]).then_inc(s_ib, 1)
                    act.wait_ge(s_pick, hs * G + (G + 2))
                    nc.scalar.copy(res[:, HALF * h:HALF * (h + 1)], ps[:, 6 + h, :]).then_inc(s_res, 1)

                stages(act, j, half)

        @block.gpsimd
        def _(pool):
            nc.gpsimd.memset(ct_blk[:, 0], 0.0).then_inc(s_zero, 1)
            nc.gpsimd.memset(ct_blk[:, 1], 0.0).then_inc(s_zero, 1)
            pool.sem_inc(s_oh, 2)
            with pool.Fori(0, J) as j:
                def half(h, par, st, use, s):
                    hs = st * 2 + h
                    for g in range(G):
                        pool.wait_ge(s_ib, hs * G + (g + 3))
                        pool.wait_ge(s_pick, hs * G + (g + 1))
                        pool.sem_inc(s_alone, 1)
                        for c in range(KC):
                            op = nc.gpsimd.tensor_scalar(onehot[:, g % 2, c, :], ib16[:, g % 2, :],
                                                         iota[:, c:c + 1], None, ALU.is_equal)
                        op.then_inc(s_oh, 1)

                stages(pool, j, half)

        @block.vector
        def _(dve):
            dve.sem_inc(s_dve, PER_HALF)
            dve.sem_inc(s_pick, 2)
            dve.wait_ge(s_in, 32)
            nc.vector.tensor_scalar(cbp[:, :, 0], cb[:], -1.0, None, ALU.mult).then_inc(s_cbp, 1)
            dve.wait_ge(s_cbp, 1)
            nc.vector.scalar_tensor_tensor(out=cb_left[:], in0=cb[:], scalar=-1.0, in1=cbp[:, :, 0],
                                           op0=ALU.mult, op1=ALU.subtract).then_inc(s_cbp, 1)
            dve.wait_ge(s_cbp, 2)
            nc.vector.tensor_copy(cbp[:, :, 1], cb_left[:]).then_inc(s_cbp, 1)
            dve.wait_ge(s_cbp, 3)
            nc.vector.tensor_tensor(cb[:], cb_left[:], cbp[:, :, 1], ALU.subtract).then_inc(s_cbp, 1)
            dve.wait_ge(s_cbp, 4)
            nc.vector.tensor_copy(cbp[:, :, 2], cb[:]).then_inc(s_cbp, 2)

            def maximum(h, par, n):
                nc.vector.tensor_tensor_reduce(
                    out=scored[:, n % 4, :], in0=ps[:, n % G, :], in1=csq_slot[:, par, :], scale=1.0,
                    scalar=LOWEST, op0=ALU.add, op1=ALU.max, accum_out=top[:, h, n:n + 1]).then_inc(s_dve, 1)

            def index(h, n):
                nc.vector.max_index(idx8[:, h, n, :], top[:, h, n:n + 1].to_broadcast([P, 8]),
                                    scored[:, n % 4, :]).then_inc(s_dve, 1)

            with dve.Fori(0, J) as j:
                xj = X[:, bass.ds(j * HW, HW)]
                for h in range(2):
                    nc.vector.bn_stats(stats[:, h, :], X[:, bass.ds(j * HW + h * HALF, HALF)]).then_inc(s_gn, 1)
                dve.wait_ge(s_gn, j * 4 + 2)
                dve.sem_inc(s_alone, 1)
                nc.vector.bn_aggr(mv[:], stats[:]).then_inc(s_gn, 1)
                dve.wait_ge(s_std, j + 1)
                nc.vector.reciprocal(rstd[:], std[:]).then_inc(s_gn, 1)
                dve.wait_ge(s_gn, j * 4 + 4)
                nc.vector.tensor_scalar(xn[:], xj, mv[:, 0:1], rstd[:], ALU.subtract, ALU.mult).then_inc(s_xn, 1)

                def half(h, par, st, use, s):
                    hs = st * 2 + h
                    if h == 0:
                        dve.wait_ge(s_slot[par], use * (16 * LOADS) + 16 * LOADS)
                    dve.wait_ge(s_score, hs * TILES + 1)
                    dve.wait_ge(s_dve, hs * PER_HALF + (2 * (TILES - 4) + 3))
                    dve.sem_inc(s_alone, 1)
                    maximum(h, par, 0)
                    for n in range(TILES - 1):
                        dve.wait_ge(s_score, hs * TILES + (n + 2))
                        dve.wait_ge(s_dve, hs * PER_HALF + (PER_HALF + max_count(n)))
                        dve.sem_inc(s_alone, 1)
                        maximum(h, par, n + 1)
                        index(h, n)
                    dve.wait_ge(s_dve, hs * PER_HALF + (PER_HALF + max_count(TILES - 1)))
                    dve.sem_inc(s_alone, 1)
                    index(h, TILES - 1)

                stages(dve, j, half)
                dve.wait_ge(s_res, j * RES_PER_J + RES_PER_J)
                nc.vector.tensor_tensor(xn[:], xn[:], res[:], ALU.subtract).then_inc(s_out, 1)
                dve.wait_ge(s_out, j * 2 + 1)
                nc.vector.tensor_tensor(xj, xj, xn[:], ALU.add).then_inc(s_out, 1)
                dve.wait_ge(s_out, j * 2 + 2)
                dve.sem_inc(s_alone, 1)


PATCH = 8
PAIRS = H // PATCH
TOKT = HW // P
HID = 6 * C
QC = 2 * C
PADW = W + 2
PADHW = PADW * (H + 2)
TAPROWS = 3 * C + 4
PIX = PATCH * PATCH
PRODS = 4 + 4 * (PIX - 4) // 2
LN_EPS = 1e-5


def block_l1(nc, ps, X, io, const):
    ident, eps = const["ident"], const["eps"]
    with ExitStack() as ctx:
        def t(name, shape, dt=F32):
            return ctx.enter_context(nc.sbuf_tensor("l1_" + name, shape, dt))

        def sem(name):
            return ctx.enter_context(nc.semaphore("l1_" + name))

        stats = t("stats", [P, 2, 6])
        mv = t("mv", [P, 2])
        std = t("std", [P, 1])
        rstd = t("rstd", [P, 1])
        xpad = t("xpad", [P, H + 2, PADW])
        xt = t("xt", [P, 3, 3, HW])
        xi = t("xi", [TAPROWS, 3, G, HW])
        wh = t("wh", [TAPROWS, HID])
        wd = t("wd", [TAPROWS, 3, HID])
        wc = t("wc", [TAPROWS, 3, HID])
        fa = t("fa", [P, 2, PRODS])
        fb = t("fb", [P, 2, PRODS])
        fc = t("fc", [PRODS, PIX])
        lnw = t("lnw", [P, QC])
        lnb = t("lnb", [P, QC])
        wp = t("wp", [P, 2, C])
        bp = t("bp", [P, 1])
        qkv = t("qkv", [P, 2, TOKT, HID])
        qf = t("qf", [PRODS, 2, BANK])
        prod = t("prod", [PRODS, 2, BANK])
        msum = t("msum", [P, TOKT])
        mean = t("mean", [P, TOKT])
        cen = t("cen", [P, TOKT, QC])
        sq = t("sq", [P, TOKT, QC])
        vsum = t("vsum", [P, TOKT])
        pstd = t("pstd", [P, TOKT])
        prstd = t("prstd", [P, TOKT])
        y = [t(f"y{i}", [P, TOKT, QC]) for i in range(4)]
        yt = t("yt", [P, BANK])
        biased = t("biased", [P, 2, BANK])

        s_in = sem("in")
        s_border = sem("border")
        s_wc = sem("wc")
        s_gn = sem("gn")
        s_std = sem("std")
        s_xn = sem("xn")
        s_xta = sem("xta")
        s_xtd = sem("xtd")
        s_xi = sem("xi")
        s_conv = sem("conv")
        s_qkv = sem("qkv")
        s_dft = sem("dft")
        s_qf = sem("qf")
        s_prod = sem("prod")
        s_inv = sem("inv")
        s_ln = sem("ln")
        s_sq = sem("sq")
        s_pstd = sem("pstd")
        s_pool = sem("pool")
        s_tr = sem("tr")
        s_yt = sem("yt")
        s_proj = sem("proj")
        s_biased = sem("biased")
        s_out = sem("out")
        s_alone = sem("alone")
        LN_STEPS = 7
        ACT_TAPS = 5

        def lay_tap(copy, n):
            kx, ky = divmod(n, 3)
            src = xpad[:, ky:ky + H, kx:kx + W].rearrange("p (a r) (b c) -> p a b r c", r=PATCH, c=PATCH)
            return copy(xt[:, kx, ky, :].rearrange("p (a b r c) -> p a b r c", a=PAIRS, b=PAIRS, r=PATCH), src)

        block = ctx.enter_context(nc.Block())

        @block.sync
        def _(sp):
            loads = [(wh, "l1_wh"), (wd, "l1_wd"), (fa, "l1_fa"), (fb, "l1_fb"), (fc, "l1_fc"),
                     (lnw, "l1_lnw"), (lnb, "l1_lnb"), (wp, "l1_wp"), (bp, "l1_bp")]
            for dst, name in loads:
                sp.dma_start(dst[:], io[name]).then_inc(s_in, 16)
            for g in range(G):
                sp.dma_start(xi[3 * C:TAPROWS, :, g, :], io["l1_inside"]).then_inc(s_in, 16)
            sp.wait_ge(s_in, 16 * (len(loads) + G))
            with sp.Fori(0, J) as j:
                sp.wait_ge(s_xta, j * ACT_TAPS + ACT_TAPS)
                sp.sem_inc(s_alone, 1)
                sp.wait_ge(s_xtd, j * (9 - ACT_TAPS) + (9 - ACT_TAPS))
                sp.sem_inc(s_alone, 1)
                sp.wait_ge(s_conv, j * (G * PAIRS))
                for g in range(G):
                    for kx in range(3):
                        sp.dma_start(xi[C * kx:C * kx + C, :, g, :],
                                     xt[C * g:C * g + C, kx, :, :]).then_inc(s_xi, 16)
                sp.wait_ge(s_xi, j * (16 * 3 * G) + 16 * 3 * G)
                sp.sem_inc(s_alone, 1)

        @block.tensor
        def _(pe):
            pe.wait_ge(s_wc, 1)
            pe.wait_ge(s_in, 16 * (9 + G))
            with pe.Fori(0, J) as j:
                def conv(g):
                    if g == 0:
                        pe.wait_ge(s_xi, j * (16 * 3 * G) + 16 * 3 * G)
                        pe.wait_ge(s_yt, j * G)
                    for py in range(PAIRS):
                        if g == 0 and py < 2:
                            pe.wait_ge(s_qkv, j * (G * PAIRS))
                        else:
                            pe.wait_ge(s_qkv, j * (G * PAIRS) + (g * PAIRS + py - 1))
                        for u in range(2):
                            for ky in range(3):
                                at = P * (2 * py + u)
                                mm = pe.matmul(ps[:, py % 2, HID * u:HID * (u + 1)],
                                               xi[:, ky, g, at:at + P], wc[:, ky, :],
                                               start=(ky == 0), stop=(ky == 2))
                        mm.then_inc(s_conv, 1)

                def dft(g):
                    pe.wait_ge(s_qkv, j * (G * PAIRS) + (g + 1) * PAIRS)
                    if g:
                        pe.wait_ge(s_ln, j * (G * LN_STEPS) + (g - 1) * LN_STEPS + 3)
                        pe.wait_ge(s_yt, j * G + (g - 1))
                        pe.wait_ge(s_prod, j * (2 * G) + 2 * g)
                    else:
                        pe.wait_ge(s_ln, j * (G * LN_STEPS))
                        pe.wait_ge(s_yt, j * G)
                    for h in range(2):
                        for m, at in ((fa, 0), (fb, QC)):
                            pe.matmul(ps[0:PRODS, 2 + 2 * h + (at > 0), :], m[:, h, :],
                                      qkv[:, g % 2, :, at:at + QC], start=True, stop=True).then_inc(s_dft, 1)

                def inverse(g):
                    for h in range(2):
                        pe.wait_ge(s_prod, j * (2 * G) + (2 * g + h + 1))
                        mm = pe.matmul(ps[PIX * h:PIX * (h + 1), 2, :], fc[:], prod[:, h, :],
                                       start=True, stop=True)
                    mm.then_inc(s_inv, 1)

                def project(g):
                    pe.wait_ge(s_pool, j * (3 * G) + (3 * g + 3))
                    for py in range(PAIRS):
                        mm = pe.transpose(ps[:, 3, P * py:P * (py + 1)],
                                          y[3][:, 2 * py:2 * py + 2, :].rearrange("p t c -> p (t c)"), ident[:])
                    mm.then_inc(s_tr, 1)
                    pe.wait_ge(s_yt, j * G + (g + 1))
                    if g == 0:
                        pe.wait_ge(s_biased, j * 2)
                    for u in range(2):
                        mm = pe.matmul(ps[C * g:C * g + C, 6 + u, :], wp[:, u, :], yt[:],
                                       start=True, stop=True)
                    mm.then_inc(s_proj, 1)

                conv(0)
                for g in range(G):
                    dft(g)
                    if g + 1 < G:
                        conv(g + 1)
                    inverse(g)
                    if g:
                        project(g - 1)
                project(G - 1)

        @block.scalar
        def _(act):
            with act.Fori(0, J) as j:
                act.wait_ge(s_gn, j * 4 + 3)
                nc.scalar.activation(std[:], mv[:, 1:2], ACT.Sqrt, bias=eps[:]).then_inc(s_std, 1)

                act.wait_ge(s_xn, j + 1)
                act.wait_ge(s_xi, j * (16 * 3 * G))
                for n in range(ACT_TAPS):
                    lay_tap(nc.scalar.copy, n).then_inc(s_xta, 1)

                def copy_qkv(g):
                    for py in range(PAIRS):
                        act.wait_ge(s_conv, j * (G * PAIRS) + (g * PAIRS + py + 1))
                        if g >= 2:
                            act.wait_ge(s_pool, j * (3 * G) + (3 * (g - 2) + 3))
                        else:
                            act.wait_ge(s_pool, j * (3 * G))
                        nc.scalar.copy(qkv[:, g % 2, 2 * py:2 * py + 2, :].rearrange("p t c -> p (t c)"),
                                       ps[:, py % 2, 0:2 * HID]).then_inc(s_qkv, 1)

                def copy_yt(g):
                    act.wait_ge(s_tr, j * G + (g + 1))
                    act.wait_ge(s_proj, j * G + g)
                    nc.scalar.copy(yt[:], ps[:, 3, :]).then_inc(s_yt, 1)

                copy_qkv(0)
                for g in range(G):
                    for h in range(2):
                        act.wait_ge(s_dft, j * (4 * G) + (4 * g + 2 * h + 1))
                        act.wait_ge(s_prod, j * (2 * G) + (max(0, 2 * g - 1 + h) if g else 0))
                        nc.scalar.copy(qf[:, h, :], ps[0:PRODS, 2 + 2 * h, :]).then_inc(s_qf, 1)
                    if g + 1 < G:
                        copy_qkv(g + 1)
                    act.wait_ge(s_ln, j * (G * LN_STEPS) + (g * LN_STEPS + 4))
                    nc.scalar.activation(pstd[:], vsum[:], ACT.Sqrt, bias=eps[:],
                                         scale=1.0 / QC).then_inc(s_pstd, 1)
                    if g:
                        copy_yt(g - 1)
                copy_yt(G - 1)
                act.wait_ge(s_proj, j * G + G)
                act.wait_ge(s_out, j * PAIRS)
                for u in range(2):
                    nc.scalar.activation(biased[:, u, :], ps[:, 6 + u, :], ACT.Identity,
                                         bias=bp[:]).then_inc(s_biased, 1)

        @block.gpsimd
        def _(pool):
            nc.gpsimd.memset(xpad[:], 0.0).then_inc(s_border, 1)
            pool.wait_ge(s_in, 16 * (9 + G))
            with pool.Fori(0, J) as j:
                for g in range(G):
                    v = qkv[:, g % 2, :, 2 * QC:3 * QC]
                    pool.wait_ge(s_ln, j * (G * LN_STEPS) + (g * LN_STEPS + 3))
                    nc.gpsimd.tensor_tensor(sq[:], cen[:], cen[:], ALU.mult).then_inc(s_pool, 1)
                    pool.wait_ge(s_ln, j * (G * LN_STEPS) + (g * LN_STEPS + 6))
                    nc.gpsimd.tensor_tensor(y[1][:], y[0][:], lnw[:, None, :].to_broadcast([P, TOKT, QC]),
                                            ALU.mult).then_inc(s_pool, 1)
                    pool.wait_ge(s_ln, j * (G * LN_STEPS) + (g * LN_STEPS + 7))
                    pool.wait_ge(s_tr, j * G + g)
                    nc.gpsimd.tensor_tensor(y[3][:], y[2][:], v, ALU.mult).then_inc(s_pool, 1)

        @block.vector
        def _(dve):
            dve.wait_ge(s_in, 16 * (9 + G))
            nc.vector.tensor_tensor(wc[:], wd[:], wh[:, None, :].to_broadcast([TAPROWS, 3, HID]),
                                    ALU.mult).then_inc(s_wc, 1)
            dve.wait_ge(s_border, 1)
            with dve.Fori(0, J) as j:
                for h in range(2):
                    nc.vector.bn_stats(stats[:, h, :],
                                       X[:, bass.ds(j * HW + h * HALF, HALF)]).then_inc(s_gn, 1)
                dve.wait_ge(s_gn, j * 4 + 2)
                dve.sem_inc(s_alone, 1)
                nc.vector.bn_aggr(mv[:], stats[:]).then_inc(s_gn, 1)
                dve.wait_ge(s_std, j + 1)
                nc.vector.reciprocal(rstd[:], std[:]).then_inc(s_gn, 1)
                dve.wait_ge(s_gn, j * 4 + 4)
                dve.wait_ge(s_xta, j * ACT_TAPS)
                inside = xpad[:, 1:H + 1, 1:W + 1]
                nc.vector.tensor_scalar(inside, X[:, bass.ds(j * HW, HW)].rearrange("p (y x) -> p y x", x=W),
                                        mv[:, 0:1], rstd[:], ALU.subtract, ALU.mult).then_inc(s_xn, 1)
                dve.wait_ge(s_xn, j + 1)
                dve.wait_ge(s_xi, j * (16 * 3 * G))
                for n in range(ACT_TAPS, 9):
                    lay_tap(nc.vector.tensor_copy, n).then_inc(s_xtd, 1)
                for g in range(G):
                    for h in range(2):
                        dve.wait_ge(s_dft, j * (4 * G) + (4 * g + 2 * h + 2))
                        dve.wait_ge(s_qf, j * (2 * G) + (2 * g + h + 1))
                        nc.vector.tensor_tensor(prod[:, h, :], qf[:, h, :], ps[0:PRODS, 3 + 2 * h, :],
                                                ALU.mult).then_inc(s_prod, 1)
                    base = g * LN_STEPS
                    patches = ps[:, 2, :].rearrange("p (t c) -> p t c", c=QC)
                    dve.wait_ge(s_inv, j * G + (g + 1))
                    nc.vector.tensor_reduce(msum[:], patches, AX_X, ALU.add).then_inc(s_ln, 1)
                    dve.wait_ge(s_ln, j * (G * LN_STEPS) + (base + 1))
                    nc.vector.tensor_scalar(mean[:], msum[:], 1.0 / QC, None, ALU.mult).then_inc(s_ln, 1)
                    dve.wait_ge(s_ln, j * (G * LN_STEPS) + (base + 2))
                    nc.vector.tensor_tensor(cen[:], patches, mean[:, :, None].to_broadcast([P, TOKT, QC]),
                                            ALU.subtract).then_inc(s_ln, 1)
                    dve.wait_ge(s_pool, j * (3 * G) + (3 * g + 1))
                    nc.vector.tensor_reduce(vsum[:], sq[:], AX_X, ALU.add).then_inc(s_ln, 1)
                    dve.wait_ge(s_pstd, j * G + (g + 1))
                    nc.vector.reciprocal(prstd[:], pstd[:]).then_inc(s_ln, 1)
                    dve.wait_ge(s_ln, j * (G * LN_STEPS) + (base + 5))
                    nc.vector.tensor_tensor(y[0][:], cen[:], prstd[:, :, None].to_broadcast([P, TOKT, QC]),
                                            ALU.mult).then_inc(s_ln, 1)
                    dve.wait_ge(s_pool, j * (3 * G) + (3 * g + 2))
                    nc.vector.tensor_tensor(y[2][:], y[1][:], lnb[:, None, :].to_broadcast([P, TOKT, QC]),
                                            ALU.add).then_inc(s_ln, 1)
                xj = X[:, bass.ds(j * HW, HW)].rearrange("p (a r b c) -> p b a r c", r=PATCH, b=PAIRS, c=PATCH)
                for u in range(2):
                    dve.wait_ge(s_biased, j * 2 + (u + 1))
                    src = biased[:, u, :].rearrange("p (a x r c) -> p x a r c", x=2, r=PATCH, c=PATCH)
                    for x in range(2):
                        nc.vector.tensor_tensor(xj[:, 2 * u + x], xj[:, 2 * u + x], src[:, x],
                                                ALU.add).then_inc(s_out, 1)
                dve.wait_ge(s_out, j * PAIRS + PAIRS)
                dve.sem_inc(s_alone, 1)


TAPS = 9
MARGIN = TAPS // 2
PITCH = W + 2 * MARGIN
STEPS = H - 1
DIRS = 4


def block_l2(nc, ps, X, io, const):
    ident, eps = const["ident"], const["eps"]
    with ExitStack() as ctx:
        def t(name, shape, dt=F32):
            return ctx.enter_context(nc.sbuf_tensor("l2_" + name, shape, dt))

        def sem(name):
            return ctx.enter_context(nc.semaphore("l2_" + name))

        stats = t("stats", [P, J, 2, 6])
        mv = t("mv", [P, J, 2])
        std = t("std", [P, J])
        rstd = t("rstd", [P, J])
        seq = t("seq", [P, J, PITCH * PITCH])
        wt = t("wt", [P, DIRS, TAPS, P])
        bias = t("bias", [P, DIRS])

        s_in = sem("in")
        s_border = sem("border")
        s_gn = sem("gn")
        s_std = sem("std")
        s_xn = sem("xn")
        s_z = sem("z")
        s_line = sem("line")
        s_out = sem("out")
        s_alone = sem("alone")

        image = seq[:].rearrange("p j (y x) -> p j y x", x=PITCH)

        def line(d, n, shift=MARGIN):
            if d < 2:
                return seq[:, :, bass.ds(n * PITCH + (MARGIN * PITCH + shift), W)]
            return image[:, :, shift:shift + H, bass.ds(n + MARGIN, 1)].rearrange("p j y x -> p j (y x)")

        def scan(eng, step):
            for d in range(DIRS):
                step(d, 0, STEPS * d % 2, STEPS * d)
                with eng.Fori(0, STEPS // 2) as pair:
                    for u in range(2):
                        step(d, pair * 2 + (1 + u), (STEPS * d + 1 + u) % 2, pair * 2 + (1 + u + STEPS * d))

        def current(d, i):
            return i + 1 if d % 2 == 0 else i * -1 + (STEPS - 1)

        def previous(d, i):
            return i + 0 if d % 2 == 0 else i * -1 + STEPS

        block = ctx.enter_context(nc.Block())

        @block.sync
        def _(sp):
            sp.dma_start(wt[:], io["l2_w"]).then_inc(s_in, 16)
            sp.dma_start(bias[:], io["l2_b"]).then_inc(s_in, 16)
            sp.wait_ge(s_in, 32)

        @block.gpsimd
        def _(pool):
            nc.gpsimd.memset(seq[:], 0.0).then_inc(s_border, 1)

        @block.tensor
        def _(pe):
            pe.wait_ge(s_in, 32)
            pe.wait_ge(s_xn, J)

            def step(d, i, parity, n):
                z = ps[:, parity, 0:J * W].rearrange("p (j w) -> p j w", j=J)
                if isinstance(i, int):
                    pe.wait_ge(s_line, n + 1)
                pe.matmul(z, ident[:], line(d, current(d, i)), start=True, stop=False)
                pe.wait_ge(s_line, n + 1)
                for k in range(TAPS):
                    mm = pe.matmul(z, wt[:, d, k, :], line(d, previous(d, i), k), start=False,
                                   stop=(k == TAPS - 1))
                mm.then_inc(s_z, 1)

            scan(pe, step)

        @block.scalar
        def _(act):
            act.wait_ge(s_gn, 3 * J)
            nc.scalar.activation(std[:], mv[:, :, 1], ACT.Sqrt, bias=eps[:]).then_inc(s_std, 1)

        @block.vector
        def _(dve):
            dve.sem_inc(s_line, 1)
            for j in range(J):
                for h in range(2):
                    at = j * HW + h * HALF
                    nc.vector.bn_stats(stats[:, j, h, :], X[:, at:at + HALF]).then_inc(s_gn, 1)
            dve.wait_ge(s_gn, 2 * J)
            for j in range(J):
                nc.vector.bn_aggr(mv[:, j, :], stats[:, j]).then_inc(s_gn, 1)
            dve.wait_ge(s_std, 1)
            nc.vector.reciprocal(rstd[:], std[:]).then_inc(s_gn, 1)
            dve.wait_ge(s_gn, 3 * J + 1)
            dve.wait_ge(s_border, 1)
            for j in range(J):
                nc.vector.tensor_scalar(image[:, j, MARGIN:MARGIN + H, MARGIN:MARGIN + W],
                                        X[:, j * HW:(j + 1) * HW].rearrange("p (y x) -> p y x", x=W),
                                        mv[:, j, 0:1], rstd[:, j:j + 1], ALU.subtract,
                                        ALU.mult).then_inc(s_xn, 1)
            dve.wait_ge(s_xn, J)

            def step(d, i, parity, n):
                dve.wait_ge(s_z, n + 1)
                z = ps[:, parity, 0:J * W].rearrange("p (j w) -> p j w", j=J)
                row = line(d, current(d, i))
                nc.vector.scalar_tensor_tensor(out=row, in0=z, scalar=bias[:, d:d + 1], in1=row,
                                               op0=ALU.add, op1=ALU.max).then_inc(s_line, 1)

            scan(dve, step)
            dve.wait_ge(s_line, DIRS * STEPS + 1)
            for j in range(J):
                xj = X[:, j * HW:(j + 1) * HW].rearrange("p (y x) -> p y x", x=W)
                nc.vector.tensor_tensor(xj, xj, image[:, j, MARGIN:MARGIN + H, MARGIN:MARGIN + W],
                                        ALU.add).then_inc(s_out, 1)
            dve.wait_ge(s_out, J)


SNAKE = 9
MID = SNAKE // 2
EPITCH = W + 2 * MID
OFFC = SNAKE + 1
POINTS = [k for d in range(1, MID + 1) for k in (MID - d, MID + d)]
ITEMS = [(k, m) for k in POINTS for m in range(abs(k - MID))]
RING = 6


def l3_schedule():
    operands, used = [], {}
    n = 0
    while n < len(ITEMS):
        k, m = ITEMS[n]
        both = n + 1 < len(ITEMS) and ITEMS[n + 1][0] == k
        operands.append((k, n, n + 1 if both else None))
        used[n] = len(operands)
        if both:
            used[n + 1] = len(operands)
        n += 2 if both else 1
    return operands, used


def block_l3(nc, ps, X, io, const):
    eps = const["eps"]
    operands, used = l3_schedule()
    quads = [(n, n2) for _, n, n2 in operands if n2 is not None]
    with ExitStack() as ctx:
        def t(name, shape, dt=F32):
            return ctx.enter_context(nc.sbuf_tensor("l3_" + name, shape, dt))

        def sem(name):
            return ctx.enter_context(nc.semaphore("l3_" + name))

        stats = t("stats", [P, 2, 6])
        mv = t("mv", [P, 2])
        std = t("std", [P, 1])
        rstd = t("rstd", [P, 1])
        xz = t("xz", [P, H + 2, PADW])
        xe = t("xe", [P, EPITCH, EPITCH])
        down = t("down", [P, EPITCH - 1, EPITCH])
        up = t("up", [P, EPITCH - 1, EPITCH])
        w_off = t("w_off", [P, 9, P])
        w_dsc = t("w_dsc", [P, SNAKE, P])
        sums = t("sums", [P, len(POINTS), P])
        cols = t("cols", [P, 6])
        avg = t("avg", [P, 2, P])
        minus = t("minus", [P, MID])
        raw = t("raw", [P, 2, HW])
        gstat = t("gstat", [P, 2, 8])
        off = t("off", [P, HW])
        ramp = t("ramp", [P, 4, HW])
        term = t("term", [P, 4, HW])
        isum = t("isum", [P, RING, HW])
        y = t("y", [P, HW])

        s_in = sem("in")
        s_border = sem("border")
        s_gn = sem("gn")
        s_std = sem("std")
        s_xn = sem("xn")
        s_edge = sem("edge")
        s_dy = sem("dy")
        s_conv = sem("conv")
        s_raw = sem("raw")
        s_gs = sem("gs")
        s_gavg = sem("gavg")
        s_gstd = sem("gstd")
        s_off = sem("off")
        s_cum = sem("cum")
        s_ramp = sem("ramp")
        s_term = sem("term")
        s_sum = sem("sum")
        s_quad = sem("quad")
        s_used = sem("used")
        s_y = sem("y")
        s_out = sem("out")
        s_alone = sem("alone")
        GS = 9
        NI, NO, NQ = len(ITEMS), len(operands), len(quads)
        first = {k: next(n for n, it in enumerate(ITEMS) if it[0] == k) for k in POINTS}

        block = ctx.enter_context(nc.Block())

        @block.sync
        def _(sp):
            for dst, name in ((w_off, "l3_w_off"), (w_dsc, "l3_w_dsc"), (sums, "l3_sums"), (cols, "l3_cols"),
                              (avg, "l3_avg"), (minus, "l3_minus")):
                sp.dma_start(dst[:], io[name]).then_inc(s_in, 16)
            sp.wait_ge(s_in, 16 * 6)

        @block.tensor
        def _(pe):
            pe.wait_ge(s_in, 16 * 6)
            with pe.Fori(0, J) as j:
                def group_averages(norm):
                    for a in range(2):
                        pe.wait_ge(s_gs, j * (2 * GS) + (GS * norm + (3 if a == 0 else 5)))
                        pe.matmul(ps[:, 0, 8 * norm + a:8 * norm + a + 1], avg[:, norm, :],
                                  mv[:, 0:1] if a == 0 else gstat[:, norm, 1:2],
                                  start=True, stop=True).then_inc(s_gavg, 1)

                pe.wait_ge(s_xn, j * 2 + 1)
                pe.wait_ge(s_ramp, j * (2 * NI))
                for h in range(2):
                    for n in range(9):
                        ky, kx = divmod(n, 3)
                        mm = pe.matmul(ps[:, 2 + h, :].rearrange("p (y x) -> p y x", x=W), w_off[:, n, :],
                                       xz[:, ky + H // 2 * h:ky + H // 2 * (h + 1), kx:kx + W],
                                       start=(n == 0), stop=(n == 8))
                mm.then_inc(s_conv, 1)
                pe.wait_ge(s_edge, j * 4 + 4)
                pe.wait_ge(s_raw, j * 4)
                for k in range(SNAKE):
                    for h in range(2):
                        pe.matmul(ps[:, 6 + h, :].rearrange("p (y x) -> p y x", x=W), w_dsc[:, k, :],
                                  xe[:, MID + H // 2 * h:MID + H // 2 * (h + 1), k:k + W],
                                  start=(k == 0), stop=False, skip_group_check=True)
                group_averages(0)

                def running_sum(c):
                    if c >= 2:
                        pe.wait_ge(s_ramp, j * (2 * NI) + 2 * (first[POINTS[c - 2]] + abs(POINTS[c - 2] - MID)))
                    for h in range(2):
                        mm = pe.matmul(ps[:, 2 + 2 * (c % 2) + h, :], sums[:, c, :],
                                       off[:, HALF * h:HALF * (h + 1)], start=True, stop=True)
                    mm.then_inc(s_cum, 1)

                pe.wait_ge(s_off, j + 1)
                running_sum(0)
                running_sum(1)
                done = 2
                for q, (k, n, n2) in enumerate(operands):
                    c = POINTS.index(k)
                    while done < min(c + 2, len(POINTS)):
                        running_sum(done)
                        done += 1
                    if n2 is None:
                        pe.wait_ge(s_sum, j * NI + (n + 1))
                    else:
                        pe.wait_ge(s_quad, j * NQ + (quads.index((n, n2)) + 1))
                    for h in range(2):
                        mm = pe.matmul(ps[:, 6 + h, :], w_dsc[:, k, :],
                                       isum[:, n % RING, HALF * h:HALF * (h + 1)],
                                       start=False, stop=(q == NO - 1), skip_group_check=True)
                    mm.then_inc(s_used, 1)
                group_averages(1)

        @block.scalar
        def _(act):
            act.wait_ge(s_in, 16 * 6)
            with act.Fori(0, J) as j:
                act.wait_ge(s_gn, j * 4 + 3)
                nc.scalar.activation(std[:], mv[:, 1:2], ACT.Sqrt, bias=eps[:]).then_inc(s_std, 1)

                def copy_out(norm):
                    if norm == 0:
                        act.wait_ge(s_conv, j + 1)
                    else:
                        act.wait_ge(s_used, j * NO + NO)
                    for h in range(2):
                        nc.scalar.activation(raw[:, norm, HALF * h:HALF * (h + 1)],
                                             ps[:, (6 if norm else 2) + h, :], ACT.Identity,
                                             bias=cols[:, 3 * norm:3 * norm + 1]).then_inc(s_raw, 1)
                    act.wait_ge(s_gavg, j * 4 + (2 * norm + 2))
                    nc.scalar.activation(gstat[:, norm, 2:3], ps[:, 0, 8 * norm + 1:8 * norm + 2], ACT.Sqrt,
                                         bias=eps[:]).then_inc(s_gstd, 1)
                    act.wait_ge(s_gs, j * (2 * GS) + (GS * norm + GS))

                copy_out(0)
                nc.scalar.activation(off[:], raw[:, 0, :], ACT.Tanh, bias=gstat[:, 0, 5:6],
                                     scale=gstat[:, 0, 4:5]).then_inc(s_off, 1)
                for n, (k, m) in enumerate(ITEMS):
                    c = POINTS.index(k)
                    act.wait_ge(s_cum, j * len(POINTS) + (c + 1))
                    for e, sign in enumerate((1.0, -1.0)):
                        act.wait_ge(s_term, j * (2 * NI) + max(0, 2 * n + e - 3))
                        b = 2 + 2 * (c % 2)
                        nc.scalar.activation(ramp[:, (2 * n + e) % 4, :],
                                             ps[:, b:b + 2, :].rearrange("p b f -> p (b f)"), ACT.Relu,
                                             bias=minus[:, m:m + 1], scale=sign).then_inc(s_ramp, 1)
                copy_out(1)
                act.wait_ge(s_out, j)
                nc.scalar.activation(y[:], raw[:, 1, :], ACT.Relu, bias=gstat[:, 1, 5:6],
                                     scale=gstat[:, 1, 4:5]).then_inc(s_y, 1)

        @block.gpsimd
        def _(pool):
            nc.gpsimd.memset(xz[:], 0.0).then_inc(s_border, 1)
            with pool.Fori(0, J) as j:
                a, b = MID, MID + W
                edges = [(xe[:, a:b, 0:a], xe[:, a:b, a:a + 1].to_broadcast([P, H, MID])),
                         (xe[:, a:b, b:], xe[:, a:b, b - 1:b].to_broadcast([P, H, MID])),
                         (xe[:, 0:a, :], xe[:, a:a + 1, :].to_broadcast([P, MID, EPITCH])),
                         (xe[:, b:, :], xe[:, b - 1:b, :].to_broadcast([P, MID, EPITCH]))]
                pool.wait_ge(s_xn, j * 2 + 2)
                pool.sem_inc(s_alone, 1)
                for i, (dst, src) in enumerate(edges):
                    if i == 2:
                        pool.wait_ge(s_edge, j * 4 + 2)
                        pool.sem_inc(s_alone, 1)
                    nc.gpsimd.tensor_copy(dst, src).then_inc(s_edge, 1)
                for n in range(NI):
                    pool.wait_ge(s_term, j * (2 * NI) + (2 * n + 2))
                    pool.wait_ge(s_used, j * NO + (used[n - RING] if n >= RING else 0))
                    nc.gpsimd.tensor_tensor(isum[:, n % RING, :], term[:, 2 * n % 4, :],
                                            term[:, (2 * n + 1) % 4, :], ALU.add).then_inc(s_sum, 1)

        @block.vector
        def _(dve):
            dve.wait_ge(s_border, 1)
            dve.wait_ge(s_in, 16 * 6)
            with dve.Fori(0, J) as j:
                xj = X[:, bass.ds(j * HW, HW)]
                for h in range(2):
                    nc.vector.bn_stats(stats[:, h, :], X[:, bass.ds(j * HW + h * HALF, HALF)]).then_inc(s_gn, 1)
                dve.wait_ge(s_gn, j * 4 + 2)
                dve.sem_inc(s_alone, 1)
                nc.vector.bn_aggr(mv[:], stats[:]).then_inc(s_gn, 1)
                dve.wait_ge(s_std, j + 1)
                nc.vector.reciprocal(rstd[:], std[:]).then_inc(s_gn, 1)
                dve.wait_ge(s_gn, j * 4 + 4)
                rows = xj.rearrange("p (y x) -> p y x", x=W)
                for dst in (xz[:, 1:H + 1, 1:W + 1], xe[:, MID:MID + H, MID:MID + W]):
                    nc.vector.tensor_scalar(dst, rows, mv[:, 0:1], rstd[:], ALU.subtract,
                                            ALU.mult).then_inc(s_xn, 1)
                dve.wait_ge(s_edge, j * 4 + 4)
                nc.vector.tensor_tensor(down[:], xe[:, 1:, :], xe[:, :-1, :], ALU.subtract).then_inc(s_dy, 1)
                nc.vector.tensor_tensor(up[:], xe[:, :-1, :], xe[:, 1:, :], ALU.subtract).then_inc(s_dy, 1)

                def group_norm(norm):
                    base = GS * norm

                    def after(n):
                        dve.wait_ge(s_gs, j * (2 * GS) + (base + n))

                    g = gstat[:, norm, :]
                    mean, var = ps[:, 0, 8 * norm:8 * norm + 1], mv[:, 1:2]
                    for h in range(2):
                        dve.wait_ge(s_raw, j * 4 + (2 * norm + h + 1))
                        nc.vector.bn_stats(stats[:, h, :],
                                           raw[:, norm, HALF * h:HALF * (h + 1)]).then_inc(s_gs, 1)
                    after(2)
                    dve.sem_inc(s_alone, 1)
                    nc.vector.bn_aggr(mv[:], stats[:]).then_inc(s_gs, 1)
                    dve.wait_ge(s_gavg, j * 4 + (2 * norm + 1))
                    nc.vector.tensor_tensor(g[:, 0:1], mv[:, 0:1], mean, ALU.subtract).then_inc(s_gs, 1)
                    after(4)
                    nc.vector.scalar_tensor_tensor(out=g[:, 1:2], in0=g[:, 0:1], scalar=g[:, 0:1], in1=var,
                                                   op0=ALU.mult, op1=ALU.add).then_inc(s_gs, 1)
                    dve.wait_ge(s_gstd, j * 2 + (norm + 1))
                    nc.vector.reciprocal(g[:, 3:4], g[:, 2:3]).then_inc(s_gs, 1)
                    after(6)
                    nc.vector.tensor_tensor(g[:, 4:5], g[:, 3:4], cols[:, 3 * norm + 1:3 * norm + 2],
                                            ALU.mult).then_inc(s_gs, 1)
                    after(7)
                    nc.vector.tensor_tensor(g[:, 6:7], g[:, 4:5], mean, ALU.mult).then_inc(s_gs, 1)
                    after(8)
                    nc.vector.tensor_tensor(g[:, 5:6], cols[:, 3 * norm + 2:3 * norm + 3], g[:, 6:7],
                                            ALU.subtract).then_inc(s_gs, 1)

                group_norm(0)
                dve.wait_ge(s_dy, j * 2 + 2)

                def add_quad(i):
                    n, n2 = quads[i]
                    dve.wait_ge(s_sum, j * NI + (n2 + 1))
                    nc.vector.tensor_tensor(isum[:, n % RING, :], isum[:, n % RING, :],
                                            isum[:, n2 % RING, :], ALU.add).then_inc(s_quad, 1)

                added = 0
                for n, (k, m) in enumerate(ITEMS):
                    for e, (rows, at) in enumerate(((down, MID + m), (up, MID - m - 1))):
                        q = 2 * n + e
                        dve.wait_ge(s_ramp, j * (2 * NI) + (q + 1))
                        dve.wait_ge(s_sum, j * NI + max(0, n - 1))
                        nc.vector.scalar_tensor_tensor(
                            out=term[:, q % 4, :].rearrange("p (y x) -> p y x", x=W),
                            in0=ramp[:, q % 4, :].rearrange("p (y x) -> p y x", x=W), scalar=1.0,
                            in1=rows[:, at:at + H, k:k + W], op0=ALU.min, op1=ALU.mult).then_inc(s_term, 1)
                    while added < NQ and quads[added][1] <= n - 2:
                        add_quad(added)
                        added += 1
                while added < NQ:
                    add_quad(added)
                    added += 1
                group_norm(1)
                dve.wait_ge(s_y, j + 1)
                nc.vector.tensor_tensor(xj, xj, y[:], ALU.add).then_inc(s_out, 1)
                dve.wait_ge(s_out, j + 1)
                dve.sem_inc(s_alone, 1)


CONSTS = ["ident", "ident16", "iota", "eps", "neg_half"]


def dft_matrices(np):
    y, x = np.divmod(np.arange(PIX), PATCH)
    fa, fb, fc, seen = [], [], [], set()
    for v in range(PATCH):
        for u in range(PATCH):
            if (v, u) in seen:
                continue
            mirror = (-v % PATCH, -u % PATCH)
            seen |= {(v, u), mirror}
            angle = 2 * np.pi * ((v * y + u * x) % PATCH) / PATCH
            re, im = np.cos(angle), -np.sin(angle)
            if mirror == (v, u):
                fa, fb, fc = fa + [re], fb + [re], fc + [re / PIX]
            else:
                fa += [re, im, re, im]
                fb += [re, im, im, re]
                fc += [2 * re / PIX, -2 * re / PIX, 2 * im / PIX, 2 * im / PIX]
    fa, fb, fc = (np.array(m).astype(np.float32) for m in (fa, fb, fc))
    sides = np.zeros((2, P, 2, PRODS), np.float32)
    for n, m in enumerate((fa, fb)):
        for h in range(2):
            sides[n, PIX * h:PIX * (h + 1), h] = m.T
    return sides[0], sides[1], fc


def lay_out(inputs, np):
    f = np.float32
    a = {"x": np.ascontiguousarray(inputs["x"])}
    books = np.asarray(inputs["L0_conv_codebooks"])
    a["codes"] = np.ascontiguousarray(books.reshape(NC, KC, P, C).transpose(2, 0, 1, 3))
    a["codes_t"] = np.ascontiguousarray(books.transpose(0, 2, 1))
    a["ident"] = np.eye(P, dtype=f)
    a["ident16"] = np.eye(P, dtype=np.float16)
    a["iota"] = (np.arange(P)[:, None] + P * np.arange(KC)[None, :]).astype(f)
    a["eps"] = np.full((P, 1), GN_EPS, f)
    a["neg_half"] = np.full((P, P), -0.5, f)

    wh, wdw = np.asarray(inputs["L1_conv_w_hidden"]), np.asarray(inputs["L1_conv_w_dw"])
    bh, bdw = np.asarray(inputs["L1_conv_b_hidden"]), np.asarray(inputs["L1_conv_b_dw"])
    a["l1_wh"] = np.concatenate([np.tile(wh.T, (3, 1)), np.tile(bh[None], (3, 1)), bdw[None]])
    by_tap = wdw.transpose(2, 1, 0)
    a["l1_wd"] = np.concatenate([np.repeat(by_tap, C, axis=0), by_tap,
                                 np.tile(np.array([0, 1, 0], f)[None, :, None], (1, 1, HID))])
    inside = np.zeros((H + 2, PADW), f)
    inside[1:H + 1, 1:W + 1] = 1
    taps = np.array([[inside[ky:ky + H, kx:kx + W] for ky in range(3)] for kx in range(3)] + [np.ones((3, H, W))])
    a["l1_inside"] = taps.reshape(4, 3, PAIRS, PATCH, PAIRS, PATCH).transpose(0, 1, 2, 4, 3, 5).reshape(
        4, 3, HW).astype(f)
    a["l1_fa"], a["l1_fb"], a["l1_fc"] = dft_matrices(np)
    a["l1_lnw"] = np.tile(np.asarray(inputs["L1_conv_ln_w"])[None], (P, 1))
    a["l1_lnb"] = np.tile(np.asarray(inputs["L1_conv_ln_b"])[None], (P, 1))
    wp = np.asarray(inputs["L1_conv_w_proj"]).T
    none = np.zeros((QC, C), f)
    a["l1_wp"] = np.stack([np.concatenate([wp, none]), np.concatenate([none, wp])], axis=1)
    a["l1_bp"] = np.tile(np.asarray(inputs["L1_conv_b_proj"]), G)[:, None]

    w = np.zeros((G, C, DIRS, TAPS, G, C), f)
    names = ("ud", "du", "lr", "rl")
    for d, n in enumerate(names):
        for g in range(G):
            w[g, :, d, :, g, :] = np.asarray(inputs["L2_conv_w_" + n]).transpose(1, 2, 0)
    a["l2_w"] = w.reshape(P, DIRS, TAPS, P)
    a["l2_b"] = np.stack([np.tile(np.asarray(inputs["L2_conv_b_" + n]), G) for n in names], axis=1)

    def blocks(w, taps):
        m = np.zeros((G, C, taps, G, C), f)
        for g in range(G):
            m[g, :, :, g, 0:w.shape[0]] = w.transpose(1, 2, 0)
        return m.reshape(P, taps, P)

    def column(v):
        m = np.zeros((G, C), f)
        m[:, 0:len(v)] = v
        return m.reshape(P)

    g_in = {n: np.asarray(inputs["L3_conv_" + n]) for n in
            ("w_off", "b_off", "g_gn_off", "b_gn_off", "w_dsc", "b_dsc", "g_gn", "b_gn")}
    a["l3_w_off"] = blocks(g_in["w_off"][:OFFC].reshape(OFFC, C, 9), 9)
    a["l3_w_dsc"] = blocks(g_in["w_dsc"].reshape(C, C, SNAKE), SNAKE)
    a["l3_cols"] = np.stack([column(g_in["b_off"][:OFFC]), column(g_in["g_gn_off"][:OFFC]),
                             column(g_in["b_gn_off"][:OFFC]), column(g_in["b_dsc"]), column(g_in["g_gn"]),
                             column(g_in["b_gn"])], axis=1)
    sums = np.zeros((G, C, len(POINTS), G, C), f)
    for c, k in enumerate(POINTS):
        for i in range(k, MID) if k < MID else range(MID + 1, k + 1):
            for g in range(G):
                sums[g, i, c, g, :] = 1
    a["l3_sums"] = sums.reshape(P, len(POINTS), P)
    at = np.arange(P)
    a["l3_avg"] = np.stack([(at[:, None] // n == at[None, :] // n).astype(f) / f(n) for n in (2, 4)], axis=1)
    a["l3_minus"] = np.tile(-np.arange(MID, dtype=f)[None], (P, 1))
    return {n: np.ascontiguousarray(v) for n, v in a.items()}


def build_program(nc, io, out):
    with ExitStack() as ctx:
        def t(name, shape, dt=F32):
            return ctx.enter_context(nc.sbuf_tensor(name, shape, dt))

        X = t("X", [P, J * HW])
        ps = ctx.enter_context(nc.psum_tensor("ps", [P, 8, BANK], F32))
        const = {name: t("c_" + name, list(io[name].shape), io[name].dtype) for name in CONSTS}
        s_load = ctx.enter_context(nc.semaphore("load"))
        s_store = ctx.enter_context(nc.semaphore("store"))
        with nc.Block() as block:
            @block.sync
            def _(sp):
                for g in range(G):
                    sp.dma_start(X[C * g:C * g + C, :].rearrange("c (j f) -> c j f", j=J),
                                 io["x"][J * g:J * g + J].rearrange("j c h w -> c j (h w)")).then_inc(s_load, 16)
                for name in CONSTS:
                    sp.dma_start(const[name][:], io[name]).then_inc(s_load, 16)
                sp.wait_ge(s_load, 16 * (G + len(CONSTS)))
        for layer in LAYERS:
            layer(nc, ps, X, io, const)
        with nc.Block() as block:
            @block.sync
            def _(sp):
                for g in range(G):
                    sp.dma_start(out[J * g:J * g + J].rearrange("j c h w -> c j (h w)"),
                                 X[C * g:C * g + C, :].rearrange("c (j f) -> c j f", j=J)).then_inc(s_store, 16)
                sp.wait_ge(s_store, 16 * G)


LAYERS = [block_l0, block_l1, block_l2, block_l3]


def kernel(**inputs):
    import numpy as np
    import concourse.bacc as bacc
    from concourse.bass_utils import run_bass_kernel_spmd

    arrays = lay_out(inputs, np)
    nc = bacc.Bacc("TRN2", target_bir_lowering=False, num_devices=1)
    io = {n: nc.dram_tensor("in_" + n, a.shape, mybir.dt.from_np(a.dtype), kind="ExternalInput").ap()
          for n, a in arrays.items()}
    out = nc.dram_tensor("out", (B, C, H, W), F32, kind="ExternalOutput").ap()
    build_program(nc, io, out)
    r = run_bass_kernel_spmd(nc, [{"in_" + n: a for n, a in arrays.items()}], core_ids=[0])
    return r.results[0]["out"]
```

```python
from contextlib import ExitStack

import concourse.bass as bass
from concourse import mybir

F32 = mybir.dt.float32
BF16 = mybir.dt.bfloat16
F16 = mybir.dt.float16
U32 = mybir.dt.uint32
ALU = mybir.AluOpType
ACT = mybir.ActivationFunctionType
AX_X = mybir.AxisListType.X

P = 128
B, C, H, W = 16, 32, 32, 32
G = P // C
J = B // G
HW = H * W
BANK = 512
GN_EPS = 1e-5
START = 1

NC, K = 8, 512
KC = K // P
HALF = HW // 2
TT = HALF // P
TILES = TT * G
PARTS = 3
LOADS = G + 2
ONEHOT = ("pool", "pool", "act", "act")
DVE_SLOTS = (4, 6, 9, 11)
LOWEST = -3.0e38


def prime(nc, semaphores):
    with nc.Block() as block:
        @block.sync
        def _(sp):
            for s in semaphores:
                sp.sem_inc(s, START)


def block_l0(nc, ps, X, io, const):
    ident, ident16, iota, eps = const["ident"], const["ident16"], const["iota"], const["eps"]
    minus_iota, one = const["minus_iota"], const["one"]
    with ExitStack() as ctx:
        def t(name, shape, dt=F32):
            return ctx.enter_context(nc.sbuf_tensor("l0_" + name, shape, dt))

        semaphores = []

        def sem(name):
            semaphores.append(ctx.enter_context(nc.semaphore("l0_" + name)))
            return semaphores[-1]

        xn = t("xn", [P, J * HW])
        picked = t("picked", [P, HALF])
        res = t("res", [P, HW])
        stats = t("stats", [P, J, 2, 6])
        mv = t("mv", [P, J, 2])
        std = t("std", [P, J])
        rstd = t("rstd", [P, J])
        ct_blk = t("ct_blk", [P, 2, G, K])
        csq = t("csq", [P, NC, K])
        csq_slot = t("csq_slot", [P, 2, K])
        cb = t("cb", [P, NC, KC, C])
        cb_left = t("cb_left", [P, NC, KC, C])
        cbp = t("cbp", [P, NC, PARTS, KC, C], BF16)
        cbp_slot = t("cbp_slot", [P, 2, PARTS, KC, C], BF16)
        scored = t("scored", [P, 4, K])
        top = t("top", [P, 2, TILES])
        idx8 = t("idx8", [P, 2, TILES, 8], U32)
        idx16 = t("idx16", [P, 2, TILES], F16)
        ib16 = t("ib16", [P, G, HALF], F16)
        away = t("away", [P, 2, HALF], F16)
        onehot = t("onehot", [P, G, KC, HALF], BF16)
        ctsq = t("ctsq", [C, NC, K])

        s_in = sem("in")
        s_zero = sem("zero")
        s_sq = sem("sq")
        s_csqp = sem("csqp")
        s_csq = sem("csq")
        s_cbp = sem("cbp")
        s_slot = [sem("slot_even"), sem("slot_odd")]
        s_gn = sem("gn")
        s_std = sem("std")
        s_xn = sem("xn")
        s_res = sem("res")
        s_score = sem("score")
        s_dve = sem("dve")
        s_idx = sem("idx")
        s_ibp = sem("ibp")
        s_ib = sem("ib")
        s_away = sem("away")
        s_oh = {e: sem("oh_" + e) for e in sorted(set(ONEHOT))}
        s_pick = sem("pick")
        s_sum = sem("sum")
        s_out = sem("out")
        s_alone = sem("alone")

        PER_HALF = 2 * TILES
        SHARE = {e: [c for c in range(KC) if ONEHOT[c] == e] for e in sorted(set(ONEHOT))}

        def max_count(n):
            return max(1, 2 * n)

        prime(nc, semaphores)
        block = ctx.enter_context(nc.Block())

        def halves(eng, body):
            def stage(j, s, par, use, which=(0, 1)):
                for h in which:
                    body(h, par, j * NC + s, j * (NC // 2) + use, s if isinstance(s, int) else None, j)

            def quarter(j):
                stage(j, 0, 0, 0, (1,))
                with eng.Fori(0, (NC - 2) // 2) as pair:
                    stage(j, pair * 2 + 1, 1, pair)
                    stage(j, pair * 2 + 2, 0, pair + 1)
                stage(j, NC - 1, 1, NC // 2 - 1)

            stage(0, 0, 0, 0, (0,))
            with eng.Fori(0, J - 1) as j:
                quarter(j)
                stage(j + 1, 0, 0, 0, (0,))
            quarter(J - 1)

        @block.sync
        def _(sp):
            sp.dma_start(cb[:], io["codes"]).then_inc(s_in, 16)
            sp.dma_start(ctsq[:], io["codes_t"].rearrange("s c k -> c s k")).then_inc(s_in, 16)

            def load(s, par):
                for g in range(G):
                    src = io["codes_t"][bass.ds(s, 1)].rearrange("s c k -> (s c) k")
                    sp.dma_start(ct_blk[C * g:C * g + C, par, g, :], src).then_inc(s_slot[par], 16)
                sp.dma_start(csq_slot[:, par, :],
                             csq[:, bass.ds(s, 1), :].rearrange("p s k -> p (s k)")).then_inc(s_slot[par], 16)
                sp.dma_start(cbp_slot[:, par].rearrange("p a k c -> p (a k c)"),
                             cbp[:, bass.ds(s, 1)].rearrange("p s a k c -> p (s a k c)")).then_inc(s_slot[par], 16)

            sp.wait_ge(s_zero, START + 2)
            sp.wait_ge(s_csq, START + NC)
            sp.wait_ge(s_cbp, START + 6)
            load(0, 0)

            def quarter(j, last):
                sp.wait_ge(s_pick, START + j * (2 * G * NC) + 1)
                load(1, 1)
                with sp.Fori(0, (NC - 2) // 2) as pair:
                    for u in range(2):
                        s = pair * 2 + (1 + u)
                        sp.wait_ge(s_pick, START + (j * NC + s) * (2 * G) + 1)
                        load(s + 1, u)
                if not last:
                    sp.wait_ge(s_pick, START + (j * NC + (NC - 1)) * (2 * G) + 1)
                    load(0, 0)

            with sp.Fori(0, J - 1) as j:
                quarter(j, False)
            quarter(J - 1, True)
            for par in range(2):
                sp.wait_ge(s_slot[par], START + 16 * LOADS * (J * NC // 2))

        @block.tensor
        def _(pe):
            pe.wait_ge(s_sq, START + 1)
            for s in range(NC):
                pe.matmul(ps[:, s, :], const["neg_half"][0:C, :], ctsq[:, s, :],
                          start=True, stop=True).then_inc(s_csqp, 1)
            pe.wait_ge(s_csq, START + NC)
            pe.wait_ge(s_xn, START + J)

            def scores(h, par, hs, tt):
                for g in range(G):
                    n = G * tt + g
                    if n >= G:
                        pe.wait_ge(s_dve, START + hs * PER_HALF + (PER_HALF + max_count(n - G)))
                    else:
                        pe.wait_ge(s_dve, START + hs * PER_HALF + max_count(TILES - G + g))
                    at = HALF * h + P * tt
                    pe.matmul(ps[:, g, :], res[:, at:at + P], ct_blk[:, par, g, :],
                              start=True, stop=True).then_inc(s_score, 1)

            def spread(h, hs, g):
                if g == 0:
                    pe.wait_ge(s_idx, START + hs + 1)
                if g >= 2:
                    pe.wait_ge(s_ib, START + hs * G + (g - 1))
                for tt in range(TT):
                    mm = pe.matmul(ps[:, 4 + g % 2, P * tt:P * tt + P],
                                   idx16[:, h, G * tt + g:G * tt + g + 1].to_broadcast([P, P]), ident16[:],
                                   start=True, stop=True)
                mm.then_inc(s_ibp, 1)

            def pick(h, par, hs, g):
                for e in SHARE:
                    pe.wait_ge(s_oh[e], START + (hs * G + (g + 1)) * len(SHARE[e]))
                for a in range(PARTS):
                    for c in range(KC):
                        mm = pe.matmul(ps[C * g:C * g + C, 6 + h, :], cbp_slot[:, par, a, c, :],
                                       onehot[:, g, c, :], start=False, stop=True, skip_group_check=True)
                mm.then_inc(s_pick, 1)

            def half(h, par, st, use, s, j):
                hs = st * 2 + h
                if h == 0:
                    pe.wait_ge(s_slot[par], START + use * (16 * LOADS) + 16 * LOADS)
                pe.wait_ge(s_res, START + hs + 1)
                if isinstance(hs, int) and hs == 0:
                    for tt in range(TT):
                        scores(h, par, hs, tt)
                    return
                last, lh, lpar = hs - 1, 1 - h, par if h else 1 - par
                scores(h, par, hs, 0)
                spread(lh, last, 0)
                spread(lh, last, 1)
                scores(h, par, hs, 1)
                spread(lh, last, 2)
                spread(lh, last, 3)
                scores(h, par, hs, 2)
                if s == 0 and h == 1:
                    pe.wait_ge(s_sum, START + j * 2 + 2)
                    for i in range(2):
                        pe.matmul(ps[:, 6 + i, :], ident[:], xn[:, bass.ds(j * HW + i * HALF, HALF)],
                                  start=True, stop=True, skip_group_check=True)
                pick(lh, lpar, last, 0)
                pick(lh, lpar, last, 1)
                scores(h, par, hs, 3)
                pick(lh, lpar, last, 2)
                pick(lh, lpar, last, 3)

            halves(pe, half)
            last = 2 * J * NC - 1
            for g in range(G):
                spread(1, last, g)
            for g in range(G):
                pick(1, 1, last, g)

        @block.scalar
        def _(act):
            act.wait_ge(s_in, START + 32)
            nc.scalar.activation(ctsq[:], ctsq[:], ACT.Square).then_inc(s_sq, 1)
            for s in range(NC):
                act.wait_ge(s_csqp, START + s + 1)
                nc.scalar.copy(csq[:, s, :], ps[:, s, :]).then_inc(s_csq, 1)

            def onehot_act(hs, g):
                mine = SHARE["act"]
                for i, c in enumerate(mine):
                    n = hs * (G * len(mine)) + (g * len(mine) + i)
                    act.wait_ge(s_ib, START + hs * G + (g + 1))
                    nc.scalar.activation(away[:, (g * len(mine) + i) % 2, :], ib16[:, g, :], ACT.Abs,
                                         bias=minus_iota[:, c:c + 1]).then_inc(s_away, 1)
                    act.wait_ge(s_away, START + n + 1)
                    nc.scalar.activation(onehot[:, g, c, :], away[:, (g * len(mine) + i) % 2, :], ACT.Relu,
                                         bias=one[:], scale=-1.0).then_inc(s_oh["act"], 1)

            def first_residual(h, j):
                nc.scalar.copy(res[:, HALF * h:HALF * (h + 1)],
                               xn[:, bass.ds(j * HW + h * HALF, HALF)]).then_inc(s_res, 1)

            def half(h, par, st, use, s, j):
                hs = st * 2 + h
                act.wait_ge(s_dve, START + hs * PER_HALF + 2 * PER_HALF)
                if s == NC - 1 and not isinstance(j, int):
                    first_residual(h, j + 1)
                nc.scalar.copy(idx16[:, h, :], idx8[:, h, :, 0]).then_inc(s_idx, 1)
                for g in range(G):
                    act.wait_ge(s_ibp, START + hs * G + (g + 1))
                    nc.scalar.copy(ib16[:, g, :], ps[:, 4 + g % 2, :]).then_inc(s_ib, 1)
                    if g >= 1:
                        onehot_act(hs, g - 1)
                onehot_act(hs, G - 1)
                if s != NC - 1:
                    act.wait_ge(s_pick, START + hs * G + (G + 1))
                    nc.scalar.copy(res[:, HALF * h:HALF * (h + 1)], ps[:, 6 + h, :]).then_inc(s_res, 1)

            act.wait_ge(s_gn, START + 3 * J)
            nc.scalar.activation(std[:], mv[:, :, 1], ACT.Sqrt, bias=eps[:]).then_inc(s_std, 1)
            act.wait_ge(s_xn, START + J)
            for h in range(2):
                first_residual(h, 0)
            halves(act, half)

        @block.gpsimd
        def _(pool):
            nc.gpsimd.memset(ct_blk[:, 0], 0.0).then_inc(s_zero, 1)
            nc.gpsimd.memset(ct_blk[:, 1], 0.0).then_inc(s_zero, 1)

            def half(h, par, st, use, s, j):
                hs = st * 2 + h
                for g in range(G):
                    pool.wait_ge(s_ib, START + hs * G + (g + 1))
                    pool.sem_inc(s_alone, 1)
                    for c in SHARE["pool"]:
                        nc.gpsimd.tensor_scalar(onehot[:, g, c, :], ib16[:, g, :], iota[:, c:c + 1], None,
                                                ALU.is_equal).then_inc(s_oh["pool"], 1)

            halves(pool, half)

        @block.vector
        def _(dve):
            dve.sem_inc(s_dve, PER_HALF)
            dve.sem_inc(s_pick, 1)
            dve.wait_ge(s_in, START + 32)
            nc.vector.tensor_scalar(cbp[:, :, 0], cb[:], -1.0, None, ALU.mult).then_inc(s_cbp, 1)
            dve.wait_ge(s_cbp, START + 1)
            nc.vector.scalar_tensor_tensor(out=cb_left[:], in0=cb[:], scalar=-1.0, in1=cbp[:, :, 0],
                                           op0=ALU.mult, op1=ALU.subtract).then_inc(s_cbp, 1)
            dve.wait_ge(s_cbp, START + 2)
            nc.vector.tensor_copy(cbp[:, :, 1], cb_left[:]).then_inc(s_cbp, 1)
            dve.wait_ge(s_cbp, START + 3)
            nc.vector.tensor_tensor(cb[:], cb_left[:], cbp[:, :, 1], ALU.subtract).then_inc(s_cbp, 1)
            dve.wait_ge(s_cbp, START + 4)
            nc.vector.tensor_copy(cbp[:, :, 2], cb[:]).then_inc(s_cbp, 2)

            def maximum(h, par, n):
                nc.vector.tensor_tensor_reduce(
                    out=scored[:, n % 4, :], in0=ps[:, n % G, :], in1=csq_slot[:, par, :], scale=1.0,
                    scalar=LOWEST, op0=ALU.add, op1=ALU.max, accum_out=top[:, h, n:n + 1]).then_inc(s_dve, 1)

            def index(h, n):
                nc.vector.max_index(idx8[:, h, n, :], top[:, h, n:n + 1].to_broadcast([P, 8]),
                                    scored[:, n % 4, :]).then_inc(s_dve, 1)

            def onehot_dve(hs, g):
                dve.wait_ge(s_ib, START + hs * G + (g + 1))
                for c in SHARE["dve"]:
                    nc.vector.tensor_scalar(onehot[:, g, c, :], ib16[:, g, :], iota[:, c:c + 1], None,
                                            ALU.is_equal).then_inc(s_oh["dve"], 1)

            def finish(h, last, j):
                at = bass.ds(j * HW + h * HALF, HALF)
                dve.wait_ge(s_pick, START + last * G + (G + 1))
                dve.wait_ge(s_out, START + j * 2 + (h + 1))
                nc.vector.tensor_tensor(picked[:], xn[:, at], ps[:, 6 + h, :], ALU.subtract).then_inc(s_sum, 1)
                dve.wait_ge(s_sum, START + j * 2 + (h + 3))
                nc.vector.tensor_tensor(X[:, at], X[:, at], picked[:], ALU.add).then_inc(s_out, 1)

            def half(h, par, st, use, s, j):
                hs = st * 2 + h
                if h == 0:
                    dve.wait_ge(s_slot[par], START + use * (16 * LOADS) + 16 * LOADS)
                dve.wait_ge(s_score, START + hs * TILES + 1)
                dve.wait_ge(s_dve, START + hs * PER_HALF + (2 * (TILES - 4) + 3))
                dve.sem_inc(s_alone, 1)
                maximum(h, par, 0)
                for n in range(TILES - 1):
                    dve.wait_ge(s_score, START + hs * TILES + (n + 2))
                    dve.wait_ge(s_dve, START + hs * PER_HALF + (PER_HALF + max_count(n)))
                    dve.sem_inc(s_alone, 1)
                    maximum(h, par, n + 1)
                    index(h, n)
                    if n in DVE_SLOTS and "dve" in SHARE and not (isinstance(hs, int) and hs == 0):
                        onehot_dve(hs - 1, DVE_SLOTS.index(n))
                dve.wait_ge(s_dve, START + hs * PER_HALF + (PER_HALF + max_count(TILES - 1)))
                dve.sem_inc(s_alone, 1)
                index(h, TILES - 1)
                if s == NC - 1 and h == 1:
                    finish(0, hs - 1, j)
                if s == 0 and h == 0 and not (isinstance(hs, int) and hs == 0):
                    finish(1, hs - 1, j - 1)

            dve.sem_inc(s_sum, 2)
            dve.sem_inc(s_out, 1)
            for j in range(J):
                for h in range(2):
                    at = j * HW + h * HALF
                    nc.vector.bn_stats(stats[:, j, h, :], X[:, at:at + HALF]).then_inc(s_gn, 1)
            dve.wait_ge(s_gn, START + 2 * J)
            for j in range(J):
                nc.vector.bn_aggr(mv[:, j, :], stats[:, j]).then_inc(s_gn, 1)
            dve.wait_ge(s_std, START + 1)
            nc.vector.reciprocal(rstd[:], std[:]).then_inc(s_gn, 1)
            dve.wait_ge(s_gn, START + 3 * J + 1)
            for j in range(J):
                at = slice(j * HW, (j + 1) * HW)
                nc.vector.tensor_scalar(xn[:, at], X[:, at], mv[:, j, 0:1], rstd[:, j:j + 1], ALU.subtract,
                                        ALU.mult).then_inc(s_xn, 1)
            dve.wait_ge(s_xn, START + J)
            halves(dve, half)
            if "dve" in SHARE:
                for g in range(G):
                    onehot_dve(2 * J * NC - 1, g)
            finish(1, 2 * J * NC - 1, J - 1)
            dve.wait_ge(s_out, START + 2 * J + 1)


PATCH = 8
PAIRS = H // PATCH
TOKT = HW // P
HID = 6 * C
QC = 2 * C
PADW = W + 2
PADHW = PADW * (H + 2)
TAPROWS = 3 * C + 4
PIX = PATCH * PATCH
PRODS = 4 + 4 * (PIX - 4) // 2
LN_EPS = 1e-5


def block_l1(nc, ps, X, io, const):
    ident, eps = const["ident"], const["eps"]
    with ExitStack() as ctx:
        def t(name, shape, dt=F32):
            return ctx.enter_context(nc.sbuf_tensor("l1_" + name, shape, dt))

        semaphores = []

        def sem(name):
            semaphores.append(ctx.enter_context(nc.semaphore("l1_" + name)))
            return semaphores[-1]

        stats = t("stats", [P, J, 2, 6])
        mv = t("mv", [P, J, 2])
        std = t("std", [P, J])
        rstd = t("rstd", [P, J])
        xpad = t("xpad", [P, J, H + 2, PADW])
        xt = t("xt", [P, 3, 3, HW])
        xi = t("xi", [TAPROWS, 3, G, HW])
        wh = t("wh", [TAPROWS, HID])
        wd = t("wd", [TAPROWS, 3, HID])
        wc = t("wc", [TAPROWS, 3, HID])
        fa = t("fa", [P, 2, PRODS])
        fb = t("fb", [P, 2, PRODS])
        fc = t("fc", [PRODS, PIX])
        lnw = t("lnw", [P, QC])
        lnb = t("lnb", [P, QC])
        wp = t("wp", [P, 2, C])
        bp = t("bp", [P, 1])
        qkv = t("qkv", [P, G, TOKT, HID])
        qf = t("qf", [PRODS, 2, BANK])
        prod = t("prod", [PRODS, 2, BANK])
        msum = t("msum", [P, TOKT])
        mean = t("mean", [P, TOKT])
        cen = t("cen", [P, TOKT, QC])
        sq = t("sq", [P, TOKT, QC])
        vsum = t("vsum", [P, TOKT])
        pstd = t("pstd", [P, TOKT])
        prstd = t("prstd", [P, TOKT])
        y = [t(f"y{i}", [P, TOKT, QC]) for i in range(4)]
        yt = t("yt", [P, BANK])
        biased = t("biased", [P, 2, BANK])

        s_in = sem("in")
        s_border = sem("border")
        s_wc = sem("wc")
        s_gn = sem("gn")
        s_std = sem("std")
        s_xn = sem("xn")
        s_xta = sem("xta")
        s_xtd = sem("xtd")
        s_xi = [sem(f"xi{g}") for g in range(G)]
        s_conv = sem("conv")
        s_qkv = sem("qkv")
        s_dft = sem("dft")
        s_qf = sem("qf")
        s_prod = sem("prod")
        s_inv = sem("inv")
        s_ln = sem("ln")
        s_sq = sem("sq")
        s_pstd = sem("pstd")
        s_pool = sem("pool")
        s_tr = sem("tr")
        s_yt = sem("yt")
        s_proj = sem("proj")
        s_biased = sem("biased")
        s_out = sem("out")
        s_alone = sem("alone")
        LN_STEPS = 7
        ACT_TAPS = 9 - G

        def lay_tap(copy, n, j):
            kx, ky = divmod(n, 3)
            image = xpad[:, bass.ds(j, 1), ky:ky + H, kx:kx + W].rearrange("p j y x -> p (j y) x")
            src = image.rearrange("p (a r) (b c) -> p a b r c", r=PATCH, c=PATCH)
            return copy(xt[:, kx, ky, :].rearrange("p (a b r c) -> p a b r c", a=PAIRS, b=PAIRS, r=PATCH), src)

        prime(nc, semaphores)
        block = ctx.enter_context(nc.Block())

        @block.sync
        def _(sp):
            loads = [(wh, "l1_wh"), (wd, "l1_wd"), (fa, "l1_fa"), (fb, "l1_fb"), (fc, "l1_fc"),
                     (lnw, "l1_lnw"), (lnb, "l1_lnb"), (wp, "l1_wp"), (bp, "l1_bp")]
            for dst, name in loads:
                sp.dma_start(dst[:], io[name]).then_inc(s_in, 16)
            for g in range(G):
                sp.dma_start(xi[3 * C:TAPROWS, :, g, :], io["l1_inside"]).then_inc(s_in, 16)
            sp.wait_ge(s_in, START + 16 * (len(loads) + G))

            def gather(j, after):
                sp.wait_ge(s_xta, START + j * ACT_TAPS + ACT_TAPS)
                sp.sem_inc(s_alone, 1)
                sp.wait_ge(s_xtd, START + j * (9 - ACT_TAPS) + (9 - ACT_TAPS))
                sp.sem_inc(s_alone, 1)
                for g in range(G):
                    if after is not None:
                        sp.wait_ge(s_conv, START + after * (G * PAIRS) + PAIRS * (g + 1))
                    for kx in range(3):
                        sp.dma_start(xi[C * kx:C * kx + C, :, g, :],
                                     xt[C * g:C * g + C, kx, :, :]).then_inc(s_xi[g], 16)

            gather(0, None)
            with sp.Fori(0, J - 1) as j:
                gather(j + 1, j)
            for g in range(G):
                sp.wait_ge(s_xi[g], START + 16 * 3 * J)

        @block.tensor
        def _(pe):
            pe.wait_ge(s_wc, START + 1)
            pe.wait_ge(s_in, START + 16 * (9 + G))
            def quarter(j, last):
                def conv(g, j):
                    pe.wait_ge(s_xi[g], START + j * (16 * 3) + 16 * 3)
                    for py in range(PAIRS):
                        if g == 0 and py < 2:
                            pe.wait_ge(s_qkv, START + j * (G * PAIRS))
                        else:
                            pe.wait_ge(s_qkv, START + j * (G * PAIRS) + (g * PAIRS + py - 1))
                        for u in range(2):
                            for ky in range(3):
                                at = P * (2 * py + u)
                                mm = pe.matmul(ps[:, py % 2, HID * u:HID * (u + 1)],
                                               xi[:, ky, g, at:at + P], wc[:, ky, :],
                                               start=(ky == 0), stop=(ky == 2))
                        mm.then_inc(s_conv, 1)

                def dft(g):
                    pe.wait_ge(s_qkv, START + j * (G * PAIRS) + (g + 1) * PAIRS)
                    pe.wait_ge(s_prod, START + j * (2 * G) + 2 * g)
                    for h in range(2):
                        if h == 1:
                            pe.wait_ge(s_ln, START + j * (G * LN_STEPS) + ((g - 1) * LN_STEPS + 3 if g else 0))
                            pe.wait_ge(s_yt, START + j * G + max(0, g - 1))
                        for m, at in ((fa, 0), (fb, QC)):
                            pe.matmul(ps[0:PRODS, 2 + 2 * h + (at > 0), :], m[:, h, :],
                                      qkv[:, g, :, at:at + QC], start=True, stop=True).then_inc(s_dft, 1)

                def inverse(g):
                    for h in range(2):
                        pe.wait_ge(s_prod, START + j * (2 * G) + (2 * g + h + 1))
                        mm = pe.matmul(ps[PIX * h:PIX * (h + 1), 4, :], fc[:], prod[:, h, :],
                                       start=True, stop=True)
                    mm.then_inc(s_inv, 1)

                def project(g):
                    pe.wait_ge(s_pool, START + j * (3 * G) + (3 * G) + (3 * g + 3))
                    pe.wait_ge(s_prod, START + j * (2 * G) + 2 * min(g + 2, G))
                    for py in range(PAIRS):
                        mm = pe.transpose(ps[:, 5, P * py:P * (py + 1)],
                                          y[3][:, 2 * py:2 * py + 2, :].rearrange("p t c -> p (t c)"), ident[:])
                    mm.then_inc(s_tr, 1)
                    pe.wait_ge(s_yt, START + j * G + (g + 1))
                    if g == 0:
                        pe.wait_ge(s_biased, START + j * 2)
                    for u in range(2):
                        mm = pe.matmul(ps[C * g:C * g + C, 6 + u, :], wp[:, u, :], yt[:],
                                       start=True, stop=True)
                    mm.then_inc(s_proj, 1)

                if isinstance(j, int) and j < 0:
                    conv(0, 0)
                    return
                for g in range(G):
                    dft(g)
                    if g + 1 < G:
                        conv(g + 1, j)
                    if g:
                        project(g - 1)
                    inverse(g)
                if not last:
                    conv(0, j + 1)
                project(G - 1)

            quarter(-1, False)
            with pe.Fori(0, J - 1) as j:
                quarter(j, False)
            quarter(J - 1, True)

        @block.scalar
        def _(act):
            act.wait_ge(s_gn, START + 3 * J)
            nc.scalar.activation(std[:], mv[:, :, 1], ACT.Sqrt, bias=eps[:]).then_inc(s_std, 1)
            act.wait_ge(s_xn, START + 1)
            for n in range(ACT_TAPS):
                lay_tap(nc.scalar.copy, n, 0).then_inc(s_xta, 1)
            act.wait_ge(s_xn, START + J)

            def quarter(j, last):
                def next_taps(which):
                    if last:
                        return
                    for g in range(G):
                        act.wait_ge(s_xi[g], START + j * (16 * 3) + 16 * 3)
                    for n in which:
                        lay_tap(nc.scalar.copy, n, j + 1).then_inc(s_xta, 1)

                def copy_qkv(g, j):
                    for py in range(PAIRS):
                        act.wait_ge(s_conv, START + j * (G * PAIRS) + (g * PAIRS + py + 1))
                        act.wait_ge(s_pool, START + j * (3 * G) + 3 * (g + 1))
                        nc.scalar.copy(qkv[:, g, 2 * py:2 * py + 2, :].rearrange("p t c -> p (t c)"),
                                       ps[:, py % 2, 0:2 * HID]).then_inc(s_qkv, 1)

                def copy_yt(g):
                    act.wait_ge(s_tr, START + j * G + (g + 1))
                    act.wait_ge(s_proj, START + j * G + g)
                    nc.scalar.copy(yt[:], ps[:, 5, :]).then_inc(s_yt, 1)

                if isinstance(j, int) and j < 0:
                    copy_qkv(0, 0)
                    return
                for g in range(G):
                    for h in range(2):
                        act.wait_ge(s_dft, START + j * (4 * G) + (4 * g + 2 * h + 1))
                        act.wait_ge(s_prod, START + j * (2 * G) + (max(0, 2 * g - 1 + h) if g else 0))
                        nc.scalar.copy(qf[:, h, :], ps[0:PRODS, 2 + 2 * h, :]).then_inc(s_qf, 1)
                    if g + 1 < G:
                        copy_qkv(g + 1, j)
                    if g:
                        copy_yt(g - 1)
                    next_taps(range(3 * g, min(3 * g + 3, ACT_TAPS)))
                    act.wait_ge(s_ln, START + j * (G * LN_STEPS) + (g * LN_STEPS + 4))
                    nc.scalar.activation(pstd[:], vsum[:], ACT.Sqrt, bias=eps[:],
                                         scale=1.0 / QC).then_inc(s_pstd, 1)
                if not last:
                    copy_qkv(0, j + 1)
                copy_yt(G - 1)
                act.wait_ge(s_proj, START + j * G + G)
                act.wait_ge(s_out, START + j * PAIRS)
                for u in range(2):
                    nc.scalar.activation(biased[:, u, :], ps[:, 6 + u, :], ACT.Identity,
                                         bias=bp[:]).then_inc(s_biased, 1)

            quarter(-1, False)
            with act.Fori(0, J - 1) as j:
                quarter(j, False)
            quarter(J - 1, True)

        @block.gpsimd
        def _(pool):
            nc.gpsimd.memset(xpad[:], 0.0).then_inc(s_border, 1)
            pool.sem_inc(s_pool, 3 * G)
            pool.wait_ge(s_in, START + 16 * (9 + G))
            with pool.Fori(0, J) as j:
                for g in range(G):
                    v = qkv[:, g, :, 2 * QC:3 * QC]
                    pool.wait_ge(s_ln, START + j * (G * LN_STEPS) + (g * LN_STEPS + 3))
                    nc.gpsimd.tensor_tensor(sq[:], cen[:], cen[:], ALU.mult).then_inc(s_pool, 1)
                    pool.wait_ge(s_ln, START + j * (G * LN_STEPS) + (g * LN_STEPS + 6))
                    nc.gpsimd.tensor_tensor(y[1][:], y[0][:], lnw[:, None, :].to_broadcast([P, TOKT, QC]),
                                            ALU.mult).then_inc(s_pool, 1)
                    pool.wait_ge(s_ln, START + j * (G * LN_STEPS) + (g * LN_STEPS + 7))
                    pool.wait_ge(s_tr, START + j * G + g)
                    nc.gpsimd.tensor_tensor(y[3][:], y[2][:], v, ALU.mult).then_inc(s_pool, 1)

        @block.vector
        def _(dve):
            for j in range(J):
                for h in range(2):
                    at = j * HW + h * HALF
                    nc.vector.bn_stats(stats[:, j, h, :], X[:, at:at + HALF]).then_inc(s_gn, 1)
            dve.wait_ge(s_gn, START + 2 * J)
            for j in range(J):
                nc.vector.bn_aggr(mv[:, j, :], stats[:, j]).then_inc(s_gn, 1)
            dve.wait_ge(s_std, START + 1)
            nc.vector.reciprocal(rstd[:], std[:]).then_inc(s_gn, 1)
            dve.wait_ge(s_gn, START + 3 * J + 1)
            dve.wait_ge(s_border, START + 1)
            for j in range(J):
                nc.vector.tensor_scalar(xpad[:, j, 1:H + 1, 1:W + 1],
                                        X[:, j * HW:(j + 1) * HW].rearrange("p (y x) -> p y x", x=W),
                                        mv[:, j, 0:1], rstd[:, j:j + 1], ALU.subtract, ALU.mult).then_inc(s_xn, 1)
                if j == 0:
                    dve.wait_ge(s_xn, START + 1)
                    for n in range(ACT_TAPS, 9):
                        lay_tap(nc.vector.tensor_copy, n, 0).then_inc(s_xtd, 1)
            dve.wait_ge(s_in, START + 16 * (9 + G))
            nc.vector.tensor_tensor(wc[:], wd[:], wh[:, None, :].to_broadcast([TAPROWS, 3, HID]),
                                    ALU.mult).then_inc(s_wc, 1)
            dve.wait_ge(s_xn, START + J)

            def quarter(j, last):
                for g in range(G):
                    for h in range(2):
                        dve.wait_ge(s_dft, START + j * (4 * G) + (4 * g + 2 * h + 2))
                        dve.wait_ge(s_qf, START + j * (2 * G) + (2 * g + h + 1))
                        nc.vector.tensor_tensor(prod[:, h, :], qf[:, h, :], ps[0:PRODS, 3 + 2 * h, :],
                                                ALU.mult).then_inc(s_prod, 1)
                    base = g * LN_STEPS
                    patches = ps[:, 4, :].rearrange("p (t c) -> p t c", c=QC)
                    dve.wait_ge(s_inv, START + j * G + (g + 1))
                    nc.vector.tensor_reduce(msum[:], patches, AX_X, ALU.add).then_inc(s_ln, 1)
                    dve.wait_ge(s_ln, START + j * (G * LN_STEPS) + (base + 1))
                    nc.vector.tensor_scalar(mean[:], msum[:], 1.0 / QC, None, ALU.mult).then_inc(s_ln, 1)
                    dve.wait_ge(s_ln, START + j * (G * LN_STEPS) + (base + 2))
                    nc.vector.tensor_tensor(cen[:], patches, mean[:, :, None].to_broadcast([P, TOKT, QC]),
                                            ALU.subtract).then_inc(s_ln, 1)
                    dve.wait_ge(s_pool, START + j * (3 * G) + (3 * G) + (3 * g + 1))
                    nc.vector.tensor_reduce(vsum[:], sq[:], AX_X, ALU.add).then_inc(s_ln, 1)
                    if not last and g < 2:
                        for i in range(G):
                            dve.wait_ge(s_xi[i], START + j * (16 * 3) + 16 * 3)
                        for n in range(ACT_TAPS + 2 * g, ACT_TAPS + 2 * g + 2):
                            lay_tap(nc.vector.tensor_copy, n, j + 1).then_inc(s_xtd, 1)
                    dve.wait_ge(s_pstd, START + j * G + (g + 1))
                    nc.vector.reciprocal(prstd[:], pstd[:]).then_inc(s_ln, 1)
                    dve.wait_ge(s_ln, START + j * (G * LN_STEPS) + (base + 5))
                    nc.vector.tensor_tensor(y[0][:], cen[:], prstd[:, :, None].to_broadcast([P, TOKT, QC]),
                                            ALU.mult).then_inc(s_ln, 1)
                    dve.wait_ge(s_pool, START + j * (3 * G) + (3 * G) + (3 * g + 2))
                    nc.vector.tensor_tensor(y[2][:], y[1][:], lnb[:, None, :].to_broadcast([P, TOKT, QC]),
                                            ALU.add).then_inc(s_ln, 1)
                xj = X[:, bass.ds(j * HW, HW)].rearrange("p (a r b c) -> p b a r c", r=PATCH, b=PAIRS, c=PATCH)
                for u in range(2):
                    dve.wait_ge(s_biased, START + j * 2 + (u + 1))
                    src = biased[:, u, :].rearrange("p (a x r c) -> p x a r c", x=2, r=PATCH, c=PATCH)
                    for x in range(2):
                        nc.vector.tensor_tensor(xj[:, 2 * u + x], xj[:, 2 * u + x], src[:, x],
                                                ALU.add).then_inc(s_out, 1)

            with dve.Fori(0, J - 1) as j:
                quarter(j, False)
            quarter(J - 1, True)
            dve.wait_ge(s_out, START + PAIRS * J)


TAPS = 9
MARGIN = TAPS // 2
PITCH = W + 2 * MARGIN
STEPS = H - 1
DIRS = 4


def block_l2(nc, ps, X, io, const):
    ident, eps = const["ident"], const["eps"]
    with ExitStack() as ctx:
        def t(name, shape, dt=F32):
            return ctx.enter_context(nc.sbuf_tensor("l2_" + name, shape, dt))

        semaphores = []

        def sem(name):
            semaphores.append(ctx.enter_context(nc.semaphore("l2_" + name)))
            return semaphores[-1]

        stats = t("stats", [P, J, 2, 6])
        mv = t("mv", [P, J, 2])
        std = t("std", [P, J])
        rstd = t("rstd", [P, J])
        seq = t("seq", [P, J, PITCH * PITCH])
        wt = t("wt", [P, DIRS, TAPS, P])
        bias = t("bias", [P, DIRS])

        s_in = sem("in")
        s_border = sem("border")
        s_gn = sem("gn")
        s_std = sem("std")
        s_xn = sem("xn")
        s_z = sem("z")
        s_line = sem("line")
        s_out = sem("out")
        s_alone = sem("alone")

        image = seq[:].rearrange("p j (y x) -> p j y x", x=PITCH)

        def line(d, n, shift=MARGIN):
            if d < 2:
                return seq[:, :, bass.ds(n * PITCH + (MARGIN * PITCH + shift), W)]
            return image[:, :, shift:shift + H, bass.ds(n + MARGIN, 1)].rearrange("p j y x -> p j (y x)")

        def scan(eng, step):
            for d in range(DIRS):
                step(d, 0, STEPS * d % 2, STEPS * d)
                with eng.Fori(0, STEPS // 2) as pair:
                    for u in range(2):
                        step(d, pair * 2 + (1 + u), (STEPS * d + 1 + u) % 2, pair * 2 + (1 + u + STEPS * d))

        def current(d, i):
            return i + 1 if d % 2 == 0 else i * -1 + (STEPS - 1)

        def previous(d, i):
            return i + 0 if d % 2 == 0 else i * -1 + STEPS

        prime(nc, semaphores)
        block = ctx.enter_context(nc.Block())

        @block.sync
        def _(sp):
            sp.dma_start(wt[:], io["l2_w"]).then_inc(s_in, 16)
            sp.dma_start(bias[:], io["l2_b"]).then_inc(s_in, 16)
            sp.wait_ge(s_in, START + 32)

        @block.gpsimd
        def _(pool):
            nc.gpsimd.memset(seq[:], 0.0).then_inc(s_border, 1)

        @block.tensor
        def _(pe):
            pe.wait_ge(s_in, START + 32)
            pe.wait_ge(s_xn, START + J)

            def step(d, i, parity, n):
                z = ps[:, parity, 0:J * W].rearrange("p (j w) -> p j w", j=J)
                if isinstance(i, int):
                    pe.wait_ge(s_line, START + n + 1)
                pe.matmul(z, ident[:], line(d, current(d, i)), start=True, stop=False)
                pe.wait_ge(s_line, START + n + 1)
                for k in range(TAPS):
                    mm = pe.matmul(z, wt[:, d, k, :], line(d, previous(d, i), k), start=False,
                                   stop=(k == TAPS - 1))
                mm.then_inc(s_z, 1)

            scan(pe, step)

        @block.scalar
        def _(act):
            act.wait_ge(s_gn, START + 3 * J)
            nc.scalar.activation(std[:], mv[:, :, 1], ACT.Sqrt, bias=eps[:]).then_inc(s_std, 1)

        @block.vector
        def _(dve):
            dve.sem_inc(s_line, 1)
            for j in range(J):
                for h in range(2):
                    at = j * HW + h * HALF
                    nc.vector.bn_stats(stats[:, j, h, :], X[:, at:at + HALF]).then_inc(s_gn, 1)
            dve.wait_ge(s_gn, START + 2 * J)
            for j in range(J):
                nc.vector.bn_aggr(mv[:, j, :], stats[:, j]).then_inc(s_gn, 1)
            dve.wait_ge(s_std, START + 1)
            nc.vector.reciprocal(rstd[:], std[:]).then_inc(s_gn, 1)
            dve.wait_ge(s_gn, START + 3 * J + 1)
            dve.wait_ge(s_border, START + 1)
            for j in range(J):
                nc.vector.tensor_scalar(image[:, j, MARGIN:MARGIN + H, MARGIN:MARGIN + W],
                                        X[:, j * HW:(j + 1) * HW].rearrange("p (y x) -> p y x", x=W),
                                        mv[:, j, 0:1], rstd[:, j:j + 1], ALU.subtract,
                                        ALU.mult).then_inc(s_xn, 1)
            dve.wait_ge(s_xn, START + J)

            def step(d, i, parity, n):
                dve.wait_ge(s_z, START + n + 1)
                z = ps[:, parity, 0:J * W].rearrange("p (j w) -> p j w", j=J)
                row = line(d, current(d, i))
                nc.vector.scalar_tensor_tensor(out=row, in0=z, scalar=bias[:, d:d + 1], in1=row,
                                               op0=ALU.add, op1=ALU.max).then_inc(s_line, 1)

            scan(dve, step)
            dve.wait_ge(s_line, START + DIRS * STEPS + 1)
            for j in range(J):
                xj = X[:, j * HW:(j + 1) * HW].rearrange("p (y x) -> p y x", x=W)
                nc.vector.tensor_tensor(xj, xj, image[:, j, MARGIN:MARGIN + H, MARGIN:MARGIN + W],
                                        ALU.add).then_inc(s_out, 1)
            dve.wait_ge(s_out, START + J)


SNAKE = 9
MID = SNAKE // 2
EPITCH = W + 2 * MID
OFFC = SNAKE + 1
POINTS = [k for d in range(1, MID + 1) for k in (MID - d, MID + d)]
ITEMS = [(k, m) for k in POINTS for m in range(abs(k - MID))]
AHEAD = (0,)
RING = 6
AVERAGES_OFF = ((0, 5), (0, 7))
OWN_FIRST = 1
AVERAGES = (1, 2)
ACT_SLOTS = (1, 5, 7)
DVE_PARTS = (1, 4, 6)
ADD_SLOT = 9


def l3_schedule():
    operands, used = [], {}
    n = 0
    while n < len(ITEMS):
        k, m = ITEMS[n]
        both = n + 1 < len(ITEMS) and ITEMS[n + 1][0] == k
        operands.append((k, n, n + 1 if both else None))
        used[n] = len(operands)
        if both:
            used[n + 1] = len(operands)
        n += 2 if both else 1
    return operands, used


def block_l3(nc, ps, X, io, const):
    eps = const["eps"]
    operands, used = l3_schedule()
    quads = [(n, n2) for _, n, n2 in operands if n2 is not None]
    with ExitStack() as ctx:
        def t(name, shape, dt=F32):
            return ctx.enter_context(nc.sbuf_tensor("l3_" + name, shape, dt))

        semaphores = []

        def sem(name):
            semaphores.append(ctx.enter_context(nc.semaphore("l3_" + name)))
            return semaphores[-1]

        xstats = t("xstats", [P, J, 2, 6])
        xmv = t("xmv", [P, J, 2])
        std = t("std", [P, J])
        rstd = t("rstd", [P, J])
        xe = t("xe", [P, J, EPITCH, EPITCH])
        down = t("down", [P, J, EPITCH - 1, EPITCH])
        w_off = t("w_off", [P, 9, P])
        w_dsc = t("w_dsc", [P, SNAKE, P])
        sums = t("sums", [P, len(POINTS), P])
        cols = t("cols", [P, 6])
        avg = t("avg", [P, 2, P])
        minus = t("minus", [P, MID])
        raw = t("raw", [P, 2, HW])
        stats = t("stats", [P, 2, 2, 6])
        mv = t("mv", [P, 2, 2])
        gstat = t("gstat", [P, 2, 8])
        off = t("off", [P, J * HW])
        ramp = t("ramp", [P, 4, HW])
        y = t("y", [P, HW])
        with nc.sbuf_tensor("l3_xz", [P, J, H + 2, PADW], F32) as xz:
            pass
        term = t("term", [P, 4, HW])
        isum = t("isum", [P, RING, HW])

        s_in = sem("in")
        s_border = sem("border")
        s_gn = sem("gn")
        s_std = sem("std")
        s_xn = sem("xn")
        s_edge = sem("edge")
        s_dy = sem("dy")
        s_conv = sem("conv")
        s_raw = [sem("raw_off"), sem("raw_out")]
        s_gs = [sem("gs_off"), sem("gs_out")]
        s_gavg = [sem("gavg_off"), sem("gavg_out")]
        s_gstd = [sem("gstd_off"), sem("gstd_out")]
        s_off = sem("off")
        s_cum = sem("cum")
        s_ramp = sem("ramp")
        s_term = sem("term")
        s_sum = sem("sum")
        s_quad = sem("quad")
        s_used = sem("used")
        s_y = sem("y")
        s_out = sem("out")
        s_alone = sem("alone")
        GS = 9
        NI, NO, NQ = len(ITEMS), len(operands), len(quads)
        first = {k: next(n for n, it in enumerate(ITEMS) if it[0] == k) for k in POINTS}

        prime(nc, semaphores)
        block = ctx.enter_context(nc.Block())

        @block.sync
        def _(sp):
            for dst, name in ((w_off, "l3_w_off"), (w_dsc, "l3_w_dsc"), (sums, "l3_sums"), (cols, "l3_cols"),
                              (avg, "l3_avg"), (minus, "l3_minus")):
                sp.dma_start(dst[:], io[name]).then_inc(s_in, 16)
            sp.wait_ge(s_in, START + 16 * 6)

        @block.tensor
        def _(pe):
            pe.wait_ge(s_in, START + 16 * 6)

            def group_average(norm, j, a):
                pe.wait_ge(s_gs[norm], START + j * GS + (3 if a == 0 else 5))
                pe.matmul(ps[:, norm, a:a + 1], avg[:, norm, :],
                          mv[:, norm, 0:1] if a == 0 else gstat[:, norm, 1:2],
                          start=True, stop=True).then_inc(s_gavg[norm], 1)

            def offset_conv(j, prev):
                for h in range(2):
                    pe.wait_ge(s_raw[0], START + j * 2 + h)
                    for n in range(9):
                        ky, kx = divmod(n, 3)
                        rows = xz[:, bass.ds(j, 1), ky + H // 2 * h:ky + H // 2 * (h + 1), kx:kx + W]
                        mm = pe.matmul(ps[:, 2 + h, :].rearrange("p (y x) -> p y x", x=W), w_off[:, n, :],
                                       rows.rearrange("p j y x -> p (j y) x"),
                                       start=(n == 0), stop=(n == 8))
                        if n == 8:
                            mm.then_inc(s_conv, 1)
                        if prev is not None and (h, n) in AVERAGES_OFF:
                            group_average(0, prev, AVERAGES_OFF.index((h, n)))

            def running_sum(c, j):
                if c >= 2:
                    pe.wait_ge(s_ramp, START + j * (2 * NI) + 2 * (first[POINTS[c - 2]] + abs(POINTS[c - 2] - MID)))
                for h in range(2):
                    mm = pe.matmul(ps[:, 2 + 2 * (c % 2) + h, :], sums[:, c, :],
                                   off[:, bass.ds(j * HW + h * HALF, HALF)], start=True, stop=True)
                mm.then_inc(s_cum, 1)

            def quarter(j, prev, last):
                def own_rows(k):
                    for h in range(2):
                        rows = xe[:, bass.ds(j, 1), MID + H // 2 * h:MID + H // 2 * (h + 1), k:k + W]
                        if k == 0:
                            pe.wait_ge(s_raw[1], START + j * 2 + h)
                        pe.matmul(ps[:, 6 + h, :].rearrange("p (y x) -> p y x", x=W), w_dsc[:, k, :],
                                  rows.rearrange("p j y x -> p (j y) x"),
                                  start=(k == 0), stop=False, skip_group_check=True)
                    if k in AHEAD:
                        running_sum(3 + AHEAD.index(k), j)
                    if prev is not None and k in AVERAGES:
                        group_average(1, prev, AVERAGES.index(k))

                running_sum(2, j)
                for k in range(OWN_FIRST):
                    own_rows(k)
                done = 3 + len(AHEAD)
                for q, (k, n, n2) in enumerate(operands):
                    if not last and q >= NO - 2:
                        c = q - (NO - 2)
                        pe.wait_ge(s_ramp, START + j * (2 * NI) + 2 * (NI if c == 1 else first[POINTS[-1]]))
                        running_sum(c, j + 1)
                    c = POINTS.index(k)
                    while done < min(c + 3, len(POINTS)):
                        running_sum(done, j)
                        done += 1
                    if n2 is None:
                        pe.wait_ge(s_sum, START + j * NI + (n + 1))
                    else:
                        pe.wait_ge(s_quad, START + j * NQ + (quads.index((n, n2)) + 1))
                    for h in range(2):
                        mm = pe.matmul(ps[:, 6 + h, :], w_dsc[:, k, :],
                                       isum[:, n % RING, HALF * h:HALF * (h + 1)],
                                       start=False, stop=(q == NO - 1), skip_group_check=True)
                    mm.then_inc(s_used, 1)
                    if OWN_FIRST + q < SNAKE:
                        own_rows(OWN_FIRST + q)

            pe.wait_ge(s_xn, START + 1)
            offset_conv(0, None)
            pe.wait_ge(s_xn, START + 2 * J)
            with pe.Fori(0, J - 1) as j:
                offset_conv(j + 1, j)
            for a in range(2):
                group_average(0, J - 1, a)
            pe.wait_ge(s_off, START + J)
            pe.wait_ge(s_edge, START + 4 * J)
            running_sum(0, 0)
            running_sum(1, 0)
            quarter(0, None, False)
            with pe.Fori(0, J - 2) as prev:
                quarter(prev + 1, prev, False)
            quarter(J - 1, J - 2, True)
            for a in range(2):
                group_average(1, J - 1, a)

        @block.scalar
        def _(act):
            for norm in range(2):
                act.sem_inc(s_raw[norm], 1)
            act.wait_ge(s_gn, START + 3 * J)
            nc.scalar.activation(std[:], xmv[:, :, 1], ACT.Sqrt, bias=eps[:]).then_inc(s_std, 1)
            act.wait_ge(s_in, START + 16 * 6)

            def copy_raw(norm, j):
                for h in range(2):
                    if norm == 0:
                        act.wait_ge(s_conv, START + j * 2 + (h + 1))
                    elif h == 0:
                        act.wait_ge(s_used, START + j * NO + NO)
                    nc.scalar.activation(raw[:, norm, HALF * h:HALF * (h + 1)],
                                         ps[:, (6 if norm else 2) + h, :], ACT.Identity,
                                         bias=cols[:, 3 * norm:3 * norm + 1]).then_inc(s_raw[norm], 1)

            def group_std(norm, j):
                act.wait_ge(s_gavg[norm], START + j * 2 + 2)
                nc.scalar.activation(gstat[:, norm, 2:3], ps[:, norm, 1:2], ACT.Sqrt,
                                     bias=eps[:]).then_inc(s_gstd[norm], 1)

            def output(j):
                act.wait_ge(s_gs[1], START + j * GS + GS)
                nc.scalar.activation(y[:], raw[:, 1, :], ACT.Relu, bias=gstat[:, 1, 5:6],
                                     scale=gstat[:, 1, 4:5]).then_inc(s_y, 1)

            with act.Fori(0, J) as j:
                copy_raw(0, j)
                group_std(0, j)
                act.wait_ge(s_gs[0], START + j * GS + GS)
                nc.scalar.activation(off[:, bass.ds(j * HW, HW)], raw[:, 0, :], ACT.Tanh,
                                     bias=gstat[:, 0, 5:6], scale=gstat[:, 0, 4:5]).then_inc(s_off, 1)
                act.wait_ge(s_off, START + j + 1)
                act.sem_inc(s_alone, 1)
            def quarter(j, prev):
                for n, (k, m) in enumerate(ITEMS):
                    c = POINTS.index(k)
                    act.wait_ge(s_cum, START + j * len(POINTS) + (c + 1))
                    for e, sign in enumerate((1.0, -1.0)):
                        act.wait_ge(s_term, START + j * (2 * NI) + max(0, 2 * n + e - 3))
                        b = 2 + 2 * (c % 2)
                        nc.scalar.activation(ramp[:, (2 * n + e) % 4, :],
                                             ps[:, b:b + 2, :].rearrange("p b f -> p (b f)"), ACT.Relu,
                                             bias=minus[:, m:m + 1], scale=sign).then_inc(s_ramp, 1)
                    if prev is not None:
                        if n == ACT_SLOTS[0]:
                            copy_raw(1, prev)
                        if n == ACT_SLOTS[1]:
                            group_std(1, prev)
                        if n == ACT_SLOTS[2]:
                            output(prev)

            quarter(0, None)
            with act.Fori(0, J - 1) as prev:
                quarter(prev + 1, prev)
            copy_raw(1, J - 1)
            group_std(1, J - 1)
            output(J - 1)

        @block.gpsimd
        def _(pool):
            nc.gpsimd.memset(xz[:], 0.0).then_inc(s_border, 1)
            a, b = MID, MID + W
            with pool.Fori(0, J) as j:
                image = xe[:, bass.ds(j, 1)].rearrange("p j y x -> p (j y) x")
                edges = [(image[:, a:b, 0:a], image[:, a:b, a:a + 1].to_broadcast([P, H, MID])),
                         (image[:, a:b, b:], image[:, a:b, b - 1:b].to_broadcast([P, H, MID])),
                         (image[:, 0:a, :], image[:, a:a + 1, :].to_broadcast([P, MID, EPITCH])),
                         (image[:, b:, :], image[:, b - 1:b, :].to_broadcast([P, MID, EPITCH]))]
                pool.wait_ge(s_xn, START + j * 2 + 2)
                pool.sem_inc(s_alone, 1)
                for i, (dst, src) in enumerate(edges):
                    if i == 2:
                        pool.wait_ge(s_edge, START + j * 4 + 2)
                        pool.sem_inc(s_alone, 1)
                    nc.gpsimd.tensor_copy(dst, src).then_inc(s_edge, 1)
            with pool.Fori(0, J) as j:
                for n in range(NI):
                    pool.wait_ge(s_term, START + j * (2 * NI) + (2 * n + 2))
                    pool.wait_ge(s_used, START + j * NO + (used[n - RING] if n >= RING else 0))
                    nc.gpsimd.tensor_tensor(isum[:, n % RING, :], term[:, 2 * n % 4, :],
                                            term[:, (2 * n + 1) % 4, :], ALU.subtract).then_inc(s_sum, 1)

        @block.vector
        def _(dve):
            for j in range(J):
                for h in range(2):
                    at = j * HW + h * HALF
                    nc.vector.bn_stats(xstats[:, j, h, :], X[:, at:at + HALF]).then_inc(s_gn, 1)
            dve.wait_ge(s_gn, START + 2 * J)
            for j in range(J):
                nc.vector.bn_aggr(xmv[:, j, :], xstats[:, j]).then_inc(s_gn, 1)
            dve.wait_ge(s_std, START + 1)
            nc.vector.reciprocal(rstd[:], std[:]).then_inc(s_gn, 1)
            dve.wait_ge(s_gn, START + 3 * J + 1)
            dve.wait_ge(s_border, START + 1)
            dve.wait_ge(s_in, START + 16 * 6)
            for j in range(J):
                for dst in (xz[:, j, 1:H + 1, 1:W + 1], xe[:, j, MID:MID + H, MID:MID + W]):
                    nc.vector.tensor_scalar(dst, X[:, j * HW:(j + 1) * HW].rearrange("p (y x) -> p y x", x=W),
                                            xmv[:, j, 0:1], rstd[:, j:j + 1], ALU.subtract,
                                            ALU.mult).then_inc(s_xn, 1)

            def group_norm(norm, j, parts=(0, 1, 2)):
                def after(n):
                    dve.wait_ge(s_gs[norm], START + j * GS + n)

                g = gstat[:, norm, :]
                mean, var = ps[:, norm, 0:1], mv[:, norm, 1:2]
                if 0 in parts:
                    for h in range(2):
                        dve.wait_ge(s_raw[norm], START + j * 2 + (h + 2))
                        nc.vector.bn_stats(stats[:, norm, h, :],
                                           raw[:, norm, HALF * h:HALF * (h + 1)]).then_inc(s_gs[norm], 1)
                    after(2)
                    dve.sem_inc(s_alone, 1)
                    nc.vector.bn_aggr(mv[:, norm, :], stats[:, norm]).then_inc(s_gs[norm], 1)
                if 1 in parts:
                    dve.wait_ge(s_gavg[norm], START + j * 2 + 1)
                    nc.vector.tensor_tensor(g[:, 0:1], mv[:, norm, 0:1], mean, ALU.subtract).then_inc(s_gs[norm], 1)
                    after(4)
                    nc.vector.scalar_tensor_tensor(out=g[:, 1:2], in0=g[:, 0:1], scalar=g[:, 0:1], in1=var,
                                                   op0=ALU.mult, op1=ALU.add).then_inc(s_gs[norm], 1)
                if 2 in parts:
                    dve.wait_ge(s_gstd[norm], START + j + 1)
                    nc.vector.reciprocal(g[:, 3:4], g[:, 2:3]).then_inc(s_gs[norm], 1)
                    after(6)
                    nc.vector.tensor_tensor(g[:, 4:5], g[:, 3:4], cols[:, 3 * norm + 1:3 * norm + 2],
                                            ALU.mult).then_inc(s_gs[norm], 1)
                    after(7)
                    nc.vector.tensor_tensor(g[:, 6:7], g[:, 4:5], mean, ALU.mult).then_inc(s_gs[norm], 1)
                    after(8)
                    nc.vector.tensor_tensor(g[:, 5:6], cols[:, 3 * norm + 2:3 * norm + 3], g[:, 6:7],
                                            ALU.subtract).then_inc(s_gs[norm], 1)

            with dve.Fori(0, J) as j:
                image = xe[:, bass.ds(j, 1)].rearrange("p j y x -> p (j y) x")
                dve.wait_ge(s_edge, START + j * 4 + 4)
                nc.vector.tensor_tensor(down[:, bass.ds(j, 1)].rearrange("p j y x -> p (j y) x"),
                                        image[:, 1:, :], image[:, :-1, :], ALU.subtract).then_inc(s_dy, 1)
                group_norm(0, j)
            dve.wait_ge(s_dy, START + J)
            def add_output(j):
                xj = X[:, bass.ds(j * HW, HW)]
                dve.wait_ge(s_y, START + j + 1)
                nc.vector.tensor_tensor(xj, xj, y[:], ALU.add).then_inc(s_out, 1)

            def quarter(j, prev):
                rows = down[:, bass.ds(j, 1)].rearrange("p j y x -> p (j y) x")

                def add_quad(i):
                    n, n2 = quads[i]
                    dve.wait_ge(s_sum, START + j * NI + (n2 + 1))
                    nc.vector.tensor_tensor(isum[:, n % RING, :], isum[:, n % RING, :],
                                            isum[:, n2 % RING, :], ALU.add).then_inc(s_quad, 1)

                added = 0
                for n, (k, m) in enumerate(ITEMS):
                    for e, at in enumerate((MID + m, MID - m - 1)):
                        q = 2 * n + e
                        dve.wait_ge(s_ramp, START + j * (2 * NI) + (q + 1))
                        dve.wait_ge(s_sum, START + j * NI + max(0, n - 1))
                        nc.vector.scalar_tensor_tensor(
                            out=term[:, q % 4, :].rearrange("p (y x) -> p y x", x=W),
                            in0=ramp[:, q % 4, :].rearrange("p (y x) -> p y x", x=W), scalar=1.0,
                            in1=rows[:, at:at + H, k:k + W], op0=ALU.min, op1=ALU.mult).then_inc(s_term, 1)
                    while added < NQ and quads[added][1] <= n - 2:
                        add_quad(added)
                        added += 1
                    if prev is not None and n in DVE_PARTS:
                        group_norm(1, prev, (DVE_PARTS.index(n),))
                    if prev is not None and n == ADD_SLOT:
                        add_output(prev)
                while added < NQ:
                    add_quad(added)
                    added += 1

            quarter(0, None)
            with dve.Fori(0, J - 1) as prev:
                quarter(prev + 1, prev)
            group_norm(1, J - 1)
            add_output(J - 1)
            dve.wait_ge(s_out, START + J)


CONSTS = ["ident", "ident16", "iota", "eps", "neg_half", "minus_iota", "one"]


def dft_matrices(np):
    y, x = np.divmod(np.arange(PIX), PATCH)
    fa, fb, fc, seen = [], [], [], set()
    for v in range(PATCH):
        for u in range(PATCH):
            if (v, u) in seen:
                continue
            mirror = (-v % PATCH, -u % PATCH)
            seen |= {(v, u), mirror}
            angle = 2 * np.pi * ((v * y + u * x) % PATCH) / PATCH
            re, im = np.cos(angle), -np.sin(angle)
            if mirror == (v, u):
                fa, fb, fc = fa + [re], fb + [re], fc + [re / PIX]
            else:
                fa += [re, im, re, im]
                fb += [re, im, im, re]
                fc += [2 * re / PIX, -2 * re / PIX, 2 * im / PIX, 2 * im / PIX]
    fa, fb, fc = (np.array(m).astype(np.float32) for m in (fa, fb, fc))
    sides = np.zeros((2, P, 2, PRODS), np.float32)
    for n, m in enumerate((fa, fb)):
        for h in range(2):
            sides[n, PIX * h:PIX * (h + 1), h] = m.T
    return sides[0], sides[1], fc


def lay_out(inputs, np):
    f = np.float32
    a = {"x": np.ascontiguousarray(inputs["x"])}
    books = np.asarray(inputs["L0_conv_codebooks"])
    a["codes"] = np.ascontiguousarray(books.reshape(NC, KC, P, C).transpose(2, 0, 1, 3))
    a["codes_t"] = np.ascontiguousarray(books.transpose(0, 2, 1))
    a["ident"] = np.eye(P, dtype=f)
    a["ident16"] = np.eye(P, dtype=np.float16)
    a["iota"] = (np.arange(P)[:, None] + P * np.arange(KC)[None, :]).astype(f)
    a["minus_iota"] = -a["iota"]
    a["one"] = np.ones((P, 1), f)
    a["eps"] = np.full((P, 1), GN_EPS, f)
    a["neg_half"] = np.full((P, P), -0.5, f)

    wh, wdw = np.asarray(inputs["L1_conv_w_hidden"]), np.asarray(inputs["L1_conv_w_dw"])
    bh, bdw = np.asarray(inputs["L1_conv_b_hidden"]), np.asarray(inputs["L1_conv_b_dw"])
    a["l1_wh"] = np.concatenate([np.tile(wh.T, (3, 1)), np.tile(bh[None], (3, 1)), bdw[None]])
    by_tap = wdw.transpose(2, 1, 0)
    a["l1_wd"] = np.concatenate([np.repeat(by_tap, C, axis=0), by_tap,
                                 np.tile(np.array([0, 1, 0], f)[None, :, None], (1, 1, HID))])
    inside = np.zeros((H + 2, PADW), f)
    inside[1:H + 1, 1:W + 1] = 1
    taps = np.array([[inside[ky:ky + H, kx:kx + W] for ky in range(3)] for kx in range(3)] + [np.ones((3, H, W))])
    a["l1_inside"] = taps.reshape(4, 3, PAIRS, PATCH, PAIRS, PATCH).transpose(0, 1, 2, 4, 3, 5).reshape(
        4, 3, HW).astype(f)
    a["l1_fa"], a["l1_fb"], a["l1_fc"] = dft_matrices(np)
    a["l1_lnw"] = np.tile(np.asarray(inputs["L1_conv_ln_w"])[None], (P, 1))
    a["l1_lnb"] = np.tile(np.asarray(inputs["L1_conv_ln_b"])[None], (P, 1))
    wp = np.asarray(inputs["L1_conv_w_proj"]).T
    none = np.zeros((QC, C), f)
    a["l1_wp"] = np.stack([np.concatenate([wp, none]), np.concatenate([none, wp])], axis=1)
    a["l1_bp"] = np.tile(np.asarray(inputs["L1_conv_b_proj"]), G)[:, None]

    w = np.zeros((G, C, DIRS, TAPS, G, C), f)
    names = ("ud", "du", "lr", "rl")
    for d, n in enumerate(names):
        for g in range(G):
            w[g, :, d, :, g, :] = np.asarray(inputs["L2_conv_w_" + n]).transpose(1, 2, 0)
    a["l2_w"] = w.reshape(P, DIRS, TAPS, P)
    a["l2_b"] = np.stack([np.tile(np.asarray(inputs["L2_conv_b_" + n]), G) for n in names], axis=1)

    def blocks(w, taps):
        m = np.zeros((G, C, taps, G, C), f)
        for g in range(G):
            m[g, :, :, g, 0:w.shape[0]] = w.transpose(1, 2, 0)
        return m.reshape(P, taps, P)

    def column(v):
        m = np.zeros((G, C), f)
        m[:, 0:len(v)] = v
        return m.reshape(P)

    g_in = {n: np.asarray(inputs["L3_conv_" + n]) for n in
            ("w_off", "b_off", "g_gn_off", "b_gn_off", "w_dsc", "b_dsc", "g_gn", "b_gn")}
    a["l3_w_off"] = blocks(g_in["w_off"][:OFFC].reshape(OFFC, C, 9), 9)
    a["l3_w_dsc"] = blocks(g_in["w_dsc"].reshape(C, C, SNAKE), SNAKE)
    a["l3_cols"] = np.stack([column(g_in["b_off"][:OFFC]), column(g_in["g_gn_off"][:OFFC]),
                             column(g_in["b_gn_off"][:OFFC]), column(g_in["b_dsc"]), column(g_in["g_gn"]),
                             column(g_in["b_gn"])], axis=1)
    sums = np.zeros((G, C, len(POINTS), G, C), f)
    for c, k in enumerate(POINTS):
        for i in range(k, MID) if k < MID else range(MID + 1, k + 1):
            for g in range(G):
                sums[g, i, c, g, :] = 1
    a["l3_sums"] = sums.reshape(P, len(POINTS), P)
    at = np.arange(P)
    a["l3_avg"] = np.stack([(at[:, None] // n == at[None, :] // n).astype(f) / f(n) for n in (2, 4)], axis=1)
    a["l3_minus"] = np.tile(-np.arange(MID, dtype=f)[None], (P, 1))
    return {n: np.ascontiguousarray(v) for n, v in a.items()}


def build_program(nc, io, out):
    with ExitStack() as ctx:
        def t(name, shape, dt=F32):
            return ctx.enter_context(nc.sbuf_tensor(name, shape, dt))

        X = t("X", [P, J * HW])
        ps = ctx.enter_context(nc.psum_tensor("ps", [P, 8, BANK], F32))
        const = {name: t("c_" + name, list(io[name].shape), io[name].dtype) for name in CONSTS}
        s_load = ctx.enter_context(nc.semaphore("load"))
        s_store = ctx.enter_context(nc.semaphore("store"))
        with nc.Block() as block:
            @block.sync
            def _(sp):
                for g in range(G):
                    sp.dma_start(X[C * g:C * g + C, :].rearrange("c (j f) -> c j f", j=J),
                                 io["x"][J * g:J * g + J].rearrange("j c h w -> c j (h w)")).then_inc(s_load, 16)
                for name in CONSTS:
                    sp.dma_start(const[name][:], io[name]).then_inc(s_load, 16)
                sp.wait_ge(s_load, 16 * (G + len(CONSTS)))
        for layer in LAYERS:
            layer(nc, ps, X, io, const)
        with nc.Block() as block:
            @block.sync
            def _(sp):
                for g in range(G):
                    sp.dma_start(out[J * g:J * g + J].rearrange("j c h w -> c j (h w)"),
                                 X[C * g:C * g + C, :].rearrange("c (j f) -> c j f", j=J)).then_inc(s_store, 16)
                sp.wait_ge(s_store, 16 * G)


LAYERS = [block_l0, block_l1, block_l2, block_l3]


def kernel(**inputs):
    import numpy as np
    import concourse.bacc as bacc
    from concourse.bass_utils import run_bass_kernel_spmd

    arrays = lay_out(inputs, np)
    nc = bacc.Bacc("TRN2", target_bir_lowering=False, num_devices=1)
    io = {n: nc.dram_tensor("in_" + n, a.shape, mybir.dt.from_np(a.dtype), kind="ExternalInput").ap()
          for n, a in arrays.items()}
    out = nc.dram_tensor("out", (B, C, H, W), F32, kind="ExternalOutput").ap()
    build_program(nc, io, out)
    r = run_bass_kernel_spmd(nc, [{"in_" + n: a for n, a in arrays.items()}], core_ids=[0])
    return r.results[0]["out"]
```

```python
from contextlib import ExitStack

import concourse.bass as bass
from concourse import mybir

F32 = mybir.dt.float32
BF16 = mybir.dt.bfloat16
F16 = mybir.dt.float16
U32 = mybir.dt.uint32
ALU = mybir.AluOpType
ACT = mybir.ActivationFunctionType
AX_X = mybir.AxisListType.X

P = 128
B, C, H, W = 16, 32, 32, 32
G = P // C
J = B // G
HW = H * W
BANK = 512
EPS = 1e-5
START = 1

NC, K = 8, 512
KC = K // P
HALF = HW // 2
TT = HALF // P
TILES = TT * G
PARTS = 3
LOADS = G + 2
ONEHOT = ("pool", "pool", "act", "act")
LOWEST = -3.0e38


def prime(nc, semaphores):
    with nc.Block() as block:
        @block.sync
        def _(sp):
            for s in semaphores:
                sp.sem_inc(s, START)


def block_l0(nc, ps, X, io, const):
    ident, ident16, iota, eps = const["ident"], const["ident16"], const["iota"], const["eps"]
    minus_iota, one = const["minus_iota"], const["one"]
    with ExitStack() as ctx:
        def t(name, shape, dt=F32):
            return ctx.enter_context(nc.sbuf_tensor("l0_" + name, shape, dt))

        semaphores = []

        def sem(name):
            semaphores.append(ctx.enter_context(nc.semaphore("l0_" + name)))
            return semaphores[-1]

        xn = t("xn", [P, J * HW])
        picked = t("picked", [P, HALF])
        res = t("res", [P, HW])
        stats = t("stats", [P, J, 2, 6])
        mv = t("mv", [P, J, 2])
        std = t("std", [P, J])
        rstd = t("rstd", [P, J])
        ct_blk = t("ct_blk", [P, 2, G, K])
        csq = t("csq", [P, NC, K])
        csq_slot = t("csq_slot", [P, 2, K])
        cb = t("cb", [P, NC, KC, C])
        cb_left = t("cb_left", [P, NC, KC, C])
        cbp = t("cbp", [P, NC, PARTS, KC, C], BF16)
        cbp_slot = t("cbp_slot", [P, 2, PARTS, KC, C], BF16)
        scored = t("scored", [P, 4, K])
        top = t("top", [P, 2, TILES])
        idx8 = t("idx8", [P, 2, TILES, 8], U32)
        idx16 = t("idx16", [P, 2, TILES], F16)
        ib16 = t("ib16", [P, G, HALF], F16)
        away = t("away", [P, 2, HALF], F16)
        onehot = t("onehot", [P, G, KC, HALF], BF16)
        ctsq = t("ctsq", [P, NC, K])

        s_x = [sem("x_first"), sem("x_second")]
        s_ct = sem("ct")
        s_cb = sem("cb")
        s_in = sem("in")
        s_zero = sem("zero")
        s_sq = sem("sq")
        s_csqp = sem("csqp")
        s_csq = sem("csq")
        s_cbp = sem("cbp")
        s_slot = [sem("slot_even"), sem("slot_odd")]
        s_gn = sem("gn")
        s_std = sem("std")
        s_xn = sem("xn")
        s_res = sem("res")
        s_score = sem("score")
        s_dve = sem("dve")
        s_idx = sem("idx")
        s_ibp = sem("ibp")
        s_ib = sem("ib")
        s_away = sem("away")
        s_oh = {e: sem("oh_" + e) for e in sorted(set(ONEHOT))}
        s_pick = sem("pick")
        s_sum = sem("sum")
        s_out = sem("out")
        s_alone = sem("alone")

        PER_HALF = 2 * TILES
        LAST = 2 * J * NC - 1
        SHARE = {e: [c for c in range(KC) if ONEHOT[c] == e] for e in sorted(set(ONEHOT))}

        def max_count(n):
            return max(1, 2 * n)

        prime(nc, semaphores)
        block = ctx.enter_context(nc.Block())

        def halves(eng, body):
            def stage(j, s, par, use, which=(0, 1)):
                for h in which:
                    body(h, par, j * NC + s, j * (NC // 2) + use, s if isinstance(s, int) else None, j)

            def quarter(j):
                stage(j, 0, 0, 0, (1,))
                with eng.Fori(0, (NC - 2) // 2) as pair:
                    stage(j, pair * 2 + 1, 1, pair)
                    stage(j, pair * 2 + 2, 0, pair + 1)
                stage(j, NC - 1, 1, NC // 2 - 1)

            stage(0, 0, 0, 0, (0,))
            with eng.Fori(0, J - 1) as j:
                quarter(j)
                stage(j + 1, 0, 0, 0, (0,))
            quarter(J - 1)

        @block.sync
        def _(sp):
            for i in range(2):
                for g in range(G):
                    js = slice(i * (J // 2), (i + 1) * (J // 2))
                    quarters = X[C * g:C * g + C, HW * js.start:HW * js.stop]
                    sp.dma_start(quarters.rearrange("c (j f) -> c j f", f=HW),
                                 io["x"][J * g + js.start:J * g + js.stop].rearrange("j c h w -> c j (h w)")
                                 ).then_inc(s_x[i], 16)

            def load(s, par):
                for g in range(G):
                    src = io["codes_t"][bass.ds(s, 1)].rearrange("s c k -> (s c) k")
                    sp.dma_start(ct_blk[C * g:C * g + C, par, g, :], src).then_inc(s_slot[par], 16)
                sp.dma_start(csq_slot[:, par, :],
                             csq[:, bass.ds(s, 1), :].rearrange("p s k -> p (s k)")).then_inc(s_slot[par], 16)
                sp.dma_start(cbp_slot[:, par].rearrange("p a k c -> p (a k c)"),
                             cbp[:, bass.ds(s, 1)].rearrange("p s a k c -> p (s a k c)")).then_inc(s_slot[par], 16)

            sp.wait_ge(s_zero, START + 3)
            sp.wait_ge(s_csq, START + 1)
            sp.wait_ge(s_cbp, START + 6)
            load(0, 0)
            sp.wait_ge(s_zero, START + 4)
            sp.wait_ge(s_csq, START + NC)

            def quarter(j, last):
                sp.wait_ge(s_pick, START + j * (2 * G * NC) + 1)
                load(1, 1)
                with sp.Fori(0, (NC - 2) // 2) as pair:
                    for u in range(2):
                        s = pair * 2 + (1 + u)
                        sp.wait_ge(s_pick, START + (j * NC + s) * (2 * G) + 1)
                        load(s + 1, u)
                if not last:
                    sp.wait_ge(s_pick, START + (j * NC + (NC - 1)) * (2 * G) + 1)
                    load(0, 0)

            with sp.Fori(0, J - 1) as j:
                quarter(j, False)
            quarter(J - 1, True)
            for par in range(2):
                sp.wait_ge(s_slot[par], START + 16 * LOADS * (J * NC // 2))

        @block.tensor
        def _(pe):
            pe.wait_ge(s_ct, START + 32)
            pe.wait_ge(s_sq, START + 1)
            pe.wait_ge(s_zero, START + 2)
            for s in range(NC):
                pe.matmul(ps[:, s, :], const["neg_half"][:], ctsq[:, s, :],
                          start=True, stop=True).then_inc(s_csqp, 1)
            pe.wait_ge(s_csq, START + NC)
            pe.wait_ge(s_in, START + 16 * (len(CONSTS) - 1))
            pe.wait_ge(s_xn, START + J)

            def scores(h, par, hs, tt):
                for g in range(G):
                    n = G * tt + g
                    if n >= G:
                        pe.wait_ge(s_dve, START + hs * PER_HALF + (PER_HALF + max_count(n - G)))
                    else:
                        pe.wait_ge(s_dve, START + hs * PER_HALF + max_count(TILES - G + g))
                    at = HALF * h + P * tt
                    pe.matmul(ps[:, g, :], res[:, at:at + P], ct_blk[:, par, g, :],
                              start=True, stop=True).then_inc(s_score, 1)

            def spread(h, hs, g):
                if g == 0:
                    pe.wait_ge(s_idx, START + hs + 1)
                if g >= 2:
                    pe.wait_ge(s_ib, START + hs * G + (g - 1))
                for tt in range(TT):
                    mm = pe.matmul(ps[:, 4 + g % 2, P * tt:P * tt + P],
                                   idx16[:, h, G * tt + g:G * tt + g + 1].to_broadcast([P, P]), ident16[:],
                                   start=True, stop=True)
                mm.then_inc(s_ibp, 1)

            def pick(h, par, hs, g):
                for e in SHARE:
                    pe.wait_ge(s_oh[e], START + (hs * G + (g + 1)) * len(SHARE[e]))
                for a in range(PARTS):
                    for c in range(KC):
                        mm = pe.matmul(ps[C * g:C * g + C, 6 + h, :], cbp_slot[:, par, a, c, :],
                                       onehot[:, g, c, :], start=False, stop=True, skip_group_check=True)
                mm.then_inc(s_pick, 1)

            def half(h, par, st, use, s, j):
                hs = st * 2 + h
                if h == 0:
                    pe.wait_ge(s_slot[par], START + use * (16 * LOADS) + 16 * LOADS)
                pe.wait_ge(s_res, START + hs + 1)
                if isinstance(hs, int) and hs == 0:
                    for tt in range(TT):
                        scores(h, par, hs, tt)
                    return
                last, lh, lpar = hs - 1, 1 - h, par if h else 1 - par
                scores(h, par, hs, 0)
                spread(lh, last, 0)
                spread(lh, last, 1)
                scores(h, par, hs, 1)
                spread(lh, last, 2)
                spread(lh, last, 3)
                scores(h, par, hs, 2)
                if s == 0 and h == 1:
                    pe.wait_ge(s_sum, START + j * 2 + 2)
                    for i in range(2):
                        pe.matmul(ps[:, 6 + i, :], ident[:], xn[:, bass.ds(j * HW + i * HALF, HALF)],
                                  start=True, stop=True, skip_group_check=True)
                pick(lh, lpar, last, 0)
                pick(lh, lpar, last, 1)
                scores(h, par, hs, 3)
                pick(lh, lpar, last, 2)
                pick(lh, lpar, last, 3)

            halves(pe, half)
            for g in range(G):
                spread(1, LAST, g)
            for g in range(G):
                pick(1, 1, LAST, g)

        @block.scalar
        def _(act):
            act.dma_start(ctsq[0:C], io["codes_t"].rearrange("s c k -> c s k")).then_inc(s_ct, 16)
            act.dma_start(const["neg_half"][:], io["neg_half"]).then_inc(s_ct, 16)
            act.dma_start(cb[:], io["codes"]).then_inc(s_cb, 16)
            rest = [name for name in CONSTS if name != "neg_half"]
            for name in rest:
                act.dma_start(const[name][:], io[name]).then_inc(s_in, 16)
            act.wait_ge(s_ct, START + 32)
            nc.scalar.activation(ctsq[0:C], ctsq[0:C], ACT.Square).then_inc(s_sq, 1)
            for s in range(NC):
                act.wait_ge(s_csqp, START + s + 1)
                nc.scalar.copy(csq[:, s, :], ps[:, s, :]).then_inc(s_csq, 1)
                if s == 1:
                    act.wait_ge(s_in, START + 16 * len(rest))
                    act.wait_ge(s_gn, START + 3 * J)
                    nc.scalar.activation(std[:], mv[:, :, 1], ACT.Sqrt, bias=eps[:]).then_inc(s_std, 1)

            def onehot_act(hs, g):
                if isinstance(hs, int) and hs == LAST:
                    return
                mine = SHARE["act"]
                for i, c in enumerate(mine):
                    n = hs * (G * len(mine)) + (g * len(mine) + i)
                    act.wait_ge(s_ib, START + hs * G + (g + 1))
                    nc.scalar.activation(away[:, (g * len(mine) + i) % 2, :], ib16[:, g, :], ACT.Abs,
                                         bias=minus_iota[:, c:c + 1]).then_inc(s_away, 1)
                    act.wait_ge(s_away, START + n + 1)
                    nc.scalar.activation(onehot[:, g, c, :], away[:, (g * len(mine) + i) % 2, :], ACT.Relu,
                                         bias=one[:], scale=-1.0).then_inc(s_oh["act"], 1)

            def first_residual(h, j):
                nc.scalar.copy(res[:, HALF * h:HALF * (h + 1)],
                               xn[:, bass.ds(j * HW + h * HALF, HALF)]).then_inc(s_res, 1)

            def half(h, par, st, use, s, j):
                hs = st * 2 + h
                act.wait_ge(s_dve, START + hs * PER_HALF + 2 * PER_HALF)
                if s == NC - 1 and not isinstance(j, int):
                    first_residual(h, j + 1)
                nc.scalar.copy(idx16[:, h, :], idx8[:, h, :, 0]).then_inc(s_idx, 1)
                for g in range(G):
                    act.wait_ge(s_ibp, START + hs * G + (g + 1))
                    nc.scalar.copy(ib16[:, g, :], ps[:, 4 + g % 2, :]).then_inc(s_ib, 1)
                    if g >= 1:
                        onehot_act(hs, g - 1)
                onehot_act(hs, G - 1)
                if s != NC - 1:
                    act.wait_ge(s_pick, START + hs * G + (G + 1))
                    nc.scalar.copy(res[:, HALF * h:HALF * (h + 1)], ps[:, 6 + h, :]).then_inc(s_res, 1)

            act.wait_ge(s_xn, START + J)
            for h in range(2):
                first_residual(h, 0)
            halves(act, half)

        @block.gpsimd
        def _(pool):
            nc.gpsimd.memset(ctsq[C:2 * C], 0.0).then_inc(s_zero, 1)
            nc.gpsimd.memset(ctsq[2 * C:P], 0.0).then_inc(s_zero, 1)
            pool.wait_ge(s_zero, START + 2)
            nc.gpsimd.memset(ct_blk[:, 0], 0.0).then_inc(s_zero, 1)
            nc.gpsimd.memset(ct_blk[:, 1], 0.0).then_inc(s_zero, 1)

            def half(h, par, st, use, s, j):
                hs = st * 2 + h
                if isinstance(hs, int) and hs == LAST:
                    return
                for g in range(G):
                    pool.wait_ge(s_ib, START + hs * G + (g + 1))
                    pool.sem_inc(s_alone, 1)
                    for c in SHARE["pool"]:
                        nc.gpsimd.tensor_scalar(onehot[:, g, c, :], ib16[:, g, :], iota[:, c:c + 1], None,
                                                ALU.is_equal).then_inc(s_oh["pool"], 1)

            halves(pool, half)

        @block.vector
        def _(dve):
            dve.sem_inc(s_dve, PER_HALF)
            dve.sem_inc(s_pick, 1)
            def maximum(h, par, n):
                nc.vector.tensor_tensor_reduce(
                    out=scored[:, n % 4, :], in0=ps[:, n % G, :], in1=csq_slot[:, par, :], scale=1.0,
                    scalar=LOWEST, op0=ALU.add, op1=ALU.max, accum_out=top[:, h, n:n + 1]).then_inc(s_dve, 1)

            def index(h, n):
                nc.vector.max_index(idx8[:, h, n, :], top[:, h, n:n + 1].to_broadcast([P, 8]),
                                    scored[:, n % 4, :]).then_inc(s_dve, 1)

            def finish(h, last, j):
                at = bass.ds(j * HW + h * HALF, HALF)
                dve.wait_ge(s_pick, START + last * G + (G + 1))
                dve.wait_ge(s_out, START + j * 2 + (h + 1))
                nc.vector.tensor_tensor(picked[:], xn[:, at], ps[:, 6 + h, :], ALU.subtract).then_inc(s_sum, 1)
                dve.wait_ge(s_sum, START + j * 2 + (h + 3))
                nc.vector.tensor_tensor(X[:, at], X[:, at], picked[:], ALU.add).then_inc(s_out, 1)

            def half(h, par, st, use, s, j):
                hs = st * 2 + h
                if h == 0:
                    dve.wait_ge(s_slot[par], START + use * (16 * LOADS) + 16 * LOADS)
                dve.wait_ge(s_score, START + hs * TILES + 1)
                dve.wait_ge(s_dve, START + hs * PER_HALF + (2 * (TILES - 4) + 3))
                dve.sem_inc(s_alone, 1)
                maximum(h, par, 0)
                for n in range(TILES - 1):
                    dve.wait_ge(s_score, START + hs * TILES + (n + 2))
                    dve.wait_ge(s_dve, START + hs * PER_HALF + (PER_HALF + max_count(n)))
                    dve.sem_inc(s_alone, 1)
                    maximum(h, par, n + 1)
                    index(h, n)
                dve.wait_ge(s_dve, START + hs * PER_HALF + (PER_HALF + max_count(TILES - 1)))
                dve.sem_inc(s_alone, 1)
                index(h, TILES - 1)
                if s == NC - 1 and h == 1:
                    finish(0, hs - 1, j)
                if s == 0 and h == 0 and not (isinstance(hs, int) and hs == 0):
                    finish(1, hs - 1, j - 1)

            dve.sem_inc(s_sum, 2)
            dve.sem_inc(s_out, 1)
            dve.wait_ge(s_cb, START + 16)
            nc.vector.tensor_scalar(cbp[:, :, 0], cb[:], -1.0, None, ALU.mult).then_inc(s_cbp, 1)
            dve.wait_ge(s_cbp, START + 1)
            nc.vector.scalar_tensor_tensor(out=cb_left[:], in0=cb[:], scalar=-1.0, in1=cbp[:, :, 0],
                                           op0=ALU.mult, op1=ALU.subtract).then_inc(s_cbp, 1)
            dve.wait_ge(s_cbp, START + 2)
            nc.vector.tensor_copy(cbp[:, :, 1], cb_left[:]).then_inc(s_cbp, 1)
            dve.wait_ge(s_cbp, START + 3)
            nc.vector.tensor_tensor(cb[:], cb_left[:], cbp[:, :, 1], ALU.subtract).then_inc(s_cbp, 1)
            dve.wait_ge(s_cbp, START + 4)
            nc.vector.tensor_copy(cbp[:, :, 2], cb[:]).then_inc(s_cbp, 2)
            for j in range(J):
                if j % (J // 2) == 0:
                    dve.wait_ge(s_x[j // (J // 2)], START + 16 * G)
                for h in range(2):
                    at = j * HW + h * HALF
                    nc.vector.bn_stats(stats[:, j, h, :], X[:, at:at + HALF]).then_inc(s_gn, 1)
            dve.wait_ge(s_gn, START + 2 * J)
            for j in range(J):
                nc.vector.bn_aggr(mv[:, j, :], stats[:, j]).then_inc(s_gn, 1)
            dve.wait_ge(s_std, START + 1)
            nc.vector.reciprocal(rstd[:], std[:]).then_inc(s_gn, 1)
            dve.wait_ge(s_gn, START + 3 * J + 1)
            for j in range(J):
                at = slice(j * HW, (j + 1) * HW)
                nc.vector.tensor_scalar(xn[:, at], X[:, at], mv[:, j, 0:1], rstd[:, j:j + 1], ALU.subtract,
                                        ALU.mult).then_inc(s_xn, 1)
            dve.wait_ge(s_xn, START + J)
            halves(dve, half)
            for g in range(G):
                dve.wait_ge(s_ib, START + LAST * G + (g + 1))
                for c in range(KC):
                    nc.vector.tensor_scalar(onehot[:, g, c, :], ib16[:, g, :], iota[:, c:c + 1], None,
                                            ALU.is_equal).then_inc(s_oh[ONEHOT[c]], 1)
            finish(1, LAST, J - 1)
            dve.wait_ge(s_out, START + 2 * J + 1)


PATCH = 8
PAIRS = H // PATCH
TOKT = HW // P
HID = 6 * C
QC = 2 * C
PADW = W + 2
TAPROWS = 3 * C + 4
PIX = PATCH * PATCH
PRODS = 4 + 4 * (PIX - 4) // 2


def block_l1(nc, ps, X, io, const):
    ident, eps = const["ident"], const["eps"]
    with ExitStack() as ctx:
        def t(name, shape, dt=F32):
            return ctx.enter_context(nc.sbuf_tensor("l1_" + name, shape, dt))

        semaphores = []

        def sem(name):
            semaphores.append(ctx.enter_context(nc.semaphore("l1_" + name)))
            return semaphores[-1]

        stats = t("stats", [P, J, 2, 6])
        mv = t("mv", [P, J, 2])
        std = t("std", [P, J])
        rstd = t("rstd", [P, J])
        xpad = t("xpad", [P, J, H + 2, PADW])
        xt = t("xt", [P, 3, 3, HW])
        xi = t("xi", [TAPROWS, 3, G, HW])
        wh = t("wh", [TAPROWS, HID])
        wd = t("wd", [TAPROWS, 3, HID])
        wc = t("wc", [TAPROWS, 3, HID])
        fa = t("fa", [P, 2, PRODS])
        fb = t("fb", [P, 2, PRODS])
        fc = t("fc", [PRODS, PIX])
        lnw = t("lnw", [P, QC])
        lnb = t("lnb", [P, QC])
        wp = t("wp", [P, 2, C])
        bp = t("bp", [P, 1])
        qkv = t("qkv", [P, G, TOKT, HID])
        qf = t("qf", [PRODS, 2, BANK])
        prod = t("prod", [PRODS, 2, BANK])
        msum = t("msum", [P, TOKT])
        mean = t("mean", [P, TOKT])
        cen = t("cen", [P, TOKT, QC])
        sq = t("sq", [P, TOKT, QC])
        vsum = t("vsum", [P, TOKT])
        pstd = t("pstd", [P, TOKT])
        prstd = t("prstd", [P, TOKT])
        y = [t(f"y{i}", [P, TOKT, QC]) for i in range(4)]
        yt = t("yt", [P, BANK])
        biased = t("biased", [P, 2, BANK])

        s_in = sem("in")
        s_border = sem("border")
        s_wc = sem("wc")
        s_gn = [sem("gn_first"), sem("gn_rest")]
        s_std = sem("std")
        s_xn = sem("xn")
        s_xta = sem("xta")
        s_xtd = sem("xtd")
        s_xi = [sem(f"xi{g}") for g in range(G)]
        s_conv = sem("conv")
        s_qkv = sem("qkv")
        s_dft = sem("dft")
        s_qf = sem("qf")
        s_prod = sem("prod")
        s_inv = sem("inv")
        s_ln = sem("ln")
        s_sq = sem("sq")
        s_pstd = sem("pstd")
        s_pool = sem("pool")
        s_tr = sem("tr")
        s_yt = sem("yt")
        s_proj = sem("proj")
        s_biased = sem("biased")
        s_out = sem("out")
        s_alone = sem("alone")
        LN_STEPS = 7
        ACT_TAPS = 9 - G

        def lay_tap(copy, n, j):
            kx, ky = divmod(n, 3)
            image = xpad[:, bass.ds(j, 1), ky:ky + H, kx:kx + W].rearrange("p j y x -> p (j y) x")
            src = image.rearrange("p (a r) (b c) -> p a b r c", r=PATCH, c=PATCH)
            return copy(xt[:, kx, ky, :].rearrange("p (a b r c) -> p a b r c", a=PAIRS, b=PAIRS, r=PATCH), src)

        prime(nc, semaphores)
        block = ctx.enter_context(nc.Block())

        @block.sync
        def _(sp):
            loads = [(wh, "l1_wh"), (wd, "l1_wd"), (fa, "l1_fa"), (fb, "l1_fb"), (fc, "l1_fc"),
                     (lnw, "l1_lnw"), (lnb, "l1_lnb"), (wp, "l1_wp"), (bp, "l1_bp")]
            for dst, name in loads:
                sp.dma_start(dst[:], io[name]).then_inc(s_in, 16)
            for g in range(G):
                sp.dma_start(xi[3 * C:TAPROWS, :, g, :], io["l1_inside"]).then_inc(s_in, 16)
            sp.wait_ge(s_in, START + 16 * (len(loads) + G))

            def gather(j, after):
                sp.wait_ge(s_xta, START + j * ACT_TAPS + ACT_TAPS)
                sp.sem_inc(s_alone, 1)
                sp.wait_ge(s_xtd, START + j * (9 - ACT_TAPS) + (9 - ACT_TAPS))
                sp.sem_inc(s_alone, 1)
                for g in range(G):
                    if after is not None:
                        sp.wait_ge(s_conv, START + after * (G * PAIRS) + PAIRS * (g + 1))
                    for kx in range(3):
                        sp.dma_start(xi[C * kx:C * kx + C, :, g, :],
                                     xt[C * g:C * g + C, kx, :, :]).then_inc(s_xi[g], 16)

            gather(0, None)
            with sp.Fori(0, J - 1) as j:
                gather(j + 1, j)
            for g in range(G):
                sp.wait_ge(s_xi[g], START + 16 * 3 * J)

        @block.tensor
        def _(pe):
            pe.wait_ge(s_wc, START + 1)
            pe.wait_ge(s_in, START + 16 * (9 + G))

            def conv(g, j):
                pe.wait_ge(s_xi[g], START + j * (16 * 3) + 16 * 3)
                for py in range(PAIRS):
                    if g == 0 and py < 2:
                        pe.wait_ge(s_qkv, START + j * (G * PAIRS))
                    else:
                        pe.wait_ge(s_qkv, START + j * (G * PAIRS) + (g * PAIRS + py - 1))
                    for u in range(2):
                        for ky in range(3):
                            at = P * (2 * py + u)
                            mm = pe.matmul(ps[:, py % 2, HID * u:HID * (u + 1)],
                                           xi[:, ky, g, at:at + P], wc[:, ky, :],
                                           start=(ky == 0), stop=(ky == 2))
                    mm.then_inc(s_conv, 1)

            def dft(g, j, first):
                pe.wait_ge(s_qkv, START + j * (G * PAIRS) + (g + 1) * PAIRS)
                pe.wait_ge(s_prod, START + j * (2 * G) + 2 * g)
                for h in range(2):
                    if h == 1:
                        if not first or g >= 1:
                            pe.wait_ge(s_ln, START + j * (G * LN_STEPS) + ((g - 1) * LN_STEPS + 3))
                            pe.wait_ge(s_yt, START + j * G + (g - 1))
                    for m, at in ((fa, 0), (fb, QC)):
                        pe.matmul(ps[0:PRODS, 2 + 2 * h + (at > 0), :], m[:, h, :],
                                  qkv[:, g, :, at:at + QC], start=True, stop=True).then_inc(s_dft, 1)

            def inverse(g, j):
                pe.wait_ge(s_prod, START + j * (2 * G) + (2 * g + 2))
                for h in range(2):
                    mm = pe.matmul(ps[PIX * h:PIX * (h + 1), 4, :], fc[:], prod[:, h, :],
                                   start=True, stop=True)
                mm.then_inc(s_inv, 1)

            def project(g, j, next_dft=True):
                pe.wait_ge(s_pool, START + j * (3 * G) + (3 * G) + (3 * g + 3))
                if next_dft:
                    pe.wait_ge(s_prod, START + j * (2 * G) + 2 * (g + 2))
                for py in range(PAIRS):
                    mm = pe.transpose(ps[:, 5, P * py:P * (py + 1)],
                                      y[3][:, 2 * py:2 * py + 2, :].rearrange("p t c -> p (t c)"), ident[:])
                mm.then_inc(s_tr, 1)
                pe.wait_ge(s_yt, START + j * G + (g + 1))
                if g == 0:
                    pe.wait_ge(s_biased, START + j * 2)
                for u in range(2):
                    mm = pe.matmul(ps[C * g:C * g + C, 6 + u, :], wp[:, u, :], yt[:],
                                   start=True, stop=True)
                mm.then_inc(s_proj, 1)

            def quarter(j, prev, last):
                for g in range(G):
                    dft(g, j, prev is None)
                    if g + 1 < G:
                        conv(g + 1, j)
                    elif not last:
                        conv(0, j + 1)
                    if last and g == G - 1:
                        inverse(g, j)
                    if g:
                        project(g - 1, j)
                    elif prev is not None:
                        project(G - 1, prev)
                    if not last or g < G - 1:
                        inverse(g, j)

            conv(0, 0)
            quarter(0, None, False)
            with pe.Fori(0, J - 2) as prev:
                quarter(prev + 1, prev, False)
            quarter(J - 1, J - 2, True)
            project(G - 1, J - 1, False)

        @block.scalar
        def _(act):
            for i, js in enumerate((range(1), range(1, J))):
                act.wait_ge(s_gn[i], START + 3 * len(js))
                nc.scalar.activation(std[:, js.start:js.stop], mv[:, js.start:js.stop, 1], ACT.Sqrt,
                                     bias=eps[:]).then_inc(s_std, 1)
                if i == 0:
                    act.wait_ge(s_xn, START + 1)
                    for n in range(ACT_TAPS):
                        lay_tap(nc.scalar.copy, n, 0).then_inc(s_xta, 1)
            act.wait_ge(s_xn, START + J)

            def copy_qkv(g, j):
                for py in range(PAIRS):
                    act.wait_ge(s_conv, START + j * (G * PAIRS) + (g * PAIRS + py + 1))
                    act.wait_ge(s_pool, START + j * (3 * G) + 3 * (g + 1))
                    nc.scalar.copy(qkv[:, g, 2 * py:2 * py + 2, :].rearrange("p t c -> p (t c)"),
                                   ps[:, py % 2, 0:2 * HID]).then_inc(s_qkv, 1)

            def copy_yt(g, j):
                act.wait_ge(s_tr, START + j * G + (g + 1))
                act.wait_ge(s_proj, START + j * G + g)
                nc.scalar.copy(yt[:], ps[:, 5, :]).then_inc(s_yt, 1)

            def add_bias(j):
                act.wait_ge(s_proj, START + j * G + G)
                act.wait_ge(s_out, START + j * PAIRS)
                for u in range(2):
                    nc.scalar.activation(biased[:, u, :], ps[:, 6 + u, :], ACT.Identity,
                                         bias=bp[:]).then_inc(s_biased, 1)

            def quarter(j, prev, last):
                for g in range(G):
                    for h in range(2):
                        act.wait_ge(s_dft, START + j * (4 * G) + (4 * g + 2 * h + 1))
                        act.wait_ge(s_prod, START + j * (2 * G) + (max(0, 2 * g - 1 + h) if g else 0))
                        nc.scalar.copy(qf[:, h, :], ps[0:PRODS, 2 + 2 * h, :]).then_inc(s_qf, 1)
                    if g + 1 < G:
                        copy_qkv(g + 1, j)
                    elif not last:
                        copy_qkv(0, j + 1)
                    if g:
                        copy_yt(g - 1, j)
                    elif prev is not None:
                        copy_yt(G - 1, prev)
                        add_bias(prev)
                    if not last:
                        if g == 0:
                            for i in range(G):
                                act.wait_ge(s_xi[i], START + j * (16 * 3) + 16 * 3)
                        for n in range(3 * g, min(3 * g + 3, ACT_TAPS)):
                            lay_tap(nc.scalar.copy, n, j + 1).then_inc(s_xta, 1)
                    act.wait_ge(s_ln, START + j * (G * LN_STEPS) + (g * LN_STEPS + 4))
                    nc.scalar.activation(pstd[:], vsum[:], ACT.Sqrt, bias=eps[:],
                                         scale=1.0 / QC).then_inc(s_pstd, 1)

            copy_qkv(0, 0)
            quarter(0, None, False)
            with act.Fori(0, J - 2) as prev:
                quarter(prev + 1, prev, False)
            quarter(J - 1, J - 2, True)
            copy_yt(G - 1, J - 1)
            add_bias(J - 1)

        @block.gpsimd
        def _(pool):
            nc.gpsimd.memset(xpad[:, 0], 0.0).then_inc(s_border, 1)
            nc.gpsimd.memset(xpad[:, 1:], 0.0).then_inc(s_border, 1)
            pool.sem_inc(s_pool, 3 * G)
            pool.wait_ge(s_in, START + 16 * (9 + G))
            with pool.Fori(0, J) as j:
                for g in range(G):
                    v = qkv[:, g, :, 2 * QC:3 * QC]
                    pool.wait_ge(s_ln, START + j * (G * LN_STEPS) + (g * LN_STEPS + 3))
                    nc.gpsimd.tensor_tensor(sq[:], cen[:], cen[:], ALU.mult).then_inc(s_pool, 1)
                    pool.wait_ge(s_ln, START + j * (G * LN_STEPS) + (g * LN_STEPS + 6))
                    nc.gpsimd.tensor_tensor(y[1][:], y[0][:], lnw[:, None, :].to_broadcast([P, TOKT, QC]),
                                            ALU.mult).then_inc(s_pool, 1)
                    pool.wait_ge(s_ln, START + j * (G * LN_STEPS) + (g * LN_STEPS + 7))
                    pool.wait_ge(s_tr, START + j * G + g)
                    nc.gpsimd.tensor_tensor(y[3][:], y[2][:], v, ALU.mult).then_inc(s_pool, 1)

        @block.vector
        def _(dve):
            for i, js in enumerate((range(1), range(1, J))):
                for j in js:
                    for h in range(2):
                        at = j * HW + h * HALF
                        nc.vector.bn_stats(stats[:, j, h, :], X[:, at:at + HALF]).then_inc(s_gn[i], 1)
                dve.wait_ge(s_gn[i], START + 2 * len(js))
                for j in js:
                    nc.vector.bn_aggr(mv[:, j, :], stats[:, j]).then_inc(s_gn[i], 1)
                dve.wait_ge(s_std, START + i + 1)
                nc.vector.reciprocal(rstd[:, js.start:js.stop], std[:, js.start:js.stop]).then_inc(s_gn[i], 1)
                dve.wait_ge(s_gn[i], START + 3 * len(js) + 1)
                dve.wait_ge(s_border, START + i + 1)
                for j in js:
                    nc.vector.tensor_scalar(xpad[:, j, 1:H + 1, 1:W + 1],
                                            X[:, j * HW:(j + 1) * HW].rearrange("p (y x) -> p y x", x=W),
                                            mv[:, j, 0:1], rstd[:, j:j + 1], ALU.subtract,
                                            ALU.mult).then_inc(s_xn, 1)
                if i == 0:
                    dve.wait_ge(s_xn, START + 1)
                    for n in range(ACT_TAPS, 9):
                        lay_tap(nc.vector.tensor_copy, n, 0).then_inc(s_xtd, 1)
                    dve.wait_ge(s_in, START + 16 * (9 + G))
                    nc.vector.tensor_tensor(wc[:], wd[:], wh[:, None, :].to_broadcast([TAPROWS, 3, HID]),
                                            ALU.mult).then_inc(s_wc, 1)
            dve.wait_ge(s_xn, START + J)

            def add_output(j):
                xj = X[:, bass.ds(j * HW, HW)].rearrange("p (a r b c) -> p b a r c", r=PATCH, b=PAIRS, c=PATCH)
                for u in range(2):
                    dve.wait_ge(s_biased, START + j * 2 + (u + 1))
                    src = biased[:, u, :].rearrange("p (a x r c) -> p x a r c", x=2, r=PATCH, c=PATCH)
                    for x in range(2):
                        nc.vector.tensor_tensor(xj[:, 2 * u + x], xj[:, 2 * u + x], src[:, x],
                                                ALU.add).then_inc(s_out, 1)

            def quarter(j, prev, last):
                for g in range(G):
                    for h in range(2):
                        dve.wait_ge(s_dft, START + j * (4 * G) + (4 * g + 2 * h + 2))
                        dve.wait_ge(s_qf, START + j * (2 * G) + (2 * g + h + 1))
                        nc.vector.tensor_tensor(prod[:, h, :], qf[:, h, :], ps[0:PRODS, 3 + 2 * h, :],
                                                ALU.mult).then_inc(s_prod, 1)
                    base = g * LN_STEPS
                    patches = ps[:, 4, :].rearrange("p (t c) -> p t c", c=QC)
                    dve.wait_ge(s_inv, START + j * G + (g + 1))
                    nc.vector.tensor_reduce(msum[:], patches, AX_X, ALU.add).then_inc(s_ln, 1)
                    dve.wait_ge(s_ln, START + j * (G * LN_STEPS) + (base + 1))
                    nc.vector.tensor_scalar(mean[:], msum[:], 1.0 / QC, None, ALU.mult).then_inc(s_ln, 1)
                    dve.wait_ge(s_ln, START + j * (G * LN_STEPS) + (base + 2))
                    nc.vector.tensor_tensor(cen[:], patches, mean[:, :, None].to_broadcast([P, TOKT, QC]),
                                            ALU.subtract).then_inc(s_ln, 1)
                    dve.wait_ge(s_pool, START + j * (3 * G) + (3 * G) + (3 * g + 1))
                    nc.vector.tensor_reduce(vsum[:], sq[:], AX_X, ALU.add).then_inc(s_ln, 1)
                    if not last and g < 2:
                        for i in range(G):
                            dve.wait_ge(s_xi[i], START + j * (16 * 3) + 16 * 3)
                        for n in range(ACT_TAPS + 2 * g, ACT_TAPS + 2 * g + 2):
                            lay_tap(nc.vector.tensor_copy, n, j + 1).then_inc(s_xtd, 1)
                    dve.wait_ge(s_pstd, START + j * G + (g + 1))
                    nc.vector.reciprocal(prstd[:], pstd[:]).then_inc(s_ln, 1)
                    dve.wait_ge(s_ln, START + j * (G * LN_STEPS) + (base + 5))
                    nc.vector.tensor_tensor(y[0][:], cen[:], prstd[:, :, None].to_broadcast([P, TOKT, QC]),
                                            ALU.mult).then_inc(s_ln, 1)
                    dve.wait_ge(s_pool, START + j * (3 * G) + (3 * G) + (3 * g + 2))
                    nc.vector.tensor_tensor(y[2][:], y[1][:], lnb[:, None, :].to_broadcast([P, TOKT, QC]),
                                            ALU.add).then_inc(s_ln, 1)
                    if g == 0 and prev is not None:
                        add_output(prev)

            quarter(0, None, False)
            with dve.Fori(0, J - 2) as prev:
                quarter(prev + 1, prev, False)
            quarter(J - 1, J - 2, True)
            add_output(J - 1)
            dve.wait_ge(s_out, START + PAIRS * J)


TAPS = 9
MARGIN = TAPS // 2
PITCH = W + 2 * MARGIN
STEPS = H - 1
DIRS = 4


def block_l2(nc, ps, X, io, const):
    ident, eps = const["ident"], const["eps"]
    with ExitStack() as ctx:
        def t(name, shape, dt=F32):
            return ctx.enter_context(nc.sbuf_tensor("l2_" + name, shape, dt))

        semaphores = []

        def sem(name):
            semaphores.append(ctx.enter_context(nc.semaphore("l2_" + name)))
            return semaphores[-1]

        stats = t("stats", [P, J, 2, 6])
        mv = t("mv", [P, J, 2])
        std = t("std", [P, J])
        rstd = t("rstd", [P, J])
        seq = t("seq", [P, J, PITCH * PITCH])
        wt = t("wt", [P, DIRS, TAPS, P])
        bias = t("bias", [P, DIRS])

        s_in = sem("in")
        s_border = sem("border")
        s_gn = sem("gn")
        s_std = sem("std")
        s_xn = sem("xn")
        s_z = sem("z")
        s_line = sem("line")
        s_out = sem("out")
        s_alone = sem("alone")

        image = seq[:].rearrange("p j (y x) -> p j y x", x=PITCH)

        def line(d, n, shift=MARGIN):
            if d < 2:
                return seq[:, :, bass.ds(n * PITCH + (MARGIN * PITCH + shift), W)]
            return image[:, :, shift:shift + H, bass.ds(n + MARGIN, 1)].rearrange("p j y x -> p j (y x)")

        def scan(eng, step):
            for d in range(DIRS):
                step(d, 0, STEPS * d % 2, STEPS * d)
                with eng.Fori(0, STEPS // 2) as pair:
                    for u in range(2):
                        step(d, pair * 2 + (1 + u), (STEPS * d + 1 + u) % 2, pair * 2 + (1 + u + STEPS * d))

        def current(d, i):
            return i + 1 if d % 2 == 0 else i * -1 + (STEPS - 1)

        def previous(d, i):
            return i + 0 if d % 2 == 0 else i * -1 + STEPS

        prime(nc, semaphores)
        block = ctx.enter_context(nc.Block())

        @block.sync
        def _(sp):
            sp.dma_start(wt[:], io["l2_w"]).then_inc(s_in, 16)
            sp.dma_start(bias[:], io["l2_b"]).then_inc(s_in, 16)
            sp.wait_ge(s_in, START + 32)

        @block.gpsimd
        def _(pool):
            nc.gpsimd.memset(seq[:], 0.0).then_inc(s_border, 1)

        @block.tensor
        def _(pe):
            pe.wait_ge(s_in, START + 32)
            pe.wait_ge(s_xn, START + J)

            def step(d, i, parity, n):
                z = ps[:, parity, 0:J * W].rearrange("p (j w) -> p j w", j=J)
                if isinstance(i, int):
                    pe.wait_ge(s_line, START + n + 1)
                pe.matmul(z, ident[:], line(d, current(d, i)), start=True, stop=False)
                pe.wait_ge(s_line, START + n + 1)
                for k in range(TAPS):
                    mm = pe.matmul(z, wt[:, d, k, :], line(d, previous(d, i), k), start=False,
                                   stop=(k == TAPS - 1))
                mm.then_inc(s_z, 1)

            scan(pe, step)

        @block.scalar
        def _(act):
            act.wait_ge(s_gn, START + 3 * J)
            nc.scalar.activation(std[:], mv[:, :, 1], ACT.Sqrt, bias=eps[:]).then_inc(s_std, 1)

        @block.vector
        def _(dve):
            dve.sem_inc(s_line, 1)
            for j in range(J):
                for h in range(2):
                    at = j * HW + h * HALF
                    nc.vector.bn_stats(stats[:, j, h, :], X[:, at:at + HALF]).then_inc(s_gn, 1)
            dve.wait_ge(s_gn, START + 2 * J)
            for j in range(J):
                nc.vector.bn_aggr(mv[:, j, :], stats[:, j]).then_inc(s_gn, 1)
            dve.wait_ge(s_std, START + 1)
            nc.vector.reciprocal(rstd[:], std[:]).then_inc(s_gn, 1)
            dve.wait_ge(s_gn, START + 3 * J + 1)
            dve.wait_ge(s_border, START + 1)
            for j in range(J):
                nc.vector.tensor_scalar(image[:, j, MARGIN:MARGIN + H, MARGIN:MARGIN + W],
                                        X[:, j * HW:(j + 1) * HW].rearrange("p (y x) -> p y x", x=W),
                                        mv[:, j, 0:1], rstd[:, j:j + 1], ALU.subtract,
                                        ALU.mult).then_inc(s_xn, 1)
            dve.wait_ge(s_xn, START + J)

            def step(d, i, parity, n):
                dve.wait_ge(s_z, START + n + 1)
                z = ps[:, parity, 0:J * W].rearrange("p (j w) -> p j w", j=J)
                row = line(d, current(d, i))
                nc.vector.scalar_tensor_tensor(out=row, in0=z, scalar=bias[:, d:d + 1], in1=row,
                                               op0=ALU.add, op1=ALU.max).then_inc(s_line, 1)

            scan(dve, step)
            dve.wait_ge(s_line, START + DIRS * STEPS + 1)
            for j in range(J):
                xj = X[:, j * HW:(j + 1) * HW].rearrange("p (y x) -> p y x", x=W)
                nc.vector.tensor_tensor(xj, xj, image[:, j, MARGIN:MARGIN + H, MARGIN:MARGIN + W],
                                        ALU.add).then_inc(s_out, 1)
            dve.wait_ge(s_out, START + J)


SNAKE = 9
MID = SNAKE // 2
EPITCH = W + 2 * MID
OFFC = SNAKE + 1
POINTS = [k for d in range(1, MID + 1) for k in (MID - d, MID + d)]
ITEMS = [(k, m) for k in POINTS for m in range(abs(k - MID))]
RING = 6
OWN_SLOTS = (2, 3, 4, 5, 6, 7, 8, 9)
AVERAGES = (0, 1)
ACT_SLOTS = (1, 5, 7)
DVE_PARTS = (1, 3, 5)
CONV_SLOTS = {0: (0, 0, 5), 1: (0, 5, 9), 2: (1, 0, 5), 3: (1, 5, 9)}
AVERAGES_OFF = (4, 5)
ACT_OFF = (5, 9, 14, 16)
DVE_OFF = (9, 11, 14)
ADD_SLOT = 7


def l3_schedule():
    operands, used = [], {}
    n = 0
    while n < len(ITEMS):
        k, m = ITEMS[n]
        both = n + 1 < len(ITEMS) and ITEMS[n + 1][0] == k
        operands.append((k, n, n + 1 if both else None))
        used[n] = len(operands)
        if both:
            used[n + 1] = len(operands)
        n += 2 if both else 1
    return operands, used


def block_l3(nc, ps, X, io, const, out):
    eps = const["eps"]
    operands, used = l3_schedule()
    quads = [(n, n2) for _, n, n2 in operands if n2 is not None]
    with ExitStack() as ctx:
        def t(name, shape, dt=F32):
            return ctx.enter_context(nc.sbuf_tensor("l3_" + name, shape, dt))

        semaphores = []

        def sem(name):
            semaphores.append(ctx.enter_context(nc.semaphore("l3_" + name)))
            return semaphores[-1]

        xstats = t("xstats", [P, J, 2, 6])
        xmv = t("xmv", [P, J, 2])
        std = t("std", [P, J])
        rstd = t("rstd", [P, J])
        xe = t("xe", [P, J, EPITCH, EPITCH])
        down = t("down", [P, J, EPITCH - 1, EPITCH])
        w_off = t("w_off", [P, 9, P])
        w_dsc = t("w_dsc", [P, SNAKE, P])
        sums = t("sums", [P, len(POINTS), P])
        cols = t("cols", [P, 6])
        avg = t("avg", [P, 2, P])
        minus = t("minus", [P, MID])
        raw = t("raw", [P, 2, HW])
        stats = t("stats", [P, 2, 2, 6])
        mv = t("mv", [P, 2, 2])
        gstat = t("gstat", [P, 2, 8])
        off = t("off", [P, J * HW])
        ramp = t("ramp", [P, 4, HW])
        y = t("y", [P, HW])
        xz = t("xz", [P, J, H + 2, PADW])
        term = t("term", [P, 4, HW])
        isum = t("isum", [P, RING, HW])

        s_in = sem("in")
        s_border = sem("border")
        s_gn = [sem("gn_first"), sem("gn_rest")]
        s_std = sem("std")
        s_xn = sem("xn")
        s_edge = sem("edge")
        s_dy = sem("dy")
        s_conv = sem("conv")
        s_raw = [sem("raw_off"), sem("raw_out")]
        s_gs = [sem("gs_off"), sem("gs_out")]
        s_gavg = [sem("gavg_off"), sem("gavg_out")]
        s_gstd = [sem("gstd_off"), sem("gstd_out")]
        s_off = sem("off")
        s_cum = sem("cum")
        s_ramp = sem("ramp")
        s_term = sem("term")
        s_sum = sem("sum")
        s_quad = sem("quad")
        s_used = sem("used")
        s_y = sem("y")
        s_out = sem("out")
        s_store = sem("store")
        s_alone = sem("alone")
        GS = 9
        NI, NO, NQ = len(ITEMS), len(operands), len(quads)
        first = {k: next(n for n, it in enumerate(ITEMS) if it[0] == k) for k in POINTS}

        prime(nc, semaphores)
        block = ctx.enter_context(nc.Block())

        @block.sync
        def _(sp):
            for dst, name in ((w_off, "l3_w_off"), (w_dsc, "l3_w_dsc"), (sums, "l3_sums"), (cols, "l3_cols"),
                              (avg, "l3_avg"), (minus, "l3_minus")):
                sp.dma_start(dst[:], io[name]).then_inc(s_in, 16)
            sp.wait_ge(s_in, START + 16 * 6)
            for j in range(J):
                sp.wait_ge(s_out, START + j + 1)
                for g in range(G):
                    sp.dma_start(out[J * g + j].rearrange("c h w -> c (h w)"),
                                 X[C * g:C * g + C, HW * j:HW * (j + 1)]).then_inc(s_store, 16)
            sp.wait_ge(s_store, START + 16 * G * J)

        @block.tensor
        def _(pe):
            pe.wait_ge(s_in, START + 16 * 6)

            def group_average(norm, j, a):
                pe.wait_ge(s_gs[norm], START + j * GS + (3 if a == 0 else 5))
                pe.matmul(ps[:, 1 - norm, a:a + 1], avg[:, norm, :],
                          mv[:, norm, 0:1] if a == 0 else gstat[:, norm, 1:2],
                          start=True, stop=True).then_inc(s_gavg[norm], 1)

            def offset_conv(j, h, first_tap=0, end=9):
                if first_tap == 0:
                    pe.wait_ge(s_raw[0], START + j * 2 + (h + 1))
                for n in range(first_tap, end):
                    ky, kx = divmod(n, 3)
                    rows = xz[:, bass.ds(j, 1), ky + H // 2 * h:ky + H // 2 * (h + 1), kx:kx + W]
                    mm = pe.matmul(ps[:, 1, :].rearrange("p (y x) -> p y x", x=W), w_off[:, n, :],
                                   rows.rearrange("p j y x -> p (j y) x"),
                                   start=(n == 0), stop=(n == 8))
                if end == 9:
                    mm.then_inc(s_conv, 1)

            def running_sum(c, j):
                if c >= 2:
                    pe.wait_ge(s_ramp, START + j * (2 * NI) + 2 * (first[POINTS[c - 2]] + abs(POINTS[c - 2] - MID)))
                for h in range(2):
                    mm = pe.matmul(ps[:, 2 + 2 * (c % 2) + h, :], sums[:, c, :],
                                   off[:, bass.ds(j * HW + h * HALF, HALF)], start=True, stop=True)
                mm.then_inc(s_cum, 1)

            def quarter(j, prev, last):
                def own_rows(k):
                    for h in range(2):
                        rows = xe[:, bass.ds(j, 1), MID + H // 2 * h:MID + H // 2 * (h + 1), k:k + W]
                        if k == 0:
                            pe.wait_ge(s_raw[1], START + j * 2 + h)
                        pe.matmul(ps[:, 6 + h, :].rearrange("p (y x) -> p y x", x=W), w_dsc[:, k, :],
                                  rows.rearrange("p j y x -> p (j y) x"),
                                  start=(k == 0), stop=False, skip_group_check=True)

                running_sum(2, j)
                own_rows(0)
                done = 3
                for q, (k, n, n2) in enumerate(operands):
                    if not last and q >= NO - 2:
                        c = q - (NO - 2)
                        pe.wait_ge(s_ramp, START + j * (2 * NI) + 2 * (NI if c == 1 else first[POINTS[-1]]))
                        pe.wait_ge(s_off, START + j + 2)
                        running_sum(c, j + 1)
                    c = POINTS.index(k)
                    while done < min(c + 3, len(POINTS)):
                        running_sum(done, j)
                        done += 1
                    if n2 is None:
                        pe.wait_ge(s_sum, START + j * NI + (n + 1))
                    else:
                        pe.wait_ge(s_quad, START + j * NQ + (quads.index((n, n2)) + 1))
                    for h in range(2):
                        mm = pe.matmul(ps[:, 6 + h, :], w_dsc[:, k, :],
                                       isum[:, n % RING, HALF * h:HALF * (h + 1)],
                                       start=False, stop=(q == NO - 1), skip_group_check=True)
                    mm.then_inc(s_used, 1)
                    if prev is not None and q in AVERAGES:
                        group_average(1, prev, AVERAGES.index(q))
                    if q in OWN_SLOTS:
                        own_rows(1 + OWN_SLOTS.index(q))
                    if not last and q in CONV_SLOTS:
                        offset_conv(j + 1, *CONV_SLOTS[q])
                    if not last and q in AVERAGES_OFF:
                        group_average(0, j + 1, AVERAGES_OFF.index(q))

            pe.wait_ge(s_xn, START + 1)
            for h in range(2):
                offset_conv(0, h)
            pe.wait_ge(s_xn, START + 2 * J)
            for a in range(2):
                group_average(0, 0, a)
            pe.wait_ge(s_off, START + 1)
            pe.wait_ge(s_edge, START + 4 * J)
            running_sum(0, 0)
            running_sum(1, 0)
            quarter(0, None, False)
            with pe.Fori(0, J - 2) as prev:
                quarter(prev + 1, prev, False)
            quarter(J - 1, J - 2, True)
            for a in range(2):
                group_average(1, J - 1, a)

        @block.scalar
        def _(act):
            for norm in range(2):
                act.sem_inc(s_raw[norm], 1)
            for i, js in enumerate((range(1), range(1, J))):
                act.wait_ge(s_gn[i], START + 3 * len(js))
                nc.scalar.activation(std[:, js.start:js.stop], xmv[:, js.start:js.stop, 1], ACT.Sqrt,
                                     bias=eps[:]).then_inc(s_std, 1)
            act.wait_ge(s_in, START + 16 * 6)

            def copy_raw(norm, j, h):
                if norm == 0:
                    act.wait_ge(s_conv, START + j * 2 + (h + 1))
                    if h == 0:
                        act.wait_ge(s_off, START + j)
                elif h == 0:
                    act.wait_ge(s_used, START + j * NO + NO)
                nc.scalar.activation(raw[:, norm, HALF * h:HALF * (h + 1)],
                                     ps[:, 6 + h if norm else 1, :], ACT.Identity,
                                     bias=cols[:, 3 * norm:3 * norm + 1]).then_inc(s_raw[norm], 1)

            def group_std(norm, j):
                act.wait_ge(s_gavg[norm], START + j * 2 + 2)
                nc.scalar.activation(gstat[:, norm, 2:3], ps[:, 1 - norm, 1:2], ACT.Sqrt,
                                     bias=eps[:]).then_inc(s_gstd[norm], 1)

            def offsets(j):
                act.wait_ge(s_gs[0], START + j * GS + GS)
                nc.scalar.activation(off[:, bass.ds(j * HW, HW)], raw[:, 0, :], ACT.Tanh,
                                     bias=gstat[:, 0, 5:6], scale=gstat[:, 0, 4:5]).then_inc(s_off, 1)

            def output(j):
                act.wait_ge(s_gs[1], START + j * GS + GS)
                nc.scalar.activation(y[:], raw[:, 1, :], ACT.Relu, bias=gstat[:, 1, 5:6],
                                     scale=gstat[:, 1, 4:5]).then_inc(s_y, 1)

            for h in range(2):
                copy_raw(0, 0, h)
            group_std(0, 0)
            offsets(0)

            def quarter(j, prev, last):
                for n, (k, m) in enumerate(ITEMS):
                    c = POINTS.index(k)
                    act.wait_ge(s_cum, START + j * len(POINTS) + (c + 1))
                    for e, sign in enumerate((1.0, -1.0)):
                        act.wait_ge(s_term, START + j * (2 * NI) + max(0, 2 * n + e - 3))
                        b = 2 + 2 * (c % 2)
                        nc.scalar.activation(ramp[:, (2 * n + e) % 4, :],
                                             ps[:, b:b + 2, :].rearrange("p b f -> p (b f)"), ACT.Relu,
                                             bias=minus[:, m:m + 1], scale=sign).then_inc(s_ramp, 1)
                    if prev is not None:
                        if n == ACT_SLOTS[0]:
                            for h in range(2):
                                copy_raw(1, prev, h)
                        if n == ACT_SLOTS[1]:
                            group_std(1, prev)
                        if n == ACT_SLOTS[2]:
                            output(prev)
                    if not last and n in ACT_OFF[:2]:
                        copy_raw(0, j + 1, ACT_OFF.index(n))
                    if not last and n == ACT_OFF[2]:
                        group_std(0, j + 1)
                    if not last and n == ACT_OFF[3]:
                        offsets(j + 1)

            quarter(0, None, False)
            with act.Fori(0, J - 2) as prev:
                quarter(prev + 1, prev, False)
            quarter(J - 1, J - 2, True)
            for h in range(2):
                copy_raw(1, J - 1, h)
            group_std(1, J - 1)
            output(J - 1)

        @block.gpsimd
        def _(pool):
            nc.gpsimd.memset(xz[:, 0], 0.0).then_inc(s_border, 1)
            nc.gpsimd.memset(xz[:, 1:], 0.0).then_inc(s_border, 1)
            a, b = MID, MID + W
            with pool.Fori(0, J) as j:
                image = xe[:, bass.ds(j, 1)].rearrange("p j y x -> p (j y) x")
                edges = [(image[:, a:b, 0:a], image[:, a:b, a:a + 1].to_broadcast([P, H, MID])),
                         (image[:, a:b, b:], image[:, a:b, b - 1:b].to_broadcast([P, H, MID])),
                         (image[:, 0:a, :], image[:, a:a + 1, :].to_broadcast([P, MID, EPITCH])),
                         (image[:, b:, :], image[:, b - 1:b, :].to_broadcast([P, MID, EPITCH]))]
                pool.wait_ge(s_xn, START + j * 2 + 2)
                pool.sem_inc(s_alone, 1)
                for i, (dst, src) in enumerate(edges):
                    if i == 2:
                        pool.wait_ge(s_edge, START + j * 4 + 2)
                        pool.sem_inc(s_alone, 1)
                    nc.gpsimd.tensor_copy(dst, src).then_inc(s_edge, 1)
            with pool.Fori(0, J) as j:
                for n in range(NI):
                    pool.wait_ge(s_term, START + j * (2 * NI) + (2 * n + 2))
                    pool.wait_ge(s_used, START + j * NO + (used[n - RING] if n >= RING else 0))
                    nc.gpsimd.tensor_tensor(isum[:, n % RING, :], term[:, 2 * n % 4, :],
                                            term[:, (2 * n + 1) % 4, :], ALU.subtract).then_inc(s_sum, 1)

        @block.vector
        def _(dve):
            for i, js in enumerate((range(1), range(1, J))):
                for j in js:
                    for h in range(2):
                        at = j * HW + h * HALF
                        nc.vector.bn_stats(xstats[:, j, h, :], X[:, at:at + HALF]).then_inc(s_gn[i], 1)
                dve.wait_ge(s_gn[i], START + 2 * len(js))
                for j in js:
                    nc.vector.bn_aggr(xmv[:, j, :], xstats[:, j]).then_inc(s_gn[i], 1)
                dve.wait_ge(s_std, START + i + 1)
                nc.vector.reciprocal(rstd[:, js.start:js.stop], std[:, js.start:js.stop]).then_inc(s_gn[i], 1)
                dve.wait_ge(s_gn[i], START + 3 * len(js) + 1)
                dve.wait_ge(s_border, START + i + 1)
                for j in js:
                    for dst in (xz[:, j, 1:H + 1, 1:W + 1], xe[:, j, MID:MID + H, MID:MID + W]):
                        nc.vector.tensor_scalar(dst, X[:, j * HW:(j + 1) * HW].rearrange("p (y x) -> p y x", x=W),
                                                xmv[:, j, 0:1], rstd[:, j:j + 1], ALU.subtract,
                                                ALU.mult).then_inc(s_xn, 1)
            dve.wait_ge(s_in, START + 16 * 6)

            def group_norm(norm, j, parts=(0, 1, 2)):
                def after(n):
                    dve.wait_ge(s_gs[norm], START + j * GS + n)

                g = gstat[:, norm, :]
                mean, var = ps[:, 1 - norm, 0:1], mv[:, norm, 1:2]
                if 0 in parts:
                    for h in range(2):
                        dve.wait_ge(s_raw[norm], START + j * 2 + (h + 2))
                        nc.vector.bn_stats(stats[:, norm, h, :],
                                           raw[:, norm, HALF * h:HALF * (h + 1)]).then_inc(s_gs[norm], 1)
                    after(2)
                    dve.sem_inc(s_alone, 1)
                    nc.vector.bn_aggr(mv[:, norm, :], stats[:, norm]).then_inc(s_gs[norm], 1)
                if 1 in parts:
                    dve.wait_ge(s_gavg[norm], START + j * 2 + 1)
                    nc.vector.tensor_tensor(g[:, 0:1], mv[:, norm, 0:1], mean, ALU.subtract).then_inc(s_gs[norm], 1)
                    after(4)
                    nc.vector.scalar_tensor_tensor(out=g[:, 1:2], in0=g[:, 0:1], scalar=g[:, 0:1], in1=var,
                                                   op0=ALU.mult, op1=ALU.add).then_inc(s_gs[norm], 1)
                if 2 in parts:
                    dve.wait_ge(s_gstd[norm], START + j + 1)
                    nc.vector.reciprocal(g[:, 3:4], g[:, 2:3]).then_inc(s_gs[norm], 1)
                    after(6)
                    nc.vector.tensor_tensor(g[:, 4:5], g[:, 3:4], cols[:, 3 * norm + 1:3 * norm + 2],
                                            ALU.mult).then_inc(s_gs[norm], 1)
                    after(7)
                    nc.vector.tensor_tensor(g[:, 6:7], g[:, 4:5], mean, ALU.mult).then_inc(s_gs[norm], 1)
                    after(8)
                    nc.vector.tensor_tensor(g[:, 5:6], cols[:, 3 * norm + 2:3 * norm + 3], g[:, 6:7],
                                            ALU.subtract).then_inc(s_gs[norm], 1)

            with dve.Fori(0, J) as j:
                image = xe[:, bass.ds(j, 1)].rearrange("p j y x -> p (j y) x")
                dve.wait_ge(s_edge, START + j * 4 + 4)
                nc.vector.tensor_tensor(down[:, bass.ds(j, 1)].rearrange("p j y x -> p (j y) x"),
                                        image[:, 1:, :], image[:, :-1, :], ALU.subtract).then_inc(s_dy, 1)
            group_norm(0, 0)
            dve.wait_ge(s_dy, START + J)
            def add_output(j):
                xj = X[:, bass.ds(j * HW, HW)]
                dve.wait_ge(s_y, START + j + 1)
                nc.vector.tensor_tensor(xj, xj, y[:], ALU.add).then_inc(s_out, 1)

            def quarter(j, prev, last):
                rows = down[:, bass.ds(j, 1)].rearrange("p j y x -> p (j y) x")

                def add_quad(i):
                    n, n2 = quads[i]
                    dve.wait_ge(s_sum, START + j * NI + (n2 + 1))
                    nc.vector.tensor_tensor(isum[:, n % RING, :], isum[:, n % RING, :],
                                            isum[:, n2 % RING, :], ALU.add).then_inc(s_quad, 1)

                added = 0
                for n, (k, m) in enumerate(ITEMS):
                    for e, at in enumerate((MID + m, MID - m - 1)):
                        q = 2 * n + e
                        dve.wait_ge(s_ramp, START + j * (2 * NI) + (q + 1))
                        dve.wait_ge(s_sum, START + j * NI + max(0, n - 1))
                        nc.vector.scalar_tensor_tensor(
                            out=term[:, q % 4, :].rearrange("p (y x) -> p y x", x=W),
                            in0=ramp[:, q % 4, :].rearrange("p (y x) -> p y x", x=W), scalar=1.0,
                            in1=rows[:, at:at + H, k:k + W], op0=ALU.min, op1=ALU.mult).then_inc(s_term, 1)
                    while added < NQ and quads[added][1] <= n - 2:
                        add_quad(added)
                        added += 1
                    if prev is not None and n in DVE_PARTS:
                        group_norm(1, prev, (DVE_PARTS.index(n),))
                    if prev is not None and n == ADD_SLOT:
                        add_output(prev)
                    if not last and n in DVE_OFF:
                        group_norm(0, j + 1, (DVE_OFF.index(n),))
                while added < NQ:
                    add_quad(added)
                    added += 1

            quarter(0, None, False)
            with dve.Fori(0, J - 2) as prev:
                quarter(prev + 1, prev, False)
            quarter(J - 1, J - 2, True)
            group_norm(1, J - 1)
            add_output(J - 1)
            dve.wait_ge(s_out, START + J)


CONSTS = ["ident", "ident16", "iota", "eps", "neg_half", "minus_iota", "one"]


def dft_matrices(np):
    y, x = np.divmod(np.arange(PIX), PATCH)
    fa, fb, fc, seen = [], [], [], set()
    for v in range(PATCH):
        for u in range(PATCH):
            if (v, u) in seen:
                continue
            mirror = (-v % PATCH, -u % PATCH)
            seen |= {(v, u), mirror}
            angle = 2 * np.pi * ((v * y + u * x) % PATCH) / PATCH
            re, im = np.cos(angle), -np.sin(angle)
            if mirror == (v, u):
                fa, fb, fc = fa + [re], fb + [re], fc + [re / PIX]
            else:
                fa += [re, im, re, im]
                fb += [re, im, im, re]
                fc += [2 * re / PIX, -2 * re / PIX, 2 * im / PIX, 2 * im / PIX]
    fa, fb, fc = (np.array(m).astype(np.float32) for m in (fa, fb, fc))
    sides = np.zeros((2, P, 2, PRODS), np.float32)
    for n, m in enumerate((fa, fb)):
        for h in range(2):
            sides[n, PIX * h:PIX * (h + 1), h] = m.T
    return sides[0], sides[1], fc


def lay_out(inputs, np):
    f = np.float32
    a = {"x": np.ascontiguousarray(inputs["x"])}
    books = np.asarray(inputs["L0_conv_codebooks"])
    a["codes"] = np.ascontiguousarray(books.reshape(NC, KC, P, C).transpose(2, 0, 1, 3))
    a["codes_t"] = np.ascontiguousarray(books.transpose(0, 2, 1))
    a["ident"] = np.eye(P, dtype=f)
    a["ident16"] = np.eye(P, dtype=np.float16)
    a["iota"] = (np.arange(P)[:, None] + P * np.arange(KC)[None, :]).astype(f)
    a["minus_iota"] = -a["iota"]
    a["one"] = np.ones((P, 1), f)
    a["eps"] = np.full((P, 1), EPS, f)
    a["neg_half"] = np.full((P, P), -0.5, f)

    wh, wdw = np.asarray(inputs["L1_conv_w_hidden"]), np.asarray(inputs["L1_conv_w_dw"])
    bh, bdw = np.asarray(inputs["L1_conv_b_hidden"]), np.asarray(inputs["L1_conv_b_dw"])
    a["l1_wh"] = np.concatenate([np.tile(wh.T, (3, 1)), np.tile(bh[None], (3, 1)), bdw[None]])
    by_tap = wdw.transpose(2, 1, 0)
    a["l1_wd"] = np.concatenate([np.repeat(by_tap, C, axis=0), by_tap,
                                 np.tile(np.array([0, 1, 0], f)[None, :, None], (1, 1, HID))])
    inside = np.zeros((H + 2, PADW), f)
    inside[1:H + 1, 1:W + 1] = 1
    taps = np.array([[inside[ky:ky + H, kx:kx + W] for ky in range(3)] for kx in range(3)] + [np.ones((3, H, W))])
    a["l1_inside"] = taps.reshape(4, 3, PAIRS, PATCH, PAIRS, PATCH).transpose(0, 1, 2, 4, 3, 5).reshape(
        4, 3, HW).astype(f)
    a["l1_fa"], a["l1_fb"], a["l1_fc"] = dft_matrices(np)
    a["l1_lnw"] = np.tile(np.asarray(inputs["L1_conv_ln_w"])[None], (P, 1))
    a["l1_lnb"] = np.tile(np.asarray(inputs["L1_conv_ln_b"])[None], (P, 1))
    wp = np.asarray(inputs["L1_conv_w_proj"]).T
    none = np.zeros((QC, C), f)
    a["l1_wp"] = np.stack([np.concatenate([wp, none]), np.concatenate([none, wp])], axis=1)
    a["l1_bp"] = np.tile(np.asarray(inputs["L1_conv_b_proj"]), G)[:, None]

    w = np.zeros((G, C, DIRS, TAPS, G, C), f)
    names = ("ud", "du", "lr", "rl")
    for d, n in enumerate(names):
        for g in range(G):
            w[g, :, d, :, g, :] = np.asarray(inputs["L2_conv_w_" + n]).transpose(1, 2, 0)
    a["l2_w"] = w.reshape(P, DIRS, TAPS, P)
    a["l2_b"] = np.stack([np.tile(np.asarray(inputs["L2_conv_b_" + n]), G) for n in names], axis=1)

    def blocks(w, taps):
        m = np.zeros((G, C, taps, G, C), f)
        for g in range(G):
            m[g, :, :, g, 0:w.shape[0]] = w.transpose(1, 2, 0)
        return m.reshape(P, taps, P)

    def column(v):
        m = np.zeros((G, C), f)
        m[:, 0:len(v)] = v
        return m.reshape(P)

    g_in = {n: np.asarray(inputs["L3_conv_" + n]) for n in
            ("w_off", "b_off", "g_gn_off", "b_gn_off", "w_dsc", "b_dsc", "g_gn", "b_gn")}
    a["l3_w_off"] = blocks(g_in["w_off"][:OFFC].reshape(OFFC, C, 9), 9)
    a["l3_w_dsc"] = blocks(g_in["w_dsc"].reshape(C, C, SNAKE), SNAKE)
    a["l3_cols"] = np.stack([column(g_in["b_off"][:OFFC]), column(g_in["g_gn_off"][:OFFC]),
                             column(g_in["b_gn_off"][:OFFC]), column(g_in["b_dsc"]), column(g_in["g_gn"]),
                             column(g_in["b_gn"])], axis=1)
    sums = np.zeros((G, C, len(POINTS), G, C), f)
    for c, k in enumerate(POINTS):
        for i in range(k, MID) if k < MID else range(MID + 1, k + 1):
            for g in range(G):
                sums[g, i, c, g, :] = 1
    a["l3_sums"] = sums.reshape(P, len(POINTS), P)
    at = np.arange(P)
    a["l3_avg"] = np.stack([(at[:, None] // n == at[None, :] // n).astype(f) / f(n) for n in (2, 4)], axis=1)
    a["l3_minus"] = np.tile(-np.arange(MID, dtype=f)[None], (P, 1))
    return {n: np.ascontiguousarray(v) for n, v in a.items()}


def build_program(nc, io, out):
    with ExitStack() as ctx:
        def t(name, shape, dt=F32):
            return ctx.enter_context(nc.sbuf_tensor(name, shape, dt))

        X = t("X", [P, J * HW])
        ps = ctx.enter_context(nc.psum_tensor("ps", [P, 8, BANK], F32))
        const = {name: t("c_" + name, list(io[name].shape), io[name].dtype) for name in CONSTS}
        block_l0(nc, ps, X, io, const)
        block_l1(nc, ps, X, io, const)
        block_l2(nc, ps, X, io, const)
        block_l3(nc, ps, X, io, const, out)


def kernel(**inputs):
    import numpy as np
    import concourse.bacc as bacc
    from concourse.bass_utils import run_bass_kernel_spmd

    arrays = lay_out(inputs, np)
    nc = bacc.Bacc("TRN2", target_bir_lowering=False, num_devices=1)
    io = {n: nc.dram_tensor("in_" + n, a.shape, mybir.dt.from_np(a.dtype), kind="ExternalInput").ap()
          for n, a in arrays.items()}
    out = nc.dram_tensor("out", (B, C, H, W), F32, kind="ExternalOutput").ap()
    build_program(nc, io, out)
    r = run_bass_kernel_spmd(nc, [{"in_" + n: a for n, a in arrays.items()}], core_ids=[0])
    return r.results[0]["out"]
```
